# Optimizing a Trainium2 kernel written in Bass

```python
import numpy as np
import jax
import jax.numpy as jnp

def _softmax(x, axis=-1):
    return jax.nn.softmax(x, axis=axis)

def _gelu(x):
    return jax.nn.gelu(x, approximate=True)

def _silu(x):
    return jax.nn.silu(x)

def _sigmoid(x):
    return jax.nn.sigmoid(x)

def _layernorm(x, axis=-1, eps=1e-05):
    m = jnp.mean(x, axis=axis, keepdims=True)
    v = jnp.var(x, axis=axis, keepdims=True)
    return (x - m) / jnp.sqrt(v + eps)

def _scatter_add(tgt, idx, src, axis=0):
    return tgt.at[idx].add(src)

def _segment_sum(src, seg, n):
    return jax.ops.segment_sum(src, seg, n)
kernel_name = 'mk_early_fusion_d1_tok_img1024_r4_550f61'

def setup_inputs(seed: int=0):
    np.random.seed(seed)
    _w = jnp.asarray

    def _rec_inputs():
        import jax
        import jax.numpy as jnp
        _rk = jax.random.key(seed)
        x = jax.random.uniform(jax.random.fold_in(_rk, 1), (16, 3, 256, 256), jnp.float32, 0.0, 1)
        txt = 2.40575 + 1.24603 * jax.random.normal(jax.random.fold_in(_rk, 2), (16, 128, 256), jnp.float32)
        return (x, txt)
    x, txt = _rec_inputs()

    def _L0_tok_setup():
        import jax, jax.numpy as jnp
        import numpy as np
        _GRAY_W = (0.2989, 0.587, 0.114)
        key = jax.random.key(seed)
        x = jax.random.uniform(key, (32, 3, 256, 256), dtype=jnp.float32)
        sx = jnp.array([[-3.0, 0.0, 3.0], [-10.0, 0.0, 10.0], [-3.0, 0.0, 3.0]], dtype=jnp.float32)
        scharr = jnp.stack([sx, sx.T])[:, None, :, :]
        return {'x': x, 'scharr': scharr}
    _L0_tok_all = _L0_tok_setup()
    _L0_tok_in = {k: v for k, v in _L0_tok_all.items() if k in ('scharr',)}
    del _L0_tok_all

    def _L0_attn_setup():
        import jax, jax.numpy as jnp
        import numpy as np
        import math
        DIM = 256
        NUM_HEADS = 16
        HEAD_DIM = DIM // NUM_HEADS
        SCALE = HEAD_DIM ** (-0.5)
        WINDOW_SIZE = 64
        IS_SLIDING = True
        IS_CAUSAL = True

        def _alibi_slopes(num_heads: int) -> np.ndarray:
            closest_pow2 = 2 ** math.floor(math.log2(num_heads))
            base = 2.0 ** (-2.0 ** (-(math.log2(closest_pow2) - 3)))
            powers = np.arange(1, closest_pow2 + 1, dtype=np.float32)
            slopes = base ** powers
            if num_heads != closest_pow2:
                start = 2.0 ** (-(2.0 ** (-(math.log2(closest_pow2) - 3)) - 1))
                extra = np.linspace(start, base, num_heads - closest_pow2, dtype=np.float32)
                slopes = np.concatenate([slopes, extra])
            return slopes.astype(np.float32)
        key = jax.random.key(seed)
        k_x, k_qw, k_qb, k_pw, k_pb = jax.random.split(key, 5)
        B, N, C = (2, 512, DIM)
        s = C ** (-0.5)
        return {'x': jax.random.normal(k_x, (B, N, C), dtype=jnp.float32), 'qkv_w': jax.random.normal(k_qw, (3 * C, C), dtype=jnp.float32) * s, 'qkv_b': jax.random.normal(k_qb, (3 * C,), dtype=jnp.float32) * 0.02, 'proj_w': jax.random.normal(k_pw, (C, C), dtype=jnp.float32) * s, 'proj_b': jax.random.normal(k_pb, (C,), dtype=jnp.float32) * 0.02}
    _L0_attn_all = _L0_attn_setup()
    _L0_attn_in = {k: v for k, v in _L0_attn_all.items() if k in ('qkv_w', 'qkv_b', 'proj_w', 'proj_b')}
    del _L0_attn_all

    def _L0_ffn_setup():
        import jax, jax.numpy as jnp
        import numpy as np
        from jax import lax
        D = 256
        H = 352
        E = 8
        K = 2
        ROUTER_SCALE = 1.0

        def _expert(x, w1, b1, w3, b3, w2, b2):
            h = jax.nn.silu((x @ w1 + b1) * (x @ w3 + b3))
            return h @ w2 + b2
        key = jax.random.key(seed)
        ks = jax.random.split(key, 16)
        s = 0.02
        inp = {'x': jax.random.normal(ks[0], (2, 512, D), dtype=jnp.float32), 'gate_w': jax.random.normal(ks[1], (E, D), dtype=jnp.float32) * s, 'gate_b': jax.random.normal(ks[2], (E,), dtype=jnp.float32) * s, 'w1': jax.random.normal(ks[3], (E, D, H), dtype=jnp.float32) * s, 'b1': jax.random.normal(ks[4], (E, H), dtype=jnp.float32) * s, 'w3': jax.random.normal(ks[5], (E, D, H), dtype=jnp.float32) * s, 'b3': jax.random.normal(ks[6], (E, H), dtype=jnp.float32) * s, 'w2': jax.random.normal(ks[7], (E, H, D), dtype=jnp.float32) * s, 'b2': jax.random.normal(ks[8], (E, D), dtype=jnp.float32) * s, 'sw1': jax.random.normal(ks[9], (D, H), dtype=jnp.float32) * s, 'sb1': jax.random.normal(ks[10], (H,), dtype=jnp.float32) * s, 'sw3': jax.random.normal(ks[11], (D, H), dtype=jnp.float32) * s, 'sb3': jax.random.normal(ks[12], (H,), dtype=jnp.float32) * s, 'sw2': jax.random.normal(ks[13], (H, D), dtype=jnp.float32) * s, 'sb2': jax.random.normal(ks[14], (D,), dtype=jnp.float32) * s}
        return inp
    _L0_ffn_all = _L0_ffn_setup()
    _L0_ffn_in = {k: v for k, v in _L0_ffn_all.items() if k in ('gate_w', 'gate_b', 'w1', 'b1', 'w3', 'b3', 'w2', 'b2', 'sw1', 'sb1', 'sw3', 'sb3', 'sw2', 'sb2')}
    del _L0_ffn_all
    return {'x': x, 'txt': txt, 'L0_tok_scharr': _L0_tok_in['scharr'], 'L0_attn_qkv_w': _L0_attn_in['qkv_w'], 'L0_attn_qkv_b': _L0_attn_in['qkv_b'], 'L0_attn_proj_w': _L0_attn_in['proj_w'], 'L0_attn_proj_b': _L0_attn_in['proj_b'], 'L0_ffn_gate_w': _L0_ffn_in['gate_w'], 'L0_ffn_gate_b': _L0_ffn_in['gate_b'], 'L0_ffn_w1': _L0_ffn_in['w1'], 'L0_ffn_b1': _L0_ffn_in['b1'], 'L0_ffn_w3': _L0_ffn_in['w3'], 'L0_ffn_b3': _L0_ffn_in['b3'], 'L0_ffn_w2': _L0_ffn_in['w2'], 'L0_ffn_b2': _L0_ffn_in['b2'], 'L0_ffn_sw1': _L0_ffn_in['sw1'], 'L0_ffn_sb1': _L0_ffn_in['sb1'], 'L0_ffn_sw3': _L0_ffn_in['sw3'], 'L0_ffn_sb3': _L0_ffn_in['sb3'], 'L0_ffn_sw2': _L0_ffn_in['sw2'], 'L0_ffn_sb2': _L0_ffn_in['sb2']}

def reference(x, txt, L0_tok_scharr, L0_attn_qkv_w, L0_attn_qkv_b, L0_attn_proj_w, L0_attn_proj_b, L0_ffn_gate_w, L0_ffn_gate_b, L0_ffn_w1, L0_ffn_b1, L0_ffn_w3, L0_ffn_b3, L0_ffn_w2, L0_ffn_b2, L0_ffn_sw1, L0_ffn_sb1, L0_ffn_sw3, L0_ffn_sb3, L0_ffn_sw2, L0_ffn_sb2):
    import jax
    import jax.numpy as jnp

    def _L0_tok_ref(x, scharr):
        import jax, jax.numpy as jnp
        import numpy as np
        _GRAY_W = (0.2989, 0.587, 0.114)
        w = jnp.asarray(_GRAY_W, dtype=x.dtype)
        gray = jnp.einsum('bchw,c->bhw', x, w)[:, None]
        edges = jax.lax.conv_general_dilated(gray, scharr, window_strides=(1, 1), padding='SAME', dimension_numbers=('NCHW', 'OIHW', 'NCHW'))
        abs_edges = jnp.sqrt(jnp.square(edges))
        edge = abs_edges.sum(axis=1) / 2
        return edge

    def _L0_attn_ref(x, qkv_w, qkv_b, proj_w, proj_b):
        import jax, jax.numpy as jnp
        import numpy as np
        import math
        DIM = 256
        NUM_HEADS = 16
        HEAD_DIM = DIM // NUM_HEADS
        SCALE = HEAD_DIM ** (-0.5)
        WINDOW_SIZE = 64
        IS_SLIDING = True
        IS_CAUSAL = True

        def _alibi_slopes(num_heads: int) -> np.ndarray:
            closest_pow2 = 2 ** math.floor(math.log2(num_heads))
            base = 2.0 ** (-2.0 ** (-(math.log2(closest_pow2) - 3)))
            powers = np.arange(1, closest_pow2 + 1, dtype=np.float32)
            slopes = base ** powers
            if num_heads != closest_pow2:
                start = 2.0 ** (-(2.0 ** (-(math.log2(closest_pow2) - 3)) - 1))
                extra = np.linspace(start, base, num_heads - closest_pow2, dtype=np.float32)
                slopes = np.concatenate([slopes, extra])
            return slopes.astype(np.float32)
        B, N, C = x.shape
        H, D = (NUM_HEADS, HEAD_DIM)
        slopes = jnp.asarray(_alibi_slopes(H))
        qkv = x @ qkv_w.T + qkv_b
        qkv = qkv.reshape(B, N, 3, H, D).transpose(2, 0, 3, 1, 4)
        q, k, v = (qkv[0], qkv[1], qkv[2])
        attn = jnp.einsum('bhnd,bhmd->bhnm', q, k) * SCALE
        pos = jnp.arange(N)
        rel = pos[None, :] - pos[:, None]
        alibi = slopes[:, None, None] * rel.astype(jnp.float32)
        attn = attn + alibi[None]
        if IS_SLIDING:
            attn = jnp.where(jnp.abs(rel) >= WINDOW_SIZE, -jnp.inf, attn)
        if IS_CAUSAL:
            attn = jnp.where(rel > 0, -jnp.inf, attn)
        attn = jax.nn.softmax(attn, axis=-1)
        out = jnp.einsum('bhnm,bhmd->bhnd', attn, v)
        out = out.transpose(0, 2, 1, 3).reshape(B, N, C)
        return out @ proj_w.T + proj_b

    def _L0_ffn_ref(x, gate_w, gate_b, w1, b1, w3, b3, w2, b2, sw1, sb1, sw3, sb3, sw2, sb2):
        import jax, jax.numpy as jnp
        import numpy as np
        from jax import lax
        D = 256
        H = 352
        E = 8
        K = 2
        ROUTER_SCALE = 1.0

        def _expert(x, w1, b1, w3, b3, w2, b2):
            h = jax.nn.silu((x @ w1 + b1) * (x @ w3 + b3))
            return h @ w2 + b2
        shape = x.shape
        xf = x.reshape(-1, D)
        T = xf.shape[0]
        scores = jax.nn.softmax(xf @ gate_w.T, axis=-1)
        biased = scores + gate_b
        _, idx = lax.top_k(biased, K)
        w = jnp.take_along_axis(scores, idx, axis=-1) * ROUTER_SCALE
        rw = jnp.zeros((T, E), dtype=xf.dtype).at[jnp.arange(T)[:, None], idx].add(w)
        h = jax.nn.silu((jnp.einsum('td,edh->teh', xf, w1) + b1) * (jnp.einsum('td,edh->teh', xf, w3) + b3))
        oe = jnp.einsum('teh,ehd->ted', h, w2) + b2
        y = jnp.einsum('te,ted->td', rw, oe)
        z = _expert(xf, sw1, sb1, sw3, sb3, sw2, sb2)
        return (y + z).reshape(shape)
    h = _L0_tok_ref(x, L0_tok_scharr)
    h = jnp.concatenate([h, txt], axis=1)
    h = h + _L0_attn_ref(_layernorm(h, axis=-1), L0_attn_qkv_w, L0_attn_qkv_b, L0_attn_proj_w, L0_attn_proj_b)
    h = h + _L0_ffn_ref(_layernorm(h, axis=-1), L0_ffn_gate_w, L0_ffn_gate_b, L0_ffn_w1, L0_ffn_b1, L0_ffn_w3, L0_ffn_b3, L0_ffn_w2, L0_ffn_b2, L0_ffn_sw1, L0_ffn_sb1, L0_ffn_sw3, L0_ffn_sb3, L0_ffn_sw2, L0_ffn_sb2)
    return h

_drawn_inputs = setup_inputs


def setup_inputs(seed=0):
    import zlib

    import numpy as np

    out = dict(_drawn_inputs(seed))
    spreads = {}
    factors = {'L0_attn_qkv_b': 6.464,
     'L0_attn_proj_b': 8.0,
     'L0_ffn_gate_w': 8.0,
     'L0_ffn_gate_b': 8.0,
     'L0_ffn_w1': 8.0,
     'L0_ffn_b1': 8.0,
     'L0_ffn_w3': 8.0,
     'L0_ffn_b3': 8.0,
     'L0_ffn_w2': 8.0,
     'L0_ffn_b2': 64.0,
     'L0_ffn_sw1': 8.0,
     'L0_ffn_sb1': 8.0,
     'L0_ffn_sw3': 7.982,
     'L0_ffn_sb3': 8.0,
     'L0_ffn_sw2': 7.999,
     'L0_ffn_sb2': 50.129}
    for name, (base, spread) in spreads.items():
        noise = np.random.default_rng([zlib.crc32(name.encode()), seed]).standard_normal(out[name].shape)
        drawn = base * np.exp(spread * noise) if base else spread * noise
        out[name] = jnp.asarray(drawn.astype(out[name].dtype))
    for name, factor in factors.items():
        out[name] = (out[name] * factor).astype(out[name].dtype)
    return out
```

```python
from contextlib import ExitStack

import concourse.bass as bass
from concourse import mybir

F32 = mybir.dt.float32
F16 = mybir.dt.float16
ALU = mybir.AluOpType
ACT = mybir.ActivationFunctionType
AX = mybir.AxisListType.X

P = 128
IMG = 256
C = 256
KC = C // P
HEADS, HD = 16, 16
WINDOW = 64
SCALE = HD ** -0.5
SPAN = P + WINDOW
EPS = 1e-5
HID = 352
HC = 3
HLAST = HID - 2 * P
GRAY_W = (0.2989, 0.587, 0.114)


def program(nc, x, txt, scharr, qkv_w, qkv_b, proj_w, proj_b, gate_w, gate_b, w1, b1, w3, b3, w2, b2,
            sw1, sb1, sw3, sb3, sw2, sb2, k_ident, k_shift, k_mask_a, k_mask_t, k_aug_l, k_aug_r,
            k_parity, k_before, out):
    B = x.shape[0]
    E = w1.shape[0]
    EA = E + 1
    T = (IMG + txt.shape[1]) // P
    N = T * P

    with ExitStack() as ctx:
        def sb(name, shape, dt=F32):
            return ctx.enter_context(nc.sbuf_tensor(name, shape, dt))

        def sem(name):
            return ctx.enter_context(nc.semaphore(name))

        ps = ctx.enter_context(nc.psum_tensor("ps", [P, 8, 512], F32))

        ident = sb("ident", [P, P])
        before = sb("before", [P, E, E])
        gb = sb("gb", [P, E])
        b2_all = sb("b2_all", [EA, C])
        gateT_h = sb("gateT_h", [P, KC, E], F16)
        gateT_l = sb("gateT_l", [P, KC, E], F16)
        rows = sb("rows", [E + 6, 3, P])
        rows_b3 = sb("rows_b3", [EA, 3, P])
        gate_n = sb("gate_n", [E, C])
        bias1 = sb("bias1", [P, HC, EA])
        bias3 = sb("bias3", [P, HC, EA])

        h1 = sb("h1", [P, B * T, C])
        mv = sb("mv", [P, T, 2])
        stats = sb("stats", [P, T, 6])
        gate_v = sb("gate_v", [P, 1])
        zero = sb("zero", [P, 1])
        eps = sb("eps", [P, 1])
        std = sb("std", [P, T])
        rstd = sb("rstd", [P, T])
        xn = sb("xn", [P, T, C])

        s = {n: sem(n) for n in (
            "consts", "filt_in", "nat_in", "wload", "filt_done", "identh", "setup_t", "setup_h", "setup_l",
            "bias_done", "w_hi", "w_lo", "w_free", "x_in", "txt_in", "pads", "ones", "chain", "gray", "conv",
            "absd", "edge", "xn", "xT", "xTh", "xTl", "qk", "qk_ev", "vps", "vaug", "q_hi", "k_hi", "lo", "smax",
            "mx", "mxT", "aug", "st", "exp", "av", "rs", "ao", "aoT", "aoh", "aol", "hp", "pj", "h1",
            "xn2", "xT2", "x2h", "x2l", "lg", "rmax", "rexp", "rw", "rwT", "rwTs", "b2ps", "acc0",
            "up", "u3", "prod", "silu", "hh", "hl", "yps", "yacc", "outd", "b2_in", "rb_in", "chain2", "var1", "std1", "var2", "std2")}

        def mm3(out_ap, lh, ll, rh, rl, start, stop):
            nc.tensor.matmul(out_ap, lh, rh, start=start, stop=False)
            nc.tensor.matmul(out_ap, lh, rl, start=False, stop=False)
            return nc.tensor.matmul(out_ap, ll, rh, start=False, stop=stop)

        with ExitStack() as pa:
            def sa(name, shape, dt=F32):
                return pa.enter_context(nc.sbuf_tensor(name, shape, dt))
            ident_h = sa("ident_h", [P, P], F16)
            shift = sa("shift", [P, 5, P])
            mask_a = sa("mask_a", [P, HEADS, SPAN], F16)
            mask_t = sa("mask_t", [P, SPAN], F16)
            aug_l = sa("aug_l", [64, T, HEADS, P], F16)
            aug_r = sa("aug_r", [64, N], F16)
            parity = sa("parity", [P, 2])
            filt = sa("filt", [P, 18])
            band = sa("band", [P, 6, P])
            corner = sa("corner", [P, 6, 2, P])
            bq4 = sa("bq4", [P, 6])
            bv = sa("bv", [P, C])
            pb = sa("pb", [P, C])
            nat = sa("nat", [P, 10, C])
            qkvT_h = sa("qkvT_h", [P, KC, 3 * C], F16)
            qkvT_l = sa("qkvT_l", [P, KC, 3 * C], F16)
            projT_h = sa("projT_h", [P, KC, C], F16)
            projT_l = sa("projT_l", [P, KC, C], F16)
            rows_qb = sa("rows_qb", [6, P])
            xT_h = sa("xT_h", [P, KC, N], F16)
            xT_l = sa("xT_l", [P, KC, N], F16)
            xin = sa("xin", [P, 2, 3, IMG])
            gray = sa("gray", [P, 2, IMG + 2])
            ab = sa("ab", [P, 2, 2, IMG])
            h = sa("h", [P, T, C])
            hp = sa("hp", [P, T, C])
            qs = sa("qs", [P, 2, N])
            ks = sa("ks", [P, 2, N])
            q_h = sa("q_h", [P, 2, 2, N], F16)
            q_l = sa("q_l", [P, 2, 2, N], F16)
            k_h = sa("k_h", [P, 2, N], F16)
            k_l = sa("k_l", [P, 2, N], F16)
            v_aug = sa("v_aug", [P, T, HEADS, HD + 1])
            mx = sa("mx", [P, T, HEADS])
            prob = sa("prob", [P, 3, 512])
            rs = sa("rs", [P, T, HEADS])
            ao = sa("ao", [P, T, C])
            aoT_h = sa("aoT_h", [P, KC, N], F16)
            aoT_l = sa("aoT_l", [P, KC, N], F16)

        with ExitStack() as pb_:
            def sbb(name, shape, dt=F32):
                return pb_.enter_context(nc.sbuf_tensor(name, shape, dt))
            stage = sbb("stage", [P, 2, 2 * KC * HID + HC * C])
            w1_h = sbb("w1_h", [P, EA, KC, HID], F16)
            w1_l = sbb("w1_l", [P, EA, KC, HID], F16)
            w3_h = sbb("w3_h", [P, EA, KC, HID], F16)
            w3_l = sbb("w3_l", [P, EA, KC, HID], F16)
            w2_h = sbb("w2_h", [P, EA, HC, C], F16)
            w2_l = sbb("w2_l", [P, EA, HC, C], F16)
            x2_h = sbb("x2_h", [P, KC, N], F16)
            x2_l = sbb("x2_l", [P, KC, N], F16)
            lgs = sbb("lgs", [P, T, E])
            rmax = sbb("rmax", [P, T])
            rex = sbb("rex", [P, T, E])
            rsum = sbb("rsum", [P, T])
            score = sbb("score", [P, T, E])
            biased = sbb("biased", [P, T, E])
            cmp1 = sbb("cmp1", [P, T, E, E])
            cmp2 = sbb("cmp2", [P, T, E, E])
            rank = sbb("rank", [P, T, E])
            rw = sbb("rw", [P, T, EA])
            rwT = sbb("rwT", [EA, N])
            acc = sbb("acc", [P, T, C])
            u3 = sbb("u3", [P, 2, N])
            tt = sbb("tt", [P, 2, N])
            hs = sbb("hs", [P, 2, N])
            hT_h = sbb("hT_h", [P, HC, N], F16)
            hT_l = sbb("hT_l", [P, HC, N], F16)

        block = ctx.enter_context(nc.Block())
        NW = KC * HID
        x_r = x.rearrange("b c (f p) w -> b f p c w", p=P)
        out_r = out.rearrange("b (t p) d -> b p t d", p=P)

        def heads_slice(h_i):
            return h_i // 8, 32 * ((h_i % 8) // 2), h_i % 2

        def rows_of(c):
            return P if c < HC - 1 else HLAST

        CREDITED = ("ao", "h1", "acc0", "prod", "yacc", "hl", "silu", "yps", "gray", "hp", "xn", "conv", "edge", "outd")

        @block.sync
        def _(sp):
            for n in CREDITED:
                sp.sem_inc(s[n], 1)
            sp.dma_start(filt[:, :], scharr.rearrange("a b c d -> b (a c d)").to_broadcast([P, 18])).then_inc(s["filt_in"], 16)
            for t_, d_ in ((ident, k_ident), (shift, k_shift), (mask_a, k_mask_a), (mask_t, k_mask_t),
                           (aug_l, k_aug_l), (aug_r, k_aug_r), (parity, k_parity), (before, k_before)):
                sp.dma_start(t_[:], d_).then_inc(s["consts"], 16)
            sp.dma_start(bv[:, :], qkv_b[2 * C:3 * C].rearrange("(a n) -> a n", a=1).to_broadcast([P, C])).then_inc(s["consts"], 16)
            sp.dma_start(pb[:, :], proj_b.rearrange("(a n) -> a n", a=1).to_broadcast([P, C])).then_inc(s["consts"], 16)
            sp.dma_start(gb[:, :], gate_b.rearrange("(a n) -> a n", a=1).to_broadcast([P, E])).then_inc(s["consts"], 16)
            sp.dma_start(nat[:, 0:6, :], qkv_w.rearrange("(j p) c -> p j c", p=P)).then_inc(s["nat_in"], 16)
            sp.dma_start(nat[:, 6:8, :], proj_w.rearrange("(j p) c -> p j c", p=P)).then_inc(s["nat_in"], 16)
            sp.dma_start(gate_n[:, :], gate_w).then_inc(s["nat_in"], 16)
            sp.dma_start(rows_qb[:, :], qkv_b.rearrange("(j p) -> j p", p=P)).then_inc(s["nat_in"], 16)
            sp.dma_start(b2_all[0:E, :], b2).then_inc(s["b2_in"], 16)
            sp.dma_start(b2_all[E:EA, :], sb2.rearrange("(a n) -> a n", a=1)).then_inc(s["b2_in"], 16)
            sp.wait_ge(s["pads"], 2)
            for dst, be, bs in ((rows, b1, sb1), (rows_b3, b3, sb3)):
                f = dst[0:EA].rearrange("e c p -> e (c p)")
                sp.dma_start(f[0:E, 0:HID], be).then_inc(s["rb_in"], 16)
                sp.dma_start(f[E:EA, 0:HID], bs.rearrange("(a n) -> a n", a=1)).then_inc(s["rb_in"], 16)
            with sp.Fori(0, B) as b:
                sp.wait_ge(s["gray"], b + 1)
                for f in range(2):
                    sp.dma_start(xin[:, f], x_r[b, f]).then_inc(s["x_in"], 16)
                sp.wait_ge(s["hp"], b + 1)
                sp.wait_ge(s["xn"], b + 1)
                sp.dma_start(h[:, 2, :], txt[b]).then_inc(s["txt_in"], 16)
            sp.wait_ge(s["h1"], 2 * B + 1)
            for e in range(EA):
                a1, a3, a2 = (w1[e], w3[e], w2[e]) if e < E else (sw1, sw3, sw2)
                if e >= 2:
                    sp.wait_ge(s["w_lo"], 4 * (e - 1))
                d = stage[:, e % 2, :]
                sp.dma_start(d[:, 0:NW].rearrange("p (k n) -> p k n", k=KC), a1.rearrange("(k p) n -> p k n", p=P)).then_inc(s["wload"], 16)
                sp.dma_start(d[:, NW:2 * NW].rearrange("p (k n) -> p k n", k=KC), a3.rearrange("(k p) n -> p k n", p=P)).then_inc(s["wload"], 16)
                sp.dma_start(d[:, 2 * NW:2 * NW + 2 * C].rearrange("p (k n) -> p k n", k=2), a2[0:2 * P].rearrange("(k p) n -> p k n", p=P)).then_inc(s["wload"], 16)
                sp.dma_start(d[0:HLAST, 2 * NW + 2 * C:], a2[2 * P:]).then_inc(s["wload"], 16)
                sp.wait_ge(s["wload"], 64 * (e + 1))
            with sp.Fori(0, B) as b:
                sp.wait_ge(s["yacc"], b * (EA * T) + EA * T + 1)
                sp.dma_start(out_r[b], acc[:, :, :]).then_inc(s["outd"], 16)
            sp.wait_ge(s["outd"], B * 16 + 1)

        @block.tensor
        def _(pe):
            pe.wait_ge(s["consts"], 16 * 11)
            pe.wait_ge(s["nat_in"], 64)
            pe.wait_ge(s["rb_in"], 64)
            def put(slot, in_, n):
                return nc.tensor.transpose(ps[:, slot // 4, 128 * (slot % 4):128 * (slot % 4) + n], in_, ident[0:n, 0:n])
            for j in range(8):
                for k in range(KC):
                    last = put(j * KC + k, nat[:, j, k * P:(k + 1) * P], P)
            for k in range(KC):
                last = put(16 + k, gate_n[:, k * P:(k + 1) * P], E)
            last = put(18, rows_qb[:, :], 6)
            for c in range(HC):
                put(20 + c, rows[0:EA, c, :], EA)
                last = put(24 + c, rows_b3[:, c, :], EA)
            last.then_inc(s["setup_t"], 1)

            pe.wait_ge(s["setup_l"], 3)
            pe.wait_ge(s["bias_done"], 3)
            pe.wait_ge(s["filt_done"], 1)
            with pe.Fori(0, B) as b:
                pe.wait_ge(s["gray"], b + 1 + 1)
                pe.wait_ge(s["ao"], b + 1)
                for f in range(2):
                    for q in range(2):
                        o = ps[:, f, q * IMG:(q + 1) * IMG]
                        for dx in range(3):
                            nc.tensor.matmul(o, band[:, 3 * q + dx, :], gray[:, f, dx:dx + IMG], start=dx == 0, stop=False)
                            if f == 0:
                                last = nc.tensor.matmul(o, corner[0:32, 3 * q + dx, 0, :], gray[0:32, 1, dx:dx + IMG],
                                                        start=False, stop=dx == 2)
                            else:
                                last = nc.tensor.matmul(o, corner[96:128, 3 * q + dx, 1, :], gray[96:128, 0, dx:dx + IMG],
                                                        start=False, stop=dx == 2)
                    last.then_inc(s["conv"], 1)
                pe.wait_ge(s["xn"], b + 1 + 1)
                for t in range(T):
                    for k in range(KC):
                        last = nc.tensor.transpose(ps[:, 2 + k, t * P:(t + 1) * P], xn[:, t, k * P:(k + 1) * P], ident[:, :])
                last.then_inc(s["xT"], 1)
                pe.wait_ge(s["xTl"], b + 1)
                pe.wait_ge(s["h1"], 2 * b + 1)
                for c in range(4):
                    for k in range(KC):
                        w = slice(c * P, (c + 1) * P)
                        last = mm3(ps[:, 4 + c, 0:N], qkvT_h[:, k, w], qkvT_l[:, k, w], xT_h[:, k, :], xT_l[:, k, :],
                                   k == 0, k == KC - 1)
                    last.then_inc(s["qk"], 1)
                for t in range(T):
                    for k in range(KC):
                        r = slice(t * P, (t + 1) * P)
                        last = mm3(ps[:, 2 + t // 2, (t % 2) * C:(t % 2 + 1) * C], xT_h[:, k, r], xT_l[:, k, r],
                                   qkvT_h[:, k, 2 * C:], qkvT_l[:, k, 2 * C:], k == 0, k == KC - 1)
                last.then_inc(s["vps"], 1)
                pe.wait_ge(s["qk_ev"], 4 * b + 4)
                pe.wait_ge(s["q_hi"], 2 * b + 2)
                pe.wait_ge(s["k_hi"], b + 1)
                for t in range(T):
                    for g in range(4):
                        n = 4 * t + g
                        if n >= 2:
                            pe.wait_ge(s["mx"], 12 * b + n - 1)
                        lo = 0 if t == 0 else t * P - WINDOW
                        w = (t + 1) * P - lo
                        for i in range(4):
                            hh = 4 * g + i
                            c, base, par = heads_slice(hh)
                            o = ps[:, 4 + 2 * (n % 2) + i // 2, (i % 2) * SPAN + SPAN - w:(i % 2 + 1) * SPAN]
                            nc.tensor.matmul(o, q_h[base:base + 32, par, c, t * P:(t + 1) * P], k_h[base:base + 32, c, lo:lo + w],
                                             start=True, stop=False)
                            last = nc.tensor.matmul(o, ident_h[:, :], mask_a[:, hh, SPAN - w:], start=False, stop=True)
                        last.then_inc(s["smax"], 1)
                pe.wait_ge(s["mx"], 12 * b + 12)
                pe.wait_ge(s["vaug"], 2 * b + 2)
                for t in range(T):
                    last = nc.tensor.transpose(ps[0:HEADS, 3, t * P:(t + 1) * P], mx[:, t, :], ident[:, :])
                last.then_inc(s["mxT"], 1)
                pe.wait_ge(s["aug"], b + 1)
                pe.wait_ge(s["lo"], 3 * b + 3)

                def attend(hh):
                    pe.wait_ge(s["exp"], 16 * b + hh + 1)
                    for t in range(T):
                        o = ps[:, t, hh * (HD + 1):(hh + 1) * (HD + 1)]
                        last = nc.tensor.matmul(o, prob[:, hh % 3, t * SPAN:t * SPAN + P], v_aug[:, t, hh, :],
                                                start=True, stop=True)
                        if t > 0:
                            last = nc.tensor.matmul(o[0:WINDOW], prob[:, hh % 3, (t - 1) * SPAN + P:t * SPAN],
                                                    v_aug[:, t - 1, hh, :], start=False, stop=True,
                                                    skip_group_check=True)
                    last.then_inc(s["av"], 1)

                for hh in range(HEADS):
                    c, base, par = heads_slice(hh)
                    if hh >= 3:
                        pe.wait_ge(s["exp"], 16 * b + hh - 2)
                    for j in range(T):
                        w = min(SPAN, N - j * P)
                        o = ps[:, 4 + hh % 3, j * SPAN:j * SPAN + w]
                        km, qn = slice(j * P, (j + 1) * P), slice(j * P, j * P + w)
                        nc.tensor.matmul(o, k_h[base:base + 32, c, km], q_h[base:base + 32, par, c, qn], start=True, stop=False)
                        nc.tensor.matmul(o, k_h[base:base + 32, c, km], q_l[base:base + 32, par, c, qn], start=False, stop=False)
                        nc.tensor.matmul(o, k_l[base:base + 32, c, km], q_h[base:base + 32, par, c, qn], start=False, stop=False)
                        nc.tensor.matmul(o, aug_l[:, j, hh, :], aug_r[:, qn], start=False, stop=False)
                        last = nc.tensor.matmul(o, ident_h[:, :], mask_t[:, 0:w], start=False, stop=True)
                    last.then_inc(s["st"], 1)
                    if hh >= 1:
                        attend(hh - 1)
                attend(HEADS - 1)
                pe.wait_ge(s["ao"], b + 1 + 1)
                for t in range(T):
                    for k in range(KC):
                        last = nc.tensor.transpose(ps[:, 4 + k, t * P:(t + 1) * P], ao[:, t, k * P:(k + 1) * P], ident[:, :])
                last.then_inc(s["aoT"], 1)
                pe.wait_ge(s["aol"], b + 1)
                for t in range(T):
                    for k in range(KC):
                        r = slice(t * P, (t + 1) * P)
                        last = mm3(ps[:, 6 + t // 2, (t % 2) * C:(t % 2 + 1) * C], aoT_h[:, k, r], aoT_l[:, k, r],
                                   projT_h[:, k, :], projT_l[:, k, :], k == 0, k == KC - 1)
                last.then_inc(s["pj"], 1)
            pe.wait_ge(s["h1"], 2 * B + 1)
            pe.wait_ge(s["w_lo"], 4 * EA)
            pe.wait_ge(s["b2_in"], 32)
            with pe.Fori(0, B) as b:
                pe.wait_ge(s["xn2"], b + 1)
                pe.wait_ge(s["acc0"], 2 * b + 1)
                for t in range(T):
                    for k in range(KC):
                        last = nc.tensor.transpose(ps[:, k, t * P:(t + 1) * P], xn[:, t, k * P:(k + 1) * P], ident[:, :])
                last.then_inc(s["xT2"], 1)
                pe.wait_ge(s["x2l"], b + 1)
                for t in range(T):
                    for k in range(KC):
                        r = slice(t * P, (t + 1) * P)
                        last = mm3(ps[:, 2, t * E:(t + 1) * E], x2_h[:, k, r], x2_l[:, k, r], gateT_h[:, k, :], gateT_l[:, k, :],
                                   k == 0, k == KC - 1)
                last.then_inc(s["lg"], 1)
                pe.wait_ge(s["rw"], b + 1)
                for t in range(T):
                    last = nc.tensor.transpose(ps[0:EA, 3, t * P:(t + 1) * P], rw[:, t, :], ident[:, :])
                last.then_inc(s["rwT"], 1)
                pe.wait_ge(s["rwTs"], b + 1)
                for t in range(T):
                    last = nc.tensor.matmul(ps[:, t // 2, (t % 2) * C:(t % 2 + 1) * C], rwT[:, t * P:(t + 1) * P], b2_all[:, :],
                                            start=True, stop=True)
                last.then_inc(s["b2ps"], 1)
                with pe.Fori(0, EA) as e:
                    n = b * EA + e
                    pe.wait_ge(s["acc0"], 2 * b + 2 + 1)
                    for c in range(HC):
                        m = rows_of(c)
                        if c >= 2:
                            pe.wait_ge(s["prod"], n * 3 + 1 + 1)
                        else:
                            pe.wait_ge(s["prod"], n * 3 + 1)
                        for j, (wh, wl) in enumerate(((w3_h, w3_l), (w1_h, w1_l))):
                            for k in range(KC):
                                wv = [a[:, bass.ds(e, 1), k, c * P:c * P + m].rearrange("p a n -> p (a n)") for a in (wh, wl)]
                                last = mm3(ps[0:m, 2 * (c % 2) + j, 0:N], wv[0], wv[1], x2_h[:, k, :], x2_l[:, k, :],
                                           k == 0, k == KC - 1)
                            if j == 0:
                                last.then_inc(s["up"], 1)
                        last.then_inc(s["up"], 1)
                    pe.wait_ge(s["hl"], n * 3 + 3 + 1)
                    for t in range(T):
                        pe.wait_ge(s["yacc"], n * 3 + 1)
                        for c in range(HC):
                            m = rows_of(c)
                            r = slice(t * P, (t + 1) * P)
                            wv = [a[0:m, bass.ds(e, 1), c, :].rearrange("p a n -> p (a n)") for a in (w2_h, w2_l)]
                            last = mm3(ps[:, 4 + t, 0:C], hT_h[0:m, c, r], hT_l[0:m, c, r], wv[0], wv[1], c == 0, c == HC - 1)
                        last.then_inc(s["yps"], 1)

        @block.scalar
        def _(act):
            act.wait_ge(s["consts"], 16 * 11)
            act.wait_ge(s["ones"], 1)
            nc.scalar.copy(ident_h[:, :], ident[:, :]).then_inc(s["identh"], 1)
            act.wait_ge(s["setup_t"], 1)
            for j in range(8):
                for k in range(KC):
                    slot = j * KC + k
                    src = ps[:, slot // 4, 128 * (slot % 4):128 * (slot % 4) + P]
                    dst = qkvT_h[:, k, j * P:(j + 1) * P] if j < 6 else projT_h[:, k, (j - 6) * P:(j - 5) * P]
                    nc.scalar.copy(dst, src)
            nc.scalar.copy(gateT_h[:, :, :], ps[:, 4, 0:256].rearrange("p (k n) -> p k n", k=KC)[:, :, 0:E]).then_inc(s["setup_h"], 1)
            for c in range(HC):
                nc.scalar.copy(bias1[:, c, :], ps[:, 5, c * P:c * P + EA])
                nc.scalar.copy(bias3[:, c, :], ps[:, 6, c * P:c * P + EA]).then_inc(s["bias_done"], 1)
            nc.scalar.copy(bq4[:, 2:6], ps[:, 4, 256 + 2:256 + 6])
            nc.scalar.mul(bq4[:, 0:2], ps[:, 4, 256:256 + 2], SCALE).then_inc(s["bias_done"], 1)
            act.wait_ge(s["bias_done"], 4)
            with act.Fori(0, B) as b:
                for f in range(2):
                    act.wait_ge(s["conv"], 2 * b + f + 1 + 1)
                    act.wait_ge(s["edge"], 2 * b + 1)
                    nc.scalar.activation(ab[:, f], ps[:, f, :].rearrange("p (q w) -> p q w", q=2), ACT.Abs, scale=0.5).then_inc(s["absd"], 1)
                act.wait_ge(s["var1"], b + 1)
                nc.scalar.activation(std[:, :], mv[:, :, 1], ACT.Sqrt, bias=eps[:, :]).then_inc(s["std1"], 1)
                act.wait_ge(s["xT"], b + 1)
                nc.scalar.copy(xT_h[:, :, :], ps[:, 2:4, 0:N]).then_inc(s["xTh"], 1)
                for c in range(4):
                    act.wait_ge(s["qk"], 4 * b + c + 1)
                    dst = (qs if c < 2 else ks)[:, c % 2, :]
                    nc.scalar.activation(dst, ps[:, 4 + c, 0:N], ACT.Identity, scale=SCALE if c < 2 else 1.0,
                                         bias=bq4[:, c:c + 1]).then_inc(s["qk_ev"], 1)
                act.wait_ge(s["qk_ev"], 4 * b + 4)
                for par in range(2):
                    nc.scalar.activation(q_h[:, par], qs[:, :, :], ACT.Copy, scale=parity[:, par:par + 1]).then_inc(s["q_hi"], 1)
                nc.scalar.copy(k_h[:, :, :], ks[:, :, :]).then_inc(s["k_hi"], 1)
                act.wait_ge(s["mxT"], b + 1)
                nc.scalar.mul(aug_r[0:HEADS, :], ps[0:HEADS, 3, 0:N], -1.0).then_inc(s["aug"], 1)
                for hh in range(HEADS):
                    act.wait_ge(s["st"], 16 * b + hh + 1)
                    if hh >= 3:
                        act.wait_ge(s["av"], 16 * b + hh - 2)
                    nc.scalar.activation(prob[:, hh % 3, :], ps[:, 4 + hh % 3, :], ACT.Exp).then_inc(s["exp"], 1)
                act.wait_ge(s["aoT"], b + 1)
                nc.scalar.copy(aoT_h[:, :, :], ps[:, 4:6, 0:N]).then_inc(s["aoh"], 1)
            for e in range(EA):
                act.wait_ge(s["wload"], 64 * (e + 1))
                d = stage[:, e % 2, :]
                nc.scalar.copy(w1_h[:, e], d[:, 0:NW].rearrange("p (k n) -> p k n", k=KC)).then_inc(s["w_hi"], 1)
                nc.scalar.copy(w3_h[:, e], d[:, NW:2 * NW].rearrange("p (k n) -> p k n", k=KC)).then_inc(s["w_hi"], 1)
                nc.scalar.copy(w2_h[:, e, 0:2], d[:, 2 * NW:2 * NW + 2 * C].rearrange("p (k n) -> p k n", k=2)).then_inc(s["w_hi"], 1)
                nc.scalar.copy(w2_h[0:HLAST, e, 2], d[0:HLAST, 2 * NW + 2 * C:]).then_inc(s["w_hi"], 1)
            with act.Fori(0, B) as b:
                act.wait_ge(s["var2"], b + 1)
                nc.scalar.activation(std[:, :], mv[:, :, 1], ACT.Sqrt, bias=eps[:, :]).then_inc(s["std2"], 1)
                act.wait_ge(s["xT2"], b + 1)
                nc.scalar.copy(x2_h[:, :, :], ps[:, 0:2, 0:N]).then_inc(s["x2h"], 1)
                act.wait_ge(s["rmax"], b + 1)
                nc.scalar.activation(rex[:, :, :], lgs[:, :, :], ACT.Exp).then_inc(s["rexp"], 1)
                act.wait_ge(s["rwT"], b + 1)
                nc.scalar.copy(rwT[:, :], ps[0:EA, 3, 0:N]).then_inc(s["rwTs"], 1)
                with act.Fori(0, EA) as e:
                    n = b * EA + e
                    for c in range(HC):
                        m = rows_of(c)
                        act.wait_ge(s["up"], n * 6 + 2 * c + 1)
                        if c < 2:
                            act.wait_ge(s["prod"], n * 3 + 1)
                        else:
                            act.wait_ge(s["prod"], n * 3 + 1 + 1)
                        nc.scalar.activation(u3[0:m, c % 2, :], ps[0:m, 2 * (c % 2), 0:N], ACT.Identity,
                                             bias=bias3[0:m, c, bass.ds(e, 1)]).then_inc(s["u3"], 1)
                        act.wait_ge(s["prod"], n * 3 + c + 1 + 1)
                        act.wait_ge(s["hl"], n * 3 + max(c - 1, 0) + 1)
                        nc.scalar.activation(hs[0:m, c % 2, :], tt[0:m, c % 2, :], ACT.Silu).then_inc(s["silu"], 1)

        @block.vector
        def _(dve):
            count = [0]

            def link(ins):
                count[0] += 1
                ins.then_inc(s["chain"], 1)
                dve.wait_ge(s["chain"], count[0])

            nc.vector.memset(rows[:, :, :], 0.0).then_inc(s["pads"], 1)
            nc.vector.memset(rows_b3[:, :, :], 0.0).then_inc(s["pads"], 1)
            nc.vector.memset(gray[:, :, :], 0.0)
            nc.vector.memset(eps[:, :], EPS)
            nc.vector.memset(zero[:, :], 0.0)
            nc.vector.memset(v_aug[:, :, :, HD:HD + 1], 1.0).then_inc(s["ones"], 1)
            dve.wait_ge(s["consts"], 16 * 11)
            dve.wait_ge(s["filt_in"], 16)
            for q in range(2):
                for dx in range(3):
                    i = 3 * q + dx
                    for dy in range(3):
                        fk = filt[:, 9 * q + 3 * dy + dx:9 * q + 3 * dy + dx + 1]
                        if dy == 0:
                            link(nc.vector.tensor_scalar(band[:, i, :], shift[:, dy, :], fk, None, ALU.mult))
                        else:
                            link(nc.vector.scalar_tensor_tensor(band[:, i, :], shift[:, dy, :], fk, band[:, i, :], ALU.mult, ALU.add))
                    link(nc.vector.tensor_scalar(corner[:, i, 0, :], shift[:, 3, :], filt[:, 9 * q + 6 + dx:9 * q + 7 + dx], None, ALU.mult))
                    ins = nc.vector.tensor_scalar(corner[:, i, 1, :], shift[:, 4, :], filt[:, 9 * q + dx:9 * q + dx + 1], None, ALU.mult)
                    if i < 5:
                        link(ins)
            ins.then_inc(s["filt_done"], 1)
            dve.wait_ge(s["setup_h"], 1)
            dve.wait_ge(s["bias_done"], 4)
            for j in range(8):
                for k in range(KC):
                    slot = j * KC + k
                    src = ps[:, slot // 4, 128 * (slot % 4):128 * (slot % 4) + P]
                    dst, hi = ((qkvT_l[:, k, j * P:(j + 1) * P], qkvT_h[:, k, j * P:(j + 1) * P]) if j < 6 else
                               (projT_l[:, k, (j - 6) * P:(j - 5) * P], projT_h[:, k, (j - 6) * P:(j - 5) * P]))
                    ins = nc.vector.tensor_tensor(dst, src, hi, ALU.subtract)
            ins.then_inc(s["setup_l"], 2)
            nc.vector.tensor_tensor(gateT_l[:, :, :], ps[:, 4, 0:256].rearrange("p (k n) -> p k n", k=KC)[:, :, 0:E], gateT_h[:, :, :],
                                    ALU.subtract).then_inc(s["setup_l"], 1)
            def norm(src, out_sem, seq, base, per, tag, b):
                k = [0]

                def seq_link(ins):
                    k[0] += 1
                    ins.then_inc(seq, 1)
                    dve.wait_ge(seq, base + k[0])

                for t in range(T):
                    ins = nc.vector.bn_stats(stats[:, t, :], src(t))
                    if t == T - 1:
                        seq_link(ins)
                nc.vector.memset(gate_v[:, :], 0.0)
                for t in range(T):
                    ins = nc.vector.bn_aggr(mv[:, t, :], stats[:, t, :])
                ins.then_inc(s["var" + tag], 1)
                dve.wait_ge(s["std" + tag], b + 1)
                seq_link(nc.vector.reciprocal(rstd[:, :], std[:, :]))
                for t in range(T):
                    ins = nc.vector.tensor_scalar(xn[:, t, :], src(t), mv[:, t, 0:1], rstd[:, t:t + 1], ALU.subtract, ALU.mult)
                ins.then_inc(out_sem, 1)
                assert k[0] == per

            CH = 5
            with dve.Fori(0, B) as b:
                base = b * CH + count[0]
                dve.wait_ge(s["x_in"], b * 32 + 32)
                dve.wait_ge(s["conv"], 2 * b + 1)
                g = gray[:, :, 1:IMG + 1]
                nc.vector.tensor_scalar(g, xin[:, :, 0], GRAY_W[0], None, ALU.mult).then_inc(s["chain"], 1)
                dve.wait_ge(s["chain"], base + 1)
                nc.vector.scalar_tensor_tensor(g, xin[:, :, 1], GRAY_W[1], g, ALU.mult, ALU.add).then_inc(s["chain"], 1)
                dve.wait_ge(s["chain"], base + 2)
                nc.vector.scalar_tensor_tensor(g, xin[:, :, 2], GRAY_W[2], g, ALU.mult, ALU.add).then_inc(s["gray"], 1)
                dve.wait_ge(s["hp"], b + 1)
                for f in range(2):
                    dve.wait_ge(s["absd"], 2 * b + f + 1)
                    nc.vector.tensor_tensor(h[:, f, :], ab[:, f, 0, :], ab[:, f, 1, :], ALU.add).then_inc(s["edge"], 1)
                dve.wait_ge(s["edge"], 2 * b + 2 + 1)
                dve.wait_ge(s["txt_in"], 16 * b + 16)
                norm(lambda t: h[:, t, :], s["xn"], s["chain"], base + 2, 2, "1", b)
                dve.wait_ge(s["xTh"], b + 1)
                nc.vector.tensor_tensor(xT_l[:, :, :], ps[:, 2:4, 0:N], xT_h[:, :, :], ALU.subtract).then_inc(s["xTl"], 1)
                dve.wait_ge(s["vps"], b + 1)
                dve.wait_ge(s["ones"], 1)
                nc.vector.tensor_tensor(v_aug[:, 0:2, :, 0:HD], ps[:, 2, :].rearrange("p (t h d) -> p t h d", t=2, h=HEADS),
                                        bv[:, :].rearrange("p (a h d) -> p a h d", a=1, h=HEADS).to_broadcast([P, 2, HEADS, HD]),
                                        ALU.add).then_inc(s["vaug"], 1)
                nc.vector.tensor_tensor(v_aug[:, 2, :, 0:HD], ps[:, 3, 0:C].rearrange("p (h d) -> p h d", h=HEADS),
                                        bv[:, :].rearrange("p (h d) -> p h d", h=HEADS), ALU.add).then_inc(s["vaug"], 1)
                for n in range(4 * T):
                    dve.wait_ge(s["smax"], 12 * b + n + 1)
                    t, gq = n // 4, n % 4
                    w = P if t == 0 else SPAN
                    src = ps[:, 4 + 2 * (n % 2):6 + 2 * (n % 2), 0:2 * SPAN].rearrange("p k (i w) -> p k i w", i=2)[:, :, :, SPAN - w:]
                    nc.vector.tensor_reduce(mx[:, t, 4 * gq:4 * gq + 4].rearrange("p (k i) -> p k i", k=2), src, AX, ALU.max).then_inc(s["mx"], 1)
                    if n == 2:
                        dve.wait_ge(s["q_hi"], 2 * b + 2)
                        for par in range(2):
                            nc.vector.scalar_tensor_tensor(q_l[:, par], qs[:, :, :], parity[:, par:par + 1], q_h[:, par],
                                                           ALU.mult, ALU.subtract).then_inc(s["lo"], 1)
                        dve.wait_ge(s["k_hi"], b + 1)
                        nc.vector.tensor_tensor(k_l[:, :, :], ks[:, :, :], k_h[:, :, :], ALU.subtract).then_inc(s["lo"], 1)
                dve.wait_ge(s["av"], 16 * b + 16)
                av = ps[:, 0:T, 0:HEADS * (HD + 1)].rearrange("p t (h d) -> p t h d", h=HEADS)
                nc.vector.reciprocal(rs[:, :, :], av[:, :, :, HD]).then_inc(s["chain"], 1)
                dve.wait_ge(s["chain"], base + CH)
                nc.vector.tensor_tensor(ao[:, :, :].rearrange("p t (h d) -> p t h d", h=HEADS), av[:, :, :, 0:HD],
                                        rs[:, :, :].rearrange("p t (h a) -> p t h a", a=1).to_broadcast([P, T, HEADS, HD]),
                                        ALU.mult).then_inc(s["ao"], 1)
                dve.wait_ge(s["aoh"], b + 1)
                nc.vector.tensor_tensor(aoT_l[:, :, :], ps[:, 4:6, 0:N], aoT_h[:, :, :], ALU.subtract).then_inc(s["aol"], 1)
                dve.wait_ge(s["pj"], b + 1)
                dve.wait_ge(s["hp"], b + 1 + 1)
                nc.vector.tensor_tensor(h1[:, bass.ds(b * T, 2), :], ps[:, 6, :].rearrange("p (t d) -> p t d", t=2), hp[:, 0:2, :], ALU.add).then_inc(s["h1"], 1)
                nc.vector.tensor_tensor(h1[:, bass.ds(b * T + 2, 1), :], ps[:, 7:8, 0:C], hp[:, 2:3, :], ALU.add).then_inc(s["h1"], 1)
            for e in range(EA):
                d = stage[:, e % 2, :]
                dve.wait_ge(s["w_hi"], 4 * e + 4)
                nc.vector.tensor_tensor(w1_l[:, e], d[:, 0:NW].rearrange("p (k n) -> p k n", k=KC), w1_h[:, e], ALU.subtract).then_inc(s["w_lo"], 1)
                nc.vector.tensor_tensor(w3_l[:, e], d[:, NW:2 * NW].rearrange("p (k n) -> p k n", k=KC), w3_h[:, e], ALU.subtract).then_inc(s["w_lo"], 1)
                nc.vector.tensor_tensor(w2_l[:, e, 0:2], d[:, 2 * NW:2 * NW + 2 * C].rearrange("p (k n) -> p k n", k=2), w2_h[:, e, 0:2],
                                        ALU.subtract).then_inc(s["w_lo"], 1)
                nc.vector.tensor_tensor(w2_l[0:HLAST, e, 2], d[0:HLAST, 2 * NW + 2 * C:], w2_h[0:HLAST, e, 2], ALU.subtract).then_inc(s["w_lo"], 1)

            dve.wait_ge(s["h1"], 2 * B + 1)
            nc.vector.memset(rw[:, :, :], 1.0).then_inc(s["ones"], 1)
            dve.wait_ge(s["ones"], 2)
            CB = 13
            with dve.Fori(0, B) as b:
                base = b * CB
                k = [2]

                def link2(ins):
                    k[0] += 1
                    ins.then_inc(s["chain2"], 1)
                    dve.wait_ge(s["chain2"], base + k[0])

                norm(lambda t: h1[:, bass.ds(b * T + t, 1), :].rearrange("p a n -> p (a n)"), s["xn2"], s["chain2"], base, 2, "2", b)
                dve.wait_ge(s["x2h"], b + 1)
                nc.vector.tensor_tensor(x2_l[:, :, :], ps[:, 0:2, 0:N], x2_h[:, :, :], ALU.subtract).then_inc(s["x2l"], 1)
                dve.wait_ge(s["lg"], b + 1)
                lg = ps[:, 2, 0:T * E].rearrange("p (t e) -> p t e", t=T)
                link2(nc.vector.tensor_reduce(rmax[:, :], lg, AX, ALU.max))
                nc.vector.tensor_tensor(lgs[:, :, :], lg, rmax[:, :].rearrange("p (t a) -> p t a", a=1).to_broadcast([P, T, E]),
                                        ALU.subtract).then_inc(s["rmax"], 1)
                dve.wait_ge(s["rexp"], b + 1)
                link2(nc.vector.tensor_reduce(rsum[:, :], rex[:, :, :], AX, ALU.add))
                link2(nc.vector.reciprocal(rmax[:, :], rsum[:, :]))
                link2(nc.vector.tensor_tensor(score[:, :, :], rex[:, :, :], rmax[:, :].rearrange("p (t a) -> p t a", a=1).to_broadcast([P, T, E]), ALU.mult))
                link2(nc.vector.tensor_tensor(biased[:, :, :], score[:, :, :], gb[:, :].rearrange("p (a e) -> p a e", a=1).to_broadcast([P, T, E]), ALU.add))
                for t in range(T):
                    bi = biased[:, t, :]
                    other = bi.rearrange("p (a e) -> p a e", a=1).to_broadcast([P, E, E])
                    own = bi.rearrange("p (e a) -> p e a", a=1).to_broadcast([P, E, E])
                    nc.vector.tensor_tensor(cmp1[:, t], other, own, ALU.is_gt)
                    ins = nc.vector.tensor_tensor(cmp2[:, t], other, own, ALU.is_equal)
                link2(ins)
                link2(nc.vector.tensor_tensor(cmp2[:, :, :, :], cmp2[:, :, :, :],
                                              before[:, :, :].rearrange("p (a e) f -> p a e f", a=1).to_broadcast([P, T, E, E]), ALU.mult))
                link2(nc.vector.tensor_tensor(cmp1[:, :, :, :], cmp1[:, :, :, :], cmp2[:, :, :, :], ALU.add))
                link2(nc.vector.tensor_reduce(rank[:, :, :], cmp1[:, :, :, :], AX, ALU.add))
                link2(nc.vector.tensor_scalar(rank[:, :, :], rank[:, :, :], 1.5, None, ALU.is_lt))
                nc.vector.tensor_tensor(rw[:, :, 0:E], score[:, :, :], rank[:, :, :], ALU.mult).then_inc(s["rw"], 1)
                link2(nc.vector.tensor_copy(rmax[:, :], rsum[:, :]))
                assert k[0] == CB
                dve.wait_ge(s["b2ps"], b + 1)
                dve.wait_ge(s["outd"], 16 * b + 1)
                nc.vector.tensor_tensor(acc[:, 0:2, :], ps[:, 0, :].rearrange("p (t d) -> p t d", t=2), h1[:, bass.ds(b * T, 2), :], ALU.add).then_inc(s["acc0"], 1)
                nc.vector.tensor_tensor(acc[:, 2:3, :], ps[:, 1:2, 0:C], h1[:, bass.ds(b * T + 2, 1), :], ALU.add).then_inc(s["acc0"], 1)
                with dve.Fori(0, EA) as e:
                    n = b * EA + e
                    dve.wait_ge(s["acc0"], 2 * b + 2 + 1)
                    for c in range(HC):
                        m = rows_of(c)
                        dve.wait_ge(s["up"], n * 6 + 2 * c + 2)
                        dve.wait_ge(s["u3"], n * 3 + c + 1)
                        if c < 2:
                            dve.wait_ge(s["silu"], n * 3 + 1)
                        else:
                            dve.wait_ge(s["silu"], n * 3 + 1 + 1)
                        nc.vector.scalar_tensor_tensor(tt[0:m, c % 2, :], ps[0:m, 2 * (c % 2) + 1, 0:N], bias1[0:m, c, bass.ds(e, 1)],
                                                       u3[0:m, c % 2, :], ALU.add, ALU.mult).then_inc(s["prod"], 1)
                        dve.wait_ge(s["hh"], n * 3 + c + 1)
                        dve.wait_ge(s["yps"], n * 3 + 1)
                        nc.vector.tensor_tensor(hT_l[0:m, c, :], hs[0:m, c % 2, :], hT_h[0:m, c, :], ALU.subtract).then_inc(s["hl"], 1)
                    for t in range(T):
                        dve.wait_ge(s["yps"], n * 3 + t + 1 + 1)
                        dve.wait_ge(s["yacc"], n * 3 + 1)
                        nc.vector.scalar_tensor_tensor(acc[:, t, :], ps[:, 4 + t, 0:C], rw[:, t, bass.ds(e, 1)], acc[:, t, :],
                                                       ALU.mult, ALU.add).then_inc(s["yacc"], 1)

        @block.gpsimd
        def _(pool):
            pool.wait_ge(s["consts"], 16 * 11)
            pool.wait_ge(s["ones"], 1)
            with pool.Fori(0, B) as b:
                pool.wait_ge(s["edge"], 2 * b + 2 + 1)
                pool.wait_ge(s["txt_in"], 16 * b + 16)
                pool.wait_ge(s["h1"], 2 * b + 1)
                nc.gpsimd.tensor_tensor(hp[:, :, :], h[:, :, :], pb[:, :].rearrange("p (a c) -> p a c", a=1).to_broadcast([P, T, C]),
                                        ALU.add).then_inc(s["hp"], 1)
            with pool.Fori(0, B) as b:
                with pool.Fori(0, EA) as e:
                    n = b * EA + e
                    for c in range(HC):
                        m = rows_of(c)
                        pool.wait_ge(s["silu"], n * 3 + c + 1 + 1)
                        pool.wait_ge(s["yps"], n * 3 + 1)
                        nc.gpsimd.tensor_tensor(hT_h[0:m, c, :], hs[0:m, c % 2, :], zero[0:m, :].to_broadcast([m, N]), ALU.add).then_inc(s["hh"], 1)


_INS = ['x', 'txt', 'L0_tok_scharr', 'L0_attn_qkv_w', 'L0_attn_qkv_b', 'L0_attn_proj_w', 'L0_attn_proj_b',
        'L0_ffn_gate_w', 'L0_ffn_gate_b', 'L0_ffn_w1', 'L0_ffn_b1', 'L0_ffn_w3', 'L0_ffn_b3', 'L0_ffn_w2', 'L0_ffn_b2',
        'L0_ffn_sw1', 'L0_ffn_sb1', 'L0_ffn_sw3', 'L0_ffn_sb3', 'L0_ffn_sw2', 'L0_ffn_sb2']


def shape_constants(T, E):
    import numpy as np
    heads, window, p = HEADS, WINDOW, P
    i = np.arange(p)
    eye = np.eye(p, dtype=np.float32)
    shift = np.zeros((p, 5, p), np.float32)
    for dy in range(3):
        shift[:, dy, :] = (i[:, None] == i[None, :] + dy - 1)
    shift[0, 3, p - 1] = 1
    shift[p - 1, 4, 0] = 1
    base = 2.0 ** (-2.0 ** (-(np.log2(heads) - 3)))
    slopes = (np.float64(base) ** np.arange(1, heads + 1, dtype=np.float32)).astype(np.float32).astype(np.float64)
    off = -30000.0
    n, m = i[:, None], np.arange(-window, p)[None, :]
    ok = (m <= n) & (n - m < window)
    mask_a = np.where(ok[:, None, :], slopes[None, :, None] * (m - n)[:, None, :], off).astype(np.float16)
    m, n = i[:, None], np.arange(p + window)[None, :]
    mask_t = np.where((m <= n) & (n - m < window), 0.0, off).astype(np.float16)

    def parts(v):
        out = []
        for _ in range(3):
            a = v.astype(np.float16)
            out.append(a)
            v = v - a.astype(np.float64)
        return out

    aug_l = np.zeros((64, T, heads, p), np.float16)
    aug_r = np.zeros((64, T * p), np.float16)
    for h in range(heads):
        aug_l[h, :, h, :] = 1
    for t in range(T):
        key = slopes[:, None] * (t * p + i)[None, :]
        for j, a in enumerate(parts(key)):
            aug_l[heads + j, t] = a
        for j, a in enumerate(parts(-slopes)):
            aug_l[heads + 3 + j, t] = a[:, None]
    aug_r[heads:heads + 3] = 1
    aug_r[heads + 3:heads + 6] = np.arange(T * p)
    par = ((i[:, None] // HD) % 2 == np.arange(2)[None, :]).astype(np.float32)
    before = np.broadcast_to((np.arange(E)[None, :] < np.arange(E)[:, None]).astype(np.float32), (p, E, E)).copy()
    return [("ident", eye), ("shift", shift), ("mask_a", mask_a), ("mask_t", mask_t), ("aug_l", aug_l),
            ("aug_r", aug_r), ("parity", par), ("before", before)]


def kernel(**inputs):
    import numpy as _np
    import concourse.bacc as _bacc
    from concourse import mybir as _mybir
    from concourse.bass_utils import run_bass_kernel_spmd as _run

    nc = _bacc.Bacc("TRN2", target_bir_lowering=False, num_devices=1)
    arrays, args = {}, []
    items = [(n, _np.ascontiguousarray(inputs[n])) for n in _INS]
    B, rows = inputs['x'].shape[0], inputs['x'].shape[2] + inputs['txt'].shape[1]
    items += shape_constants(rows // P, inputs['L0_ffn_w1'].shape[0])
    for name, a in items:
        arrays[f"in_{name}_dram"] = a
        args.append(nc.dram_tensor(f"in_{name}_dram", a.shape, _mybir.dt.from_np(a.dtype), kind="ExternalInput").ap())
    args.append(nc.dram_tensor("out_dram", (B, rows, C), _mybir.dt.float32, kind="ExternalOutput").ap())
    program(nc, *args)
    r = _run(nc, [arrays], core_ids=[0])
    return r.results[0]["out_dram"]
```

```python
from contextlib import ExitStack

import concourse.bass as bass
from concourse import mybir

F32 = mybir.dt.float32
F16 = mybir.dt.float16
U32 = mybir.dt.uint32
I32 = mybir.dt.int32
ALU = mybir.AluOpType
ACT = mybir.ActivationFunctionType
AX = mybir.AxisListType.X

P = 128
IMG = 256
C = 256
KC = C // P
HEADS, HD = 16, 16
QUADS, G = 4, 4
WINDOW = 64
SCALE = HD ** -0.5
SPAN = P + WINDOW
EPS = 1e-5
HID = 352
HC = 3
HLAST = HID - 2 * P
TW = 2 * P
GRAY_W = (0.2989, 0.587, 0.114)
FB = 6


def tile_count(tokens, experts):
    n = (2 * tokens + experts * (TW - 1)) // TW
    return n + n % 2


def head_of(q, g):
    return 8 * (q // 2) + 2 * g + q % 2


def need(eng, sem, value):
    if not (isinstance(value, int) and value <= 0):
        eng.wait_ge(sem, value)


def program(nc, x, txt, scharr, qkv_w, qkv_b, proj_w, proj_b, gate_w, gate_b, w1, b1, w3, b3, w2, b2,
            sw1, sb1, sw3, sb3, sw2, sb2, k_ident, k_shift, k_mask_a, k_mask_t, k_aug_l, k_aug_c,
            k_parity, k_before, k_tri, k_ebase, k_pad, k_tile, out):
    B = x.shape[0]
    E = w1.shape[0]
    EA = E + 1
    T = (IMG + txt.shape[1]) // P
    N = T * P
    REGION = B * N + TW
    NT = tile_count(B * N, E)
    NW = KC * HID
    xs_d = nc.dram_tensor("xs_scratch", (E * REGION, C), F32, kind="Internal").ap()
    ys_d = nc.dram_tensor("ys_scratch", (NT * TW, C), F32, kind="Internal").ap()
    h1_d = nc.dram_tensor("h1_scratch", (B, P, T, C), F32, kind="Internal").ap()
    x2_d = nc.dram_tensor("x2_scratch", (B, P, 2, KC, N), F16, kind="Internal").ap()

    with ExitStack() as ctx:
        def sb(name, shape, dt=F32):
            return ctx.enter_context(nc.sbuf_tensor(name, shape, dt))

        ps = ctx.enter_context(nc.psum_tensor("ps", [P, 8, 512], F32))

        before = sb("before", [P, E, E])
        tri = sb("tri", [P, 2, P], F16)
        ident = sb("ident", [P, P])
        ebase = sb("ebase", [P, E])
        padbase = sb("padbase", [P, 2, E])
        sb2b = sb("sb2b", [P, C])
        bias1 = sb("bias1", [P, HC, EA])
        bias3 = sb("bias3", [P, HC, EA])
        one_v = sb("one_v", [P, 1])
        one_p = sb("one_p", [P, 64])
        one_a = sb("one_a", [P, 1])
        zero = sb("zero", [P, 1])
        eps = sb("eps", [P, 1])
        place = sb("place", [P, B * T, 2])
        dest = sb("dest", [P, B * T, 2], U32)
        wts = sb("wts", [P, B * T, 2])
        counts = sb("counts", [P, E], F16)
        padidx = sb("padidx", [P, 2, E], U32)
        zrow = sb("zrow", [P, C])
        tile_i = sb("tile_i", [P, E], I32)
        tile_f = sb("tile_f", [P, E])
        back = sb("back", [P, E])
        tile_cum = sb("tile_cum", [1, E])
        tile_red = sb("tile_red", [1, 4, NT])
        tile_tab = sb("tile_tab", [1, 2, NT], I32)
        w1_h = sb("w1_h", [P, EA, KC, HID], F16)
        w1_l = sb("w1_l", [P, EA, KC, HID], F16)
        w3_h = sb("w3_h", [P, EA, KC, HID], F16)
        w3_l = sb("w3_l", [P, EA, KC, HID], F16)
        w2_h = sb("w2_h", [P, EA, HC, C], F16)
        w2_l = sb("w2_l", [P, EA, HC, C], F16)

        with ExitStack() as pa:
            def sa(name, shape, dt=F32):
                return pa.enter_context(nc.sbuf_tensor(name, shape, dt))
            stage = sa("stage", [P, 2 * NW + HC * C])
            nat = stage[:, 0:8 * C].rearrange("p (j c) -> p j c", c=C)
            ident_h = sa("ident_h", [P, P], F16)
            mask_a = sa("mask_a", [P, HEADS, SPAN], F16)
            mask_t = sa("mask_t", [P, SPAN], F16)
            aug_l = sa("aug_l", [P, T, QUADS, P], F16)
            aug_c = sa("aug_c", [P, N], F16)
            parity = sa("parity", [P, 2])
            filt = sa("filt", [P, 18])
            band = sa("band", [P, 6, P])
            corner = sa("corner", [P, 6, P])
            bq4 = sa("bq4", [P, 6])
            bv = sa("bv", [P, C])
            pb = sa("pb", [P, C])
            gb = sa("gb", [P, E])
            qkvT_h = sa("qkvT_h", [P, KC, 3 * C], F16)
            qkvT_l = sa("qkvT_l", [P, KC, 3 * C], F16)
            projT_h = sa("projT_h", [P, KC, C], F16)
            projT_l = sa("projT_l", [P, KC, C], F16)
            gateT_h = sa("gateT_h", [P, KC, E], F16)
            gateT_l = sa("gateT_l", [P, KC, E], F16)
            xin = sa("xin", [P, 2, 3, IMG])
            gray = sa("gray", [P, 2, IMG + 2])
            ab = sa("ab", [P, 2, IMG])
            h = sa("h", [P, T, C])
            hp = sa("hp", [P, 2, T, C])
            stats = sa("stats", [P, 2, T, 6])
            mv = sa("mv", [P, 2, T, 2])
            std = sa("std", [P, 2, T])
            rstd = sa("rstd", [P, 2, T])
            xn1 = sa("xn1", [P, T, C])
            xT_h = sa("xT_h", [P, KC, N], F16)
            xT_l = sa("xT_l", [P, KC, N], F16)
            qs = sa("qs", [P, 2, N])
            q_h = sa("q_h", [P, 2, 2, 2, N], F16)
            q_l = sa("q_l", [P, 2, 2, 2, N], F16)
            k_h = sa("k_h", [P, 2, 2, N], F16)
            k_l = sa("k_l", [P, 2, 2, N], F16)
            v_aug = sa("v_aug", [P, 2, T, HEADS, HD + 1])
            mx = sa("mx", [P, T, P])
            aug_r = sa("aug_r", [P, N], F16)
            prob = sa("prob", [P, 2, G, 512])
            flat = prob[:, :, :, :].rearrange("p a g n -> p (a g n)")
            shift = flat[:, 0:5 * P].rearrange("p (j n) -> p j n", j=5)
            rows_b1 = flat[0:EA, 8 * P:11 * P].rearrange("p (c n) -> p c n", c=HC)
            rows_b3 = flat[0:EA, 11 * P:14 * P].rearrange("p (c n) -> p c n", c=HC)
            rows_qb = flat[0:6, 14 * P:15 * P]
            gate_n = flat[0:E, 16 * P:18 * P]
            rs = sa("rs", [P, T, G])
            ao = sa("ao", [P, T, C])
            aoT_h = sa("aoT_h", [P, KC, N], F16)
            aoT_l = sa("aoT_l", [P, KC, N], F16)
            h1 = sa("h1", [P, T, C])
            xn2 = sa("xn2", [P, T, C])
            x2 = sa("x2", [P, 2, KC, N], F16)
            lgs = sa("lgs", [P, T, E])
            rmax = sa("rmax", [P, T])
            rex = sa("rex", [P, T, E])
            rsum = sa("rsum", [P, T])
            rinv = sa("rinv", [P, T])
            score = sa("score", [P, T, E])
            biased = sa("biased", [P, T, E])
            cmp1 = sa("cmp1", [P, T, E, E])
            cmp2 = sa("cmp2", [P, T, E, E])
            rank = sa("rank", [P, T, E])
            pick = sa("pick", [P, T, 2, E])
            pickw = sa("pickw", [P, T, 2, E])
            chosen = sa("chosen", [P, T, E], F16)
            chosen_n = sa("chosen_n", [P, E])
            slot = sa("slot", [P, T, E])
            slot_f = sa("slot_f", [P, T, 2])
            idx = sa("idx", [P, T, 2], U32)

        with ExitStack() as pe_:
            def se(name, shape, dt=F32):
                return pe_.enter_context(nc.sbuf_tensor(name, shape, dt))
            tilerow = se("tilerow", [1, NT, E])
            tile_cmp = se("tile_cmp", [1, NT, E])
            tile_mul = se("tile_mul", [1, NT, E])
            moved = se("moved", [P, E, B * T, 2])
            b2b = se("b2b", [P, E, C])
            xg = se("xg", [P, 2, 2, C])
            xe_h = se("xe_h", [P, 2, KC, TW], F16)
            xe_l = se("xe_l", [P, 2, KC, TW], F16)
            yo = se("yo", [P, 2, 2, C])
            x2c = se("x2c", [P, 2, 2, KC, N], F16)
            h1c = se("h1c", [P, 2, T, C])
            yg = se("yg", [P, 2, T, 2, C])
            idxc = se("idxc", [P, 2, T, 2], U32)
            acc = se("acc", [P, 2, T, C])
            u3 = se("u3", [P, 2, N])
            prd = se("prd", [P, 2, N])
            hs = se("hs", [P, 2, N])
            hT_h = se("hT_h", [P, 2, HC, N], F16)
            hT_l = se("hT_l", [P, 2, HC, N], F16)

        s = {n: ctx.enter_context(nc.semaphore(n)) for n in (
            "consts", "consts2", "nat_in", "rb_in", "pads", "ones", "ident_h", "setup_t", "setup_h", "setup_l",
            "bias_done", "filt_done", "chain", "w_in", "w_hi", "w_lo",
            "x_in", "txt_in", "gsum", "gray", "conv", "absd", "edge", "hp", "var1", "std1", "rst1", "xn1", "xT", "xTh", "xTl",
            "qk", "q_ev", "vps", "vaug", "q_hi", "k_hi", "q_lo", "k_lo", "smax", "mx", "mxT", "aug", "st", "exp", "av",
            "rs", "ao", "aoT", "aoh", "aol", "pj", "h1", "var2", "std2", "rst2", "xn2", "xT2", "x2h", "x2l",
            "lg", "rmax", "lgs", "rexp", "chosen", "pos", "rt", "pp", "idx", "h1s", "h1_out", "x2_out", "scat",
            "stat1", "stat2",
            "total", "padidx", "padsc", "tab", "tabc",
            "xg0", "xg1", "xT3", "xeh", "xel", "up", "u3", "prod", "silu", "hh", "hl", "yps", "yo", "st0", "st1",
            "cx0", "cx1", "ch0", "ch1", "idxc", "g0", "g1", "cup", "cu3", "cprod", "csilu", "chh", "chl", "cyps",
            "cacc", "cfirst", "cdone", "co0", "co1")}
        N_CONST, N_CONST2 = 8, 8

        def mm3(out_ap, lh, ll, rh, rl, start, stop):
            nc.tensor.matmul(out_ap, lh, rh, start=start, stop=False)
            nc.tensor.matmul(out_ap, lh, rl, start=False, stop=False)
            return nc.tensor.matmul(out_ap, ll, rh, start=False, stop=stop)

        def row(v):
            return v.rearrange("(a n) -> a n", a=1)

        def rows_of(c):
            return P if c < HC - 1 else HLAST

        def bank_tiles(k):
            return ps[:, FB + k, :].rearrange("p (t d) -> p t d", t=2) if k == 0 else ps[:, FB + 1:FB + 2, 0:C]

        block = ctx.enter_context(nc.Block())
        x_r = x.rearrange("b c (f p) w -> b f p c w", p=P)
        out_r = out.rearrange("b (t p) d -> b p t d", p=P)

        def images(eng, body):
            body(0, 0, True, False)
            with eng.Fori(0, (B - 2) // 2) as u:
                body(2 * u + 1, 1, False, False)
                body(2 * u + 2, 0, False, False)
            body(B - 1, 1, False, True)

        def pairs(eng, count, body):
            body(0, 0, False)
            body(1, 1, False)
            with eng.Fori(1, count // 2 - 1) as u:
                body(2 * u, 0, False)
                body(2 * u + 1, 1, False)
            body(count - 2, 0, False)
            body(count - 1, 1, True)

        def in_slot(n, par):
            return 8 * n + 8 * (2 - par)

        @block.sync
        def _(sp):
            sp.dma_start(nat[:, 0:6, :], qkv_w.rearrange("(j p) c -> p j c", p=P)).then_inc(s["nat_in"], 16)
            sp.dma_start(nat[:, 6:8, :], proj_w.rearrange("(j p) c -> p j c", p=P)).then_inc(s["nat_in"], 16)
            sp.dma_start(gate_n[:, :], gate_w).then_inc(s["nat_in"], 16)
            sp.dma_start(rows_qb[:, :], qkv_b.rearrange("(j p) -> j p", p=P)).then_inc(s["nat_in"], 16)
            sp.dma_start(filt[:, :], scharr.rearrange("a b c d -> b (a c d)").to_broadcast([P, 18])).then_inc(s["consts"], 16)
            for dst, src in ((ident, k_ident), (shift, k_shift), (parity, k_parity), (mask_a, k_mask_a), (mask_t, k_mask_t),
                             (aug_l, k_aug_l), (aug_c, k_aug_c)):
                sp.dma_start(dst[:], src).then_inc(s["consts"], 16)

            def load_x(n):
                need(sp, s["gray"], n)
                for f in range(2):
                    sp.dma_start(xin[:, f], x_r[n, f]).then_inc(s["x_in"], 16)

            def load_txt(n):
                need(sp, s["hp"], n)
                need(sp, s["xn1"], n)
                sp.dma_start(h[:, 2, :], txt[n]).then_inc(s["txt_in"], 16)

            load_x(0)
            load_txt(0)
            for dst, src in ((bv, row(qkv_b[2 * C:3 * C])), (pb, row(proj_b)), (sb2b, row(sb2)), (gb, row(gate_b))):
                sp.dma_start(dst[:, :], src.to_broadcast([P, src.shape[1]])).then_inc(s["consts2"], 16)
            for dst, src in ((before, k_before), (tri, k_tri), (ebase, k_ebase), (padbase, k_pad)):
                sp.dma_start(dst[:], src).then_inc(s["consts2"], 16)
            sp.wait_ge(s["pads"], 2)
            for dst, be, bs in ((rows_b1, b1, sb1), (rows_b3, b3, sb3)):
                f = dst[:, :, :].rearrange("e c p -> e (c p)")
                sp.dma_start(f[0:E, 0:HID], be).then_inc(s["rb_in"], 16)
                sp.dma_start(f[E:EA, 0:HID], row(bs)).then_inc(s["rb_in"], 16)

            load_x(1)

            def body(i, par, first, last):
                if not last:
                    load_txt(i + 1)
                    if not (isinstance(i, int) and i + 2 >= B):
                        load_x(i + 2)
                if not first:
                    store(i - 1)

            def store(n):
                need(sp, s["h1"], 2 * n + 2)
                sp.dma_start(h1_d[n], h1[:, :, :]).then_inc(s["h1_out"], 16)
                need(sp, s["x2l"], n + 1)
                sp.dma_start(x2_d[n], x2[:, :, :, :]).then_inc(s["x2_out"], 16)

            body(0, 0, True, False)
            with sp.Fori(0, (B - 4) // 2) as u:
                body(2 * u + 1, 1, False, False)
                body(2 * u + 2, 0, False, False)
            body(B - 3, 1, False, False)
            body(B - 2, 0, False, False)
            body(B - 1, 1, False, True)
            store(B - 1)

            sp.wait_ge(s["total"], 1)
            sp.wait_ge(s["scat"], 96 * B)
            sp.wait_ge(s["x2_out"], 16 * B)
            sp.wait_ge(s["h1_out"], 16 * B)
            sp.dma_start(tilerow[:], k_tile).then_inc(s["tabc"], 16)
            for e in range(E):
                sp.dma_start(b2b[:, e, :], b2[e:e + 1, :].to_broadcast([P, C])).then_inc(s["tabc"], 16)

            sp.wait_ge(s["padsc"], 16 * 2 * E)
            sp.wait_ge(s["tab"], 1)

            def rows(dram, r):
                return dram[bass.ds(r, TW), :].rearrange("(t p) d -> p t d", p=P)

            def load_tile(j, par, used):
                need(sp, s["xT3"], used)
                first = sp.value_load(tile_tab[0:1, 1, bass.ds(j, 1)], min_val=0, max_val=E * REGION - TW)
                sp.dma_start(xg[:, par], rows(xs_d, first)).then_inc(s[f"xg{par}"], 16)

            load_tile(0, 0, 0)
            load_tile(1, 1, 0)

            def body_b(j, par, last):
                if not (isinstance(j, int) and j + 2 >= NT):
                    load_tile(j + 2, par, j + 1)
                sp.wait_ge(s["yo"], 2 * j + 2)
                sp.dma_start(rows(ys_d, j * TW), yo[:, par]).then_inc(s[f"st{par}"], 16)
            pairs(sp, NT, body_b)
            sp.wait_ge(s["st0"], 16 * (NT // 2))
            sp.wait_ge(s["st1"], 16 * (NT // 2))

            def load_c(n, par, used):
                need(sp, s["cyps"], 3 * used)
                sp.dma_start(x2c[:, par], x2_d[n]).then_inc(s[f"cx{par}"], 16)
                need(sp, s["cdone"], used)
                sp.dma_start(h1c[:, par], h1_d[n]).then_inc(s[f"ch{par}"], 16)

            load_c(0, 0, 0)
            load_c(1, 1, 0)

            def body_c(n, par, last):
                sp.wait_ge(s["cdone"], n + 1)
                sp.dma_start(out_r[n], acc[:, par]).then_inc(s[f"co{par}"], 16)
                if not (isinstance(n, int) and n + 2 >= B):
                    load_c(n + 2, par, n + 1)
            pairs(sp, B, body_c)
            sp.wait_ge(s["co0"], 16 * (B // 2))
            sp.wait_ge(s["co1"], 16 * (B // 2))

        @block.tensor
        def _(pe):
            pe.wait_ge(s["nat_in"], 64)
            pe.wait_ge(s["consts"], 16 * N_CONST)
            pe.wait_ge(s["rb_in"], 64)

            def turn(slot, in_, n):
                return nc.tensor.transpose(ps[:, slot // 4, P * (slot % 4):P * (slot % 4) + n], in_, ident[0:n, 0:n])

            for j in range(8):
                for k in range(KC):
                    turn(j * KC + k, nat[:, j, k * P:(k + 1) * P], P)
            for k in range(KC):
                turn(16 + k, gate_n[:, k * P:(k + 1) * P], E)
            turn(18, rows_qb[:, :], 6)
            for c in range(HC):
                turn(20 + c, rows_b1[:, c, :], EA)
                last = turn(24 + c, rows_b3[:, c, :], EA)
            last.then_inc(s["setup_t"], 1)
            pe.wait_ge(s["setup_l"], 2)
            pe.wait_ge(s["bias_done"], 3)
            pe.wait_ge(s["filt_done"], 1)
            pe.wait_ge(s["ident_h"], 1)
            pe.wait_ge(s["consts2"], 16 * N_CONST2)

            def conv(n, f):
                pe.wait_ge(s["gray"], n + 1)
                for q in range(2):
                    o = ps[:, FB + f, q * IMG:(q + 1) * IMG]
                    r = slice(0, 32) if f == 0 else slice(96, 128)
                    for dx in range(3):
                        i = 3 * q + dx
                        nc.tensor.matmul(o, band[:, i, :], gray[:, f, dx:dx + IMG], start=dx == 0, stop=False)
                        last = nc.tensor.matmul(o, corner[r, i, :], gray[r, 1 - f, dx:dx + IMG], start=False, stop=dx == 2)
                last.then_inc(s["conv"], 1)

            def turn_rows(src, sem):
                for t in range(T):
                    for k in range(KC):
                        last = nc.tensor.transpose(ps[:, FB + k, t * P:(t + 1) * P], src[:, t, k * P:(k + 1) * P], ident[:, :])
                last.then_inc(sem, 1)

            def qk(n, c):
                for k in range(KC):
                    w = slice(c * P, (c + 1) * P)
                    last = mm3(ps[:, FB + c % 2, 0:N], qkvT_h[:, k, w], qkvT_l[:, k, w], xT_h[:, k, :], xT_l[:, k, :],
                               k == 0, k == KC - 1)
                last.then_inc(s["qk"], 1)

            def by_rows(lh, ll, rh, rl, sem):
                for t in range(T):
                    for k in range(KC):
                        r = slice(t * P, (t + 1) * P)
                        last = mm3(ps[:, FB + t // 2, (t % 2) * C:(t % 2 + 1) * C], lh[:, k, r], ll[:, k, r],
                                   rh[:, k], rl[:, k], k == 0, k == KC - 1)
                last.then_inc(sem, 1)

            def smax(n, par, q):
                need(pe, s["exp"], 16 * n + 4 * q)
                c, pr = q // 2, q % 2
                cols = [(t, 0 if t == 0 else t * P - WINDOW, (t + 1) * P, 0 if t == 0 else P + (t - 1) * SPAN) for t in range(T)]
                for t, lo, hi, at in cols:
                    for g in range(G):
                        r = slice(32 * g, 32 * g + 32)
                        nc.tensor.matmul(ps[:, g, at:at + hi - lo], q_h[r, par, pr, c, t * P:(t + 1) * P], k_h[r, par, c, lo:hi],
                                         start=t == 0, stop=False, skip_group_check=True)
                for g in range(G):
                    for t, lo, hi, at in cols:
                        last = nc.tensor.matmul(ps[:, g, at:at + hi - lo], ident_h[:, :], mask_a[:, head_of(q, g), SPAN - hi + lo:],
                                                start=False, stop=True, skip_group_check=True)
                last.then_inc(s["smax"], 1)

            def max_turn(n, q):
                pe.wait_ge(s["mx"], 4 * n + q + 1)
                for t in range(T):
                    last = nc.tensor.transpose(ps[:, 0, t * P:(t + 1) * P], mx[:, t, :], ident[:, :])
                last.then_inc(s["mxT"], 1)

            def scores(n, par, q):
                pe.wait_ge(s["aug"], 4 * n + q + 1)
                c, pr = q // 2, q % 2
                for j in range(T):
                    w = min(SPAN, N - j * P)
                    km, qn, at = slice(j * P, (j + 1) * P), slice(j * P, j * P + w), j * SPAN
                    for step in range(4):
                        for g in range(G):
                            r = slice(32 * g, 32 * g + 32)
                            kk, qq = ((k_h[r, par, c, km], q_h[r, par, pr, c, qn]), (k_h[r, par, c, km], q_l[r, par, pr, c, qn]),
                                      (k_l[r, par, c, km], q_h[r, par, pr, c, qn]), (aug_l[r, j, q, :], aug_r[r, qn]))[step]
                            nc.tensor.matmul(ps[:, g, at:at + w], kk, qq, start=j == 0 and step == 0, stop=False,
                                             skip_group_check=True)
                for g in range(G):
                    for j in range(T):
                        w = min(SPAN, N - j * P)
                        last = nc.tensor.matmul(ps[:, g, j * SPAN:j * SPAN + w], ident_h[:, :], mask_t[:, 0:w], start=False, stop=True,
                                                skip_group_check=True)
                    last.then_inc(s["st"], 1)

            def attend(n, par, q):
                need(pe, s["ao"], 4 * n + q - 1)
                for g in range(G):
                    pe.wait_ge(s["exp"], 16 * n + 4 * q + g + 1)
                    hh = head_of(q, g)
                    for t in range(T):
                        o = ps[:, 4 + q % 2, (t * G + g) * (HD + 1):(t * G + g + 1) * (HD + 1)]
                        last = nc.tensor.matmul(o, prob[:, q % 2, g, t * SPAN:t * SPAN + P], v_aug[:, par, t, hh, :],
                                                start=True, stop=True)
                        if t > 0:
                            last = nc.tensor.matmul(o[0:WINDOW], prob[:, q % 2, g, (t - 1) * SPAN + P:t * SPAN],
                                                    v_aug[:, par, t - 1, hh, :], start=False, stop=True, skip_group_check=True)
                last.then_inc(s["av"], 1)

            def gate(n):
                for t in range(T):
                    for k in range(KC):
                        r = slice(t * P, (t + 1) * P)
                        last = mm3(ps[:, FB, t * E:(t + 1) * E], x2[:, 0, k, r], x2[:, 1, k, r], gateT_h[:, k, :], gateT_l[:, k, :],
                                   k == 0, k == KC - 1)
                last.then_inc(s["lg"], 1)

            def position(n):
                pe.wait_ge(s["chosen"], n + 1)
                need(pe, s["pp"], n)
                for t in range(T):
                    o = ps[:, FB + 1, t * E:(t + 1) * E]
                    nc.tensor.matmul(o, tri[:, 0, :], chosen[:, t, :], start=True, stop=False)
                    for t2 in range(t):
                        nc.tensor.matmul(o, tri[:, 1, :], chosen[:, t2, :], start=False, stop=False)
                    last = nc.tensor.matmul(o, tri[:, 1, :], counts[:, :], start=False, stop=True)
                last.then_inc(s["pos"], 1)

            def front_x(n):
                pe.wait_ge(s["xn1"], n + 1)
                turn_rows(xn1, s["xT"])

            conv(0, 0)
            conv(0, 1)
            pe.wait_ge(s["absd"], 2)
            front_x(0)
            pe.wait_ge(s["xTl"], 1)
            for c in range(4):
                if c >= 2:
                    pe.wait_ge(s["q_ev"], c - 1)
                qk(0, c)
            pe.wait_ge(s["k_lo"], 2)
            by_rows(xT_h, xT_l, qkvT_h[:, :, 2 * C:], qkvT_l[:, :, 2 * C:], s["vps"])
            pe.wait_ge(s["q_hi"], 2)
            pe.wait_ge(s["q_lo"], 2)

            def body(i, par, first, last):
                smax(i, par, 0)
                pe.wait_ge(s["vaug"], 2 * i + 2)
                if not first:
                    pe.wait_ge(s["ao"], 4 * i)
                    turn_rows(ao, s["aoT"])
                    pe.wait_ge(s["aol"], i)
                if not last:
                    conv(i + 1, 0)
                max_turn(i, 0)
                scores(i, par, 0)
                if not last:
                    conv(i + 1, 1)
                smax(i, par, 1)
                if not last:
                    pe.wait_ge(s["absd"], 2 * i + 4)
                if not first:
                    by_rows(aoT_h, aoT_l, projT_h, projT_l, s["pj"])
                max_turn(i, 1)
                scores(i, par, 1)
                attend(i, par, 0)
                if not first:
                    pe.wait_ge(s["h1"], 2 * i)
                if not last:
                    front_x(i + 1)
                smax(i, par, 2)
                if not last:
                    pe.wait_ge(s["xTl"], i + 2)
                if not first:
                    pe.wait_ge(s["xn2"], i)
                    turn_rows(xn2, s["xT2"])
                max_turn(i, 2)
                if not first:
                    pe.wait_ge(s["x2l"], i)
                if not last:
                    qk(i + 1, 0)
                scores(i, par, 2)
                attend(i, par, 1)
                if not last:
                    qk(i + 1, 1)
                    pe.wait_ge(s["q_ev"], 2 * i + 3)
                if not first:
                    gate(i - 1)
                smax(i, par, 3)
                if not first:
                    pe.wait_ge(s["lgs"], i)
                if not last:
                    qk(i + 1, 2)
                    pe.wait_ge(s["q_ev"], 2 * i + 4)
                    qk(i + 1, 3)
                max_turn(i, 3)
                scores(i, par, 3)
                if not last:
                    pe.wait_ge(s["k_lo"], 2 * i + 4)
                    by_rows(xT_h, xT_l, qkvT_h[:, :, 2 * C:], qkvT_l[:, :, 2 * C:], s["vps"])
                attend(i, par, 2)
                if not last:
                    pe.wait_ge(s["vaug"], 2 * i + 4)
                if not first:
                    position(i - 1)
                attend(i, par, 3)
                if not first:
                    pe.wait_ge(s["pp"], i)
                if not last:
                    pe.wait_ge(s["q_hi"], 2 * i + 4)
                    pe.wait_ge(s["q_lo"], 2 * i + 4)

            images(pe, body)
            pe.wait_ge(s["ao"], 4 * B)
            turn_rows(ao, s["aoT"])
            pe.wait_ge(s["aol"], B)
            by_rows(aoT_h, aoT_l, projT_h, projT_l, s["pj"])
            pe.wait_ge(s["h1"], 2 * B)
            pe.wait_ge(s["xn2"], B)
            turn_rows(xn2, s["xT2"])
            pe.wait_ge(s["x2l"], B)
            gate(B - 1)
            pe.wait_ge(s["lgs"], B)
            position(B - 1)
            pe.wait_ge(s["pp"], B)
            nc.tensor.matmul(ps[:, 0, 0:E], tri[:, 1, :], counts[:, :], start=True, stop=True).then_inc(s["total"], 1)

            pe.wait_ge(s["tab"], 1)
            pe.wait_ge(s["w_lo"], 4 * EA)

            def turn_tile(n, par, nth):
                pe.wait_ge(s[f"xg{par}"], nth)
                need(pe, s["xel"], n)
                for t in range(2):
                    for k in range(KC):
                        last = nc.tensor.transpose(ps[:, 6, k * TW + t * P:k * TW + (t + 1) * P], xg[:, par, t, k * P:(k + 1) * P], ident[:, :])
                last.then_inc(s["xT3"], 1)

            def up(n, par, c, e, xh, xl, width, names):
                m = rows_of(c)
                need(pe, s[names["prod"]], 3 * n + c - 1)
                o = (par + c) % 2
                for j, (wh, wl) in enumerate(((w3_h, w3_l), (w1_h, w1_l))):
                    for k in range(KC):
                        wv = [a[:, e, k, c * P:c * P + m] if isinstance(e, int) else
                              a[:, bass.ds(e, 1), k, c * P:c * P + m].rearrange("p a n -> p (a n)") for a in (wh, wl)]
                        last = mm3(ps[0:m, 2 * o + j, 0:width], wv[0], wv[1], xh[:, k, :], xl[:, k, :], k == 0, k == KC - 1)
                    last.then_inc(s[names["up"]], 1)

            def down(n, par, t, e, names):
                for c in range(HC):
                    m = rows_of(c)
                    r = slice(t * P, (t + 1) * P)
                    wv = [a[0:m, e, c, :] if isinstance(e, int) else
                          a[0:m, bass.ds(e, 1), c, :].rearrange("p a n -> p (a n)") for a in (w2_h, w2_l)]
                    last = mm3(ps[:, 4 + t, 0:C], hT_h[0:m, par, c, r], hT_l[0:m, par, c, r], wv[0], wv[1], c == 0, c == HC - 1)
                last.then_inc(s[names["yps"]], 1)

            def expert(j):
                return pe.value_load(tile_tab[0:1, 0, bass.ds(j, 1)], min_val=0, max_val=E - 1)

            NB = dict(prod="prod", up="up", yps="yps")
            turn_tile(0, 0, 16)
            pe.wait_ge(s["xel"], 1)
            e0 = expert(0)
            for c in range(HC):
                up(0, 0, c, e0, xe_h[:, 0], xe_l[:, 0], TW, NB)

            def body_b(j, par, last):
                if not last:
                    turn_tile(j + 1, 1 - par, in_slot(j + 1, 1 - par))
                    e1 = expert(j + 1)
                    pe.wait_ge(s["xel"], j + 2)
                    up(j + 1, 1 - par, 0, e1, xe_h[:, 1 - par], xe_l[:, 1 - par], TW, NB)
                e = expert(j)
                for t in range(2):
                    if t == 0:
                        pe.wait_ge(s["hl"], 3 * j + 3)
                    need(pe, s["yo"], 2 * j + t - 1)
                    down(j, par, t, e, NB)
                    if not last:
                        up(j + 1, 1 - par, 1 + t, e1, xe_h[:, 1 - par], xe_l[:, 1 - par], TW, NB)
            pairs(pe, NT, body_b)

            NC = dict(prod="cprod", up="cup", yps="cyps")
            pe.wait_ge(s["yo"], 2 * NT)
            pe.wait_ge(s["prod"], 3 * NT)
            pe.wait_ge(s["cx0"], 16)
            for c in range(HC):
                up(0, 0, c, E, x2c[:, 0, 0], x2c[:, 0, 1], N, NC)

            def body_c(n, par, last):
                if not last:
                    pe.wait_ge(s[f"cx{1 - par}"], in_slot(n + 1, 1 - par))
                for t in range(T):
                    if not last:
                        up(n + 1, 1 - par, t, E, x2c[:, 1 - par, 0], x2c[:, 1 - par, 1], N, NC)
                    if t == 0:
                        pe.wait_ge(s["chl"], 3 * n + 3)
                    need(pe, s["cacc"], 3 * n + t - 2)
                    down(n, par, t, E, NC)
            pairs(pe, B, body_c)

        @block.scalar
        def _(act):
            act.wait_ge(s["consts"], 16 * N_CONST)
            act.wait_ge(s["ones"], 1)
            nc.scalar.copy(ident_h[:, :], ident[:, :]).then_inc(s["ident_h"], 1)
            act.wait_ge(s["setup_t"], 1)
            for j in range(8):
                for k in range(KC):
                    at = j * KC + k
                    dst = qkvT_h[:, k, j * P:(j + 1) * P] if j < 6 else projT_h[:, k, (j - 6) * P:(j - 5) * P]
                    nc.scalar.copy(dst, ps[:, at // 4, P * (at % 4):P * (at % 4 + 1)])
            nc.scalar.copy(gateT_h[:, :, :], ps[:, 4, 0:KC * P].rearrange("p (k n) -> p k n", k=KC)[:, :, 0:E]).then_inc(s["setup_h"], 1)
            nc.scalar.copy(bias1[:, :, :], ps[:, 5, 0:HC * P].rearrange("p (c n) -> p c n", c=HC)[:, :, 0:EA]).then_inc(s["bias_done"], 1)
            nc.scalar.copy(bias3[:, :, :], ps[:, 6, 0:HC * P].rearrange("p (c n) -> p c n", c=HC)[:, :, 0:EA]).then_inc(s["bias_done"], 1)
            nc.scalar.copy(bq4[:, 2:6], ps[:, 4, 2 * P + 2:2 * P + 6])
            nc.scalar.mul(bq4[:, 0:2], ps[:, 4, 2 * P:2 * P + 2], SCALE).then_inc(s["bias_done"], 1)
            act.wait_ge(s["bias_done"], 3)

            def edge_abs(n, f):
                act.wait_ge(s["conv"], 2 * n + f + 1)
                need(act, s["edge"], 2 * n + f)
                nc.scalar.activation(ab[:, :, :], ps[:, FB + f, :].rearrange("p (q w) -> p q w", q=2), ACT.Abs, scale=0.5).then_inc(s["absd"], 1)

            def root(n, k):
                act.wait_ge(s["var1" if k == 0 else "var2"], n + 1)
                nc.scalar.activation(std[:, k, :], mv[:, k, :, 1], ACT.Sqrt, bias=eps[:, :]).then_inc(s["std1" if k == 0 else "std2"], 1)

            def xt_high(n):
                act.wait_ge(s["xT"], n + 1)
                need(act, s["vps"], n)
                nc.scalar.copy(xT_h[:, :, :], ps[:, FB:FB + 2, 0:N]).then_inc(s["xTh"], 1)

            def qk_out(n, par, c):
                act.wait_ge(s["qk"], 4 * n + c + 1)
                if c < 2:
                    need(act, s["q_lo"], 2 * n)
                    nc.scalar.activation(qs[:, c, :], ps[:, FB + c, 0:N], ACT.Identity, scale=SCALE, bias=bq4[:, c:c + 1]).then_inc(s["q_ev"], 1)
                else:
                    nc.scalar.activation(k_h[:, par, c - 2, :], ps[:, FB + c - 2, 0:N], ACT.Identity, bias=bq4[:, c:c + 1]).then_inc(s["k_hi"], 1)

            def qk_high(n, par):
                act.wait_ge(s["q_ev"], 2 * n + 2)
                for pr in range(2):
                    nc.scalar.activation(q_h[:, par, pr], qs[:, :, :], ACT.Copy, scale=parity[:, pr:pr + 1]).then_inc(s["q_hi"], 1)

            def softmax_exp(n, q):
                for g in range(G):
                    act.wait_ge(s["st"], 16 * n + 4 * q + g + 1)
                    if g == 0:
                        need(act, s["av"], 4 * n + q - 1)
                    nc.scalar.activation(prob[:, q % 2, g, :], ps[:, g, :], ACT.Exp).then_inc(s["exp"], 1)

            def ao_high(n):
                act.wait_ge(s["aoT"], n + 1)
                nc.scalar.copy(aoT_h[:, :, :], ps[:, FB:FB + 2, 0:N]).then_inc(s["aoh"], 1)

            def x2_high(n):
                act.wait_ge(s["xT2"], n + 1)
                need(act, s["x2_out"], 16 * n)
                nc.scalar.copy(x2[:, 0], ps[:, FB:FB + 2, 0:N]).then_inc(s["x2h"], 1)

            def gate_exp(n):
                act.wait_ge(s["lgs"], n + 1)
                nc.scalar.activation(rex[:, :, :], lgs[:, :, :], ACT.Exp).then_inc(s["rexp"], 1)

            edge_abs(0, 0)
            edge_abs(0, 1)
            root(0, 0)
            xt_high(0)
            for c in range(4):
                qk_out(0, 0, c)
            qk_high(0, 0)

            def body(i, par, first, last):
                if not first:
                    ao_high(i - 1)
                if not last:
                    edge_abs(i + 1, 0)
                softmax_exp(i, 0)
                if not last:
                    edge_abs(i + 1, 1)
                    root(i + 1, 0)
                if not first:
                    root(i - 1, 1)
                softmax_exp(i, 1)
                if not last:
                    xt_high(i + 1)
                if not first:
                    x2_high(i - 1)
                if not last:
                    qk_out(i + 1, 1 - par, 0)
                softmax_exp(i, 2)
                if not last:
                    qk_out(i + 1, 1 - par, 1)
                if not first:
                    gate_exp(i - 1)
                if not last:
                    qk_out(i + 1, 1 - par, 2)
                    qk_out(i + 1, 1 - par, 3)
                    qk_high(i + 1, 1 - par)
                softmax_exp(i, 3)

            images(act, body)
            ao_high(B - 1)
            root(B - 1, 1)
            x2_high(B - 1)
            gate_exp(B - 1)

            act.wait_ge(s["tab"], 1)

            def up_out(n, par, c, e, width, nm):
                m = rows_of(c)
                o = (par + c) % 2
                act.wait_ge(s[nm + "up"], 6 * n + 2 * c + 1)
                need(act, s[nm + "prod"], 3 * n + c - 1)
                bias = bias3[0:m, c, e:e + 1] if isinstance(e, int) else bias3[0:m, c, bass.ds(e, 1)]
                nc.scalar.activation(u3[0:m, o, 0:width], ps[0:m, 2 * o, 0:width], ACT.Identity, bias=bias).then_inc(s[nm + "u3"], 1)
                act.wait_ge(s[nm + "prod"], 3 * n + c + 1)
                need(act, s[nm + "hl"], 3 * n + c - 1)
                nc.scalar.activation(hs[0:m, o, 0:width], prd[0:m, o, 0:width], ACT.Silu).then_inc(s[nm + "silu"], 1)

            def tile_high(n, par):
                act.wait_ge(s["xT3"], n + 1)
                nc.scalar.copy(xe_h[:, par], ps[:, 6, :].rearrange("p (k n) -> p k n", k=KC)).then_inc(s["xeh"], 1)

            def one_tile(n, par):
                nc.scalar.activation(one_a[:, :], zero[:, :], ACT.Silu)
                tile_high(n, par)
                e = act.value_load(tile_tab[0:1, 0, bass.ds(n, 1)], min_val=0, max_val=E - 1)
                for c in range(HC):
                    up_out(n, par, c, e, TW, "")

            one_tile(0, 0)

            def body_b(j, par, last):
                if not last:
                    one_tile(j + 1, 1 - par)
            pairs(act, NT, body_b)
            act.wait_ge(s["hl"], 3 * NT)
            for c in range(HC):
                up_out(0, 0, c, E, N, "c")

            def body_c(n, par, last):
                nc.scalar.activation(one_a[:, :], zero[:, :], ACT.Silu)
                if not last:
                    for c in range(HC):
                        up_out(n + 1, 1 - par, c, E, N, "c")
            pairs(act, B, body_c)

        @block.vector
        def _(dve):
            nc.vector.memset(rows_b1[:, :, :], 0.0).then_inc(s["pads"], 1)
            nc.vector.memset(rows_b3[:, :, :], 0.0).then_inc(s["pads"], 1)
            nc.vector.memset(gray[:, :, :], 0.0)
            nc.vector.memset(mx[:, :, :], 0.0)
            nc.vector.memset(v_aug[:, :, :, :, HD:HD + 1], 1.0)
            nc.vector.memset(counts[:, :], 0.0)
            nc.vector.memset(zrow[:, :], 0.0)
            nc.vector.memset(zero[:, :], 0.0)
            nc.vector.memset(eps[:, :], EPS).then_inc(s["ones"], 1)
            dve.wait_ge(s["ones"], 1)
            dve.wait_ge(s["consts"], 16 * N_CONST)
            count = [0]

            def link(ins):
                count[0] += 1
                ins.then_inc(s["chain"], 1)
                dve.wait_ge(s["chain"], count[0])

            for q in range(2):
                for dx in range(3):
                    i = 3 * q + dx
                    tap = [filt[:, 9 * q + 3 * dy + dx:9 * q + 3 * dy + dx + 1] for dy in range(3)]
                    link(nc.vector.tensor_scalar(band[:, i, :], shift[:, 0, :], tap[0], None, ALU.mult))
                    link(nc.vector.scalar_tensor_tensor(band[:, i, :], shift[:, 1, :], tap[1], band[:, i, :], ALU.mult, ALU.add))
                    link(nc.vector.scalar_tensor_tensor(band[:, i, :], shift[:, 2, :], tap[2], band[:, i, :], ALU.mult, ALU.add))
                    link(nc.vector.tensor_scalar(corner[:, i, :], shift[:, 3, :], tap[2], None, ALU.mult))
                    link(nc.vector.scalar_tensor_tensor(corner[:, i, :], shift[:, 4, :], tap[0], corner[:, i, :], ALU.mult, ALU.add))
            nc.vector.memset(one_v[:, :], 1.0).then_inc(s["filt_done"], 1)
            dve.wait_ge(s["setup_h"], 1)
            dve.wait_ge(s["bias_done"], 3)
            for j in range(8):
                for k in range(KC):
                    at = j * KC + k
                    w = slice(j * P, (j + 1) * P) if j < 6 else slice((j - 6) * P, (j - 5) * P)
                    lo, hi = (qkvT_l, qkvT_h) if j < 6 else (projT_l, projT_h)
                    ins = nc.vector.tensor_tensor(lo[:, k, w], ps[:, at // 4, P * (at % 4):P * (at % 4 + 1)], hi[:, k, w], ALU.subtract)
            ins.then_inc(s["setup_l"], 1)
            nc.vector.tensor_tensor(gateT_l[:, :, :], ps[:, 4, 0:KC * P].rearrange("p (k n) -> p k n", k=KC)[:, :, 0:E], gateT_h[:, :, :],
                                    ALU.subtract).then_inc(s["setup_l"], 1)
            dve.wait_ge(s["consts2"], 16 * N_CONST2)

            def to_gray(n):
                dve.wait_ge(s["x_in"], 32 * n + 32)
                need(dve, s["conv"], 2 * n)
                g = gray[:, :, 1:IMG + 1]
                nc.vector.tensor_scalar(g, xin[:, :, 0], GRAY_W[0], None, ALU.mult).then_inc(s["gsum"], 1)
                dve.wait_ge(s["gsum"], 2 * n + 1)
                nc.vector.scalar_tensor_tensor(g, xin[:, :, 1], GRAY_W[1], g, ALU.mult, ALU.add).then_inc(s["gsum"], 1)
                dve.wait_ge(s["gsum"], 2 * n + 2)
                nc.vector.scalar_tensor_tensor(g, xin[:, :, 2], GRAY_W[2], g, ALU.mult, ALU.add).then_inc(s["gray"], 1)

            def edge_sum(n, f):
                dve.wait_ge(s["absd"], 2 * n + f + 1)
                if f == 0:
                    need(dve, s["hp"], n)
                nc.vector.tensor_tensor(h[:, f, :], ab[:, 0, :], ab[:, 1, :], ALU.add).then_inc(s["edge"], 1)

            def norm(n, k, src, dst, done):
                tag = str(k + 1)
                need(dve, s["var" + tag], n)
                for t in range(T):
                    ins = nc.vector.bn_stats(stats[:, k, t, :], src[:, t, :])
                ins.then_inc(s["stat" + tag], 1)
                dve.wait_ge(s["stat" + tag], n + 1)
                nc.vector.memset(one_v[:, :], 1.0)
                for t in range(T):
                    ins = nc.vector.bn_aggr(mv[:, k, t, :], stats[:, k, t, :])
                ins.then_inc(s["var" + tag], 1)
                dve.wait_ge(s["std" + tag], n + 1)
                nc.vector.reciprocal(rstd[:, k, :], std[:, k, :]).then_inc(s["rst" + tag], 1)
                dve.wait_ge(s["rst" + tag], n + 1)
                for t in range(T):
                    ins = nc.vector.tensor_scalar(dst[:, t, :], src[:, t, :], mv[:, k, t, 0:1], rstd[:, k, t:t + 1], ALU.subtract, ALU.mult)
                ins.then_inc(done, 1)

            def norm1(n):
                dve.wait_ge(s["edge"], 2 * n + 2)
                dve.wait_ge(s["txt_in"], 16 * n + 16)
                need(dve, s["xT"], n)
                norm(n, 0, h, xn1, s["xn1"])

            def xt_low(n):
                dve.wait_ge(s["xTh"], n + 1)
                nc.vector.tensor_tensor(xT_l[:, :, :], ps[:, FB:FB + 2, 0:N], xT_h[:, :, :], ALU.subtract).then_inc(s["xTl"], 1)

            def v_out(n, par):
                dve.wait_ge(s["vps"], n + 1)
                for k, (t0, t1) in enumerate(((0, 2), (2, T))):
                    nc.vector.tensor_tensor(v_aug[:, par, t0:t1, :, 0:HD], bank_tiles(k).rearrange("p t (h d) -> p t h d", h=HEADS),
                                            bv[:, :].rearrange("p (a h d) -> p a h d", a=1, h=HEADS).to_broadcast([P, t1 - t0, HEADS, HD]),
                                            ALU.add).then_inc(s["vaug"], 1)

            def q_low(n, par):
                dve.wait_ge(s["q_hi"], 2 * n + 2)
                for pr in range(2):
                    nc.vector.scalar_tensor_tensor(q_l[:, par, pr], qs[:, :, :], parity[:, pr:pr + 1], q_h[:, par, pr],
                                                   ALU.mult, ALU.subtract).then_inc(s["q_lo"], 1)

            def k_low(n, par, c):
                dve.wait_ge(s["k_hi"], 2 * n + c + 1)
                nc.vector.scalar_tensor_tensor(k_l[:, par, c, :], ps[:, FB + c, 0:N], bq4[:, 2 + c:3 + c], k_h[:, par, c, :],
                                               ALU.add, ALU.subtract).then_inc(s["k_lo"], 1)

            def row_max(n, q):
                dve.wait_ge(s["smax"], 4 * n + q + 1)
                need(dve, s["mxT"], 4 * n + q)
                for t in range(T):
                    at, w = (0, P) if t == 0 else (P + (t - 1) * SPAN, SPAN)
                    ins = nc.vector.tensor_reduce(mx[:, t, :].rearrange("p (g r) -> p g r", g=G)[:, :, 0], ps[:, 0:G, at:at + w], AX, ALU.max)
                ins.then_inc(s["mx"], 1)

            def augment(n, q):
                dve.wait_ge(s["mxT"], 4 * n + q + 1)
                need(dve, s["st"], 16 * n + 4 * q)
                nc.vector.tensor_tensor(aug_r[:, :], aug_c[:, :], ps[:, 0, 0:N], ALU.subtract).then_inc(s["aug"], 1)

            def normalise(n, q):
                dve.wait_ge(s["av"], 4 * n + q + 1)
                need(dve, s["aoT"], n)
                need(dve, s["ao"], 4 * n + q)
                o = ps[:, 4 + q % 2, 0:T * G * (HD + 1)].rearrange("p (t g d) -> p t g d", t=T, g=G)
                nc.vector.reciprocal(rs[:, :, :], o[:, :, :, HD]).then_inc(s["rs"], 1)
                dve.wait_ge(s["rs"], 4 * n + q + 1)
                dst = ao[:, :, :].rearrange("p t (c g r d) -> p c r t g d", c=2, g=G, r=2)[:, q // 2, q % 2]
                nc.vector.tensor_tensor(dst, o[:, :, :, 0:HD],
                                        rs[:, :, :].rearrange("p t (g a) -> p t g a", a=1).to_broadcast([P, T, G, HD]),
                                        ALU.mult).then_inc(s["ao"], 1)

            def ao_low(n):
                dve.wait_ge(s["aoh"], n + 1)
                nc.vector.tensor_tensor(aoT_l[:, :, :], ps[:, FB:FB + 2, 0:N], aoT_h[:, :, :], ALU.subtract).then_inc(s["aol"], 1)

            def residual(n, par):
                dve.wait_ge(s["pj"], n + 1)
                dve.wait_ge(s["hp"], n + 1)
                need(dve, s["h1_out"], 16 * n)
                for k, (t0, t1) in enumerate(((0, 2), (2, T))):
                    nc.vector.tensor_tensor(h1[:, t0:t1, :], bank_tiles(k), hp[:, par, t0:t1, :], ALU.add).then_inc(s["h1"], 1)

            def norm2(n):
                dve.wait_ge(s["h1"], 2 * n + 2)
                need(dve, s["scat"], 96 * n)
                norm(n, 1, h1, xn2, s["xn2"])

            def x2_low(n):
                dve.wait_ge(s["x2h"], n + 1)
                nc.vector.tensor_tensor(x2[:, 1], ps[:, FB:FB + 2, 0:N], x2[:, 0], ALU.subtract).then_inc(s["x2l"], 1)

            RT = 12

            def per_tile(v, k):
                return v.rearrange("p (t a) -> p t a", a=1).to_broadcast([P, T, k])

            def route(n):
                k = [0]

                def then(ins):
                    k[0] += 1
                    ins.then_inc(s["rt"], 1)
                    dve.wait_ge(s["rt"], RT * n + k[0])

                dve.wait_ge(s["lg"], n + 1)
                lg = ps[:, FB, 0:T * E].rearrange("p (t e) -> p t e", t=T)
                then(nc.vector.tensor_reduce(rmax[:, :], lg, AX, ALU.max))
                nc.vector.tensor_tensor(lgs[:, :, :], lg, per_tile(rmax[:, :], E), ALU.subtract).then_inc(s["lgs"], 1)
                dve.wait_ge(s["rexp"], n + 1)
                then(nc.vector.tensor_reduce(rsum[:, :], rex[:, :, :], AX, ALU.add))
                then(nc.vector.reciprocal(rinv[:, :], rsum[:, :]))
                then(nc.vector.tensor_tensor(score[:, :, :], rex[:, :, :], per_tile(rinv[:, :], E), ALU.mult))
                then(nc.vector.tensor_tensor(biased[:, :, :], score[:, :, :], gb[:, :].rearrange("p (a e) -> p a e", a=1).to_broadcast([P, T, E]), ALU.add))
                for t in range(T):
                    bi = biased[:, t, :]
                    other = bi.rearrange("p (a e) -> p a e", a=1).to_broadcast([P, E, E])
                    own = bi.rearrange("p (e a) -> p e a", a=1).to_broadcast([P, E, E])
                    nc.vector.tensor_tensor(cmp1[:, t], other, own, ALU.is_gt)
                    ins = nc.vector.tensor_tensor(cmp2[:, t], other, own, ALU.is_equal)
                then(ins)
                then(nc.vector.tensor_tensor(cmp2[:, :, :, :], cmp2[:, :, :, :],
                                             before[:, :, :].rearrange("p (a e) f -> p a e f", a=1).to_broadcast([P, T, E, E]), ALU.mult))
                then(nc.vector.tensor_tensor(cmp1[:, :, :, :], cmp1[:, :, :, :], cmp2[:, :, :, :], ALU.add))
                then(nc.vector.tensor_reduce(rank[:, :, :], cmp1[:, :, :, :], AX, ALU.add))
                nc.vector.tensor_scalar(chosen[:, :, :], rank[:, :, :], 1.5, None, ALU.is_lt).then_inc(s["chosen"], 1)
                nc.vector.tensor_scalar(pick[:, :, 0, :], rank[:, :, :], 0.0, None, ALU.is_equal)
                then(nc.vector.tensor_scalar(pick[:, :, 1, :], rank[:, :, :], 1.0, None, ALU.is_equal))
                nc.vector.tensor_tensor(pickw[:, :, 0, :], pick[:, :, 0, :], score[:, :, :], ALU.mult)
                then(nc.vector.tensor_tensor(pickw[:, :, 1, :], pick[:, :, 1, :], score[:, :, :], ALU.mult))
                then(nc.vector.tensor_reduce(wts[:, bass.ds(n * T, T), :] if not isinstance(n, int) else wts[:, n * T:(n + 1) * T, :],
                                             pickw[:, :, :, :], AX, ALU.add))
                assert k[0] == RT

            PP = 4

            def places(n):
                k = [0]

                def then(ins):
                    k[0] += 1
                    ins.then_inc(s["idx"], 1)
                    dve.wait_ge(s["idx"], (PP + 1) * n + k[0])

                dve.wait_ge(s["pos"], n + 1)
                then(nc.vector.tensor_tensor(slot[:, :, :], ps[:, FB + 1, 0:T * E].rearrange("p (t e) -> p t e", t=T),
                                             ebase[:, :].rearrange("p (a e) -> p a e", a=1).to_broadcast([P, T, E]), ALU.add))
                nc.vector.tensor_tensor(pickw[:, :, 0, :], pick[:, :, 0, :], slot[:, :, :], ALU.mult)
                nc.vector.tensor_tensor(pickw[:, :, 1, :], pick[:, :, 1, :], slot[:, :, :], ALU.mult)
                then(nc.vector.tensor_reduce(chosen_n[:, :], chosen[:, :, :].rearrange("p t e -> p e t"), AX, ALU.add))
                nc.vector.tensor_tensor(counts[:, :], counts[:, :], chosen_n[:, :], ALU.add).then_inc(s["pp"], 1)
                then(nc.vector.tensor_reduce(slot_f[:, :, :], pickw[:, :, :, :], AX, ALU.add))
                need(dve, s["scat"], 96 * n)
                then(nc.vector.tensor_copy(place[:, bass.ds(n * T, T), :] if not isinstance(n, int) else place[:, n * T:(n + 1) * T, :],
                                           slot_f[:, :, :]))
                nc.vector.tensor_copy(idx[:, :, :], slot_f[:, :, :]).then_inc(s["idx"], 1)
                assert k[0] == PP

            to_gray(0)
            edge_sum(0, 0)
            edge_sum(0, 1)
            norm1(0)
            to_gray(1)
            xt_low(0)
            k_low(0, 0, 0)
            k_low(0, 0, 1)
            v_out(0, 0)
            q_low(0, 0)

            def body(i, par, first, last):
                row_max(i, 0)
                if not first:
                    ao_low(i - 1)
                augment(i, 0)
                if not last:
                    edge_sum(i + 1, 0)
                    edge_sum(i + 1, 1)
                    if not (isinstance(i, int) and i + 2 >= B):
                        to_gray(i + 2)
                    norm1(i + 1)
                row_max(i, 1)
                if not first:
                    residual(i - 1, 1 - par)
                augment(i, 1)
                if not first:
                    norm2(i - 1)
                normalise(i, 0)
                if not last:
                    xt_low(i + 1)
                row_max(i, 2)
                if not first:
                    x2_low(i - 1)
                augment(i, 2)
                normalise(i, 1)
                if not first:
                    route(i - 1)
                row_max(i, 3)
                augment(i, 3)
                if not last:
                    k_low(i + 1, 1 - par, 0)
                    k_low(i + 1, 1 - par, 1)
                    v_out(i + 1, 1 - par)
                    q_low(i + 1, 1 - par)
                normalise(i, 2)
                if not first:
                    places(i - 1)
                normalise(i, 3)

            body(0, 0, True, False)
            with dve.Fori(0, (B - 4) // 2) as u:
                body(2 * u + 1, 1, False, False)
                body(2 * u + 2, 0, False, False)
            body(B - 3, 1, False, False)
            body(B - 2, 0, False, False)
            body(B - 1, 1, False, True)
            ao_low(B - 1)
            residual(B - 1, 1)
            norm2(B - 1)
            x2_low(B - 1)
            route(B - 1)
            places(B - 1)

            dve.wait_ge(s["total"], 1)
            tot = ps[:, 0, 0:E]
            for z in range(2):
                nc.vector.tensor_tensor(padidx[:, z, :], tot, padbase[:, z, :], ALU.add).then_inc(s["padidx"], 1)
            shift_by = TW.bit_length() - 1
            link(nc.vector.tensor_scalar(tile_i[:, :], tot, float(TW - 1), None, ALU.add))
            link(nc.vector.tensor_scalar(tile_i[:, :], tile_i[:, :], shift_by, None, ALU.arith_shift_right))
            link(nc.vector.tensor_copy(tile_f[:, :], tile_i[:, :]))
            link(nc.vector.tensor_copy(tile_cum[:, :], tile_f[0:1, :]))
            for e in range(1, E):
                link(nc.vector.tensor_tensor(tile_cum[:, e:e + 1], tile_cum[:, e - 1:e], tile_f[0:1, e:e + 1], ALU.add))
            wide = [1, NT, E]
            dve.wait_ge(s["tabc"], 16 * (1 + E))
            link(nc.vector.tensor_tensor(tile_cmp[:, :, :], tilerow[:, :, :],
                                         tile_cum[:, :].rearrange("p (a e) -> p a e", a=1).to_broadcast(wide), ALU.is_ge))
            link(nc.vector.tensor_tensor(tile_mul[:, :, :], tile_cmp[:, :, :],
                                         tile_f[0:1, :].rearrange("p (a e) -> p a e", a=1).to_broadcast(wide), ALU.mult))
            link(nc.vector.tensor_reduce(tile_red[:, 0, :], tile_cmp[:, :, :], AX, ALU.add))
            link(nc.vector.tensor_reduce(tile_red[:, 1, :], tile_mul[:, :, :], AX, ALU.add))
            link(nc.vector.tensor_scalar(tile_red[:, 2, :], tile_red[:, 0, :], float(E), None, ALU.is_lt))
            link(nc.vector.tensor_tensor(tile_red[:, 0, :], tile_red[:, 0, :], tile_red[:, 2, :], ALU.mult))
            link(nc.vector.tensor_tensor(tile_red[:, 1, :], tilerow[:, :, 0], tile_red[:, 1, :], ALU.subtract))
            link(nc.vector.tensor_scalar(tile_red[:, 1, :], tile_red[:, 1, :], float(TW), None, ALU.mult))
            link(nc.vector.tensor_tensor(tile_red[:, 1, :], tile_red[:, 1, :], tile_red[:, 2, :], ALU.mult))
            link(nc.vector.tensor_scalar(tile_red[:, 3, :], tile_red[:, 0, :], float(REGION), None, ALU.mult))
            link(nc.vector.tensor_tensor(tile_red[:, 3, :], tile_red[:, 3, :], tile_red[:, 1, :], ALU.add))
            link(nc.vector.tensor_copy(tile_tab[:, 0, :], tile_red[:, 0, :]))
            nc.vector.tensor_copy(tile_tab[:, 1, :], tile_red[:, 3, :]).then_inc(s["tab"], 1)
            dve.wait_ge(s["tab"], 1)
            link(nc.vector.tensor_scalar(back[:, :], tile_f[:, :], float(TW), float(-REGION), ALU.mult, ALU.add))
            for e in range(1, E):
                nc.vector.tensor_scalar(moved[:, e - 1], place[:, :, :], float(e * REGION), back[:, e - 1:e], ALU.is_ge, ALU.mult)
            link(nc.vector.tensor_copy(moved[:, E - 1], place[:, :, :]))
            link(nc.vector.tensor_reduce(place[:, :, :], moved[:, :, :, :].rearrange("p e n k -> p n k e"), AX, ALU.add))
            link(nc.vector.tensor_copy(dest[:, :, :], place[:, :, :]))

            def times(n, par, c, e, width, nm):
                m = rows_of(c)
                o = (par + c) % 2
                dve.wait_ge(s[nm + "up"], 6 * n + 2 * c + 2)
                dve.wait_ge(s[nm + "u3"], 3 * n + c + 1)
                need(dve, s[nm + "silu"], 3 * n + c - 1)
                bias = bias1[0:m, c, e:e + 1] if isinstance(e, int) else bias1[0:m, c, bass.ds(e, 1)]
                nc.vector.scalar_tensor_tensor(prd[0:m, o, 0:width], ps[0:m, 2 * o + 1, 0:width], bias, u3[0:m, o, 0:width],
                                               ALU.add, ALU.mult).then_inc(s[nm + "prod"], 1)

            def hidden_low(n, par, c, width, nm):
                m = rows_of(c)
                o = (par + c) % 2
                dve.wait_ge(s[nm + "hh"], 3 * n + c + 1)
                nc.vector.tensor_tensor(hT_l[0:m, par, c, 0:width], hs[0:m, o, 0:width], hT_h[0:m, par, c, 0:width],
                                        ALU.subtract).then_inc(s[nm + "hl"], 1)

            def tile_low(n, par):
                dve.wait_ge(s["xeh"], n + 1)
                nc.vector.tensor_tensor(xe_l[:, par], ps[:, 6, :].rearrange("p (k n) -> p k n", k=KC), xe_h[:, par],
                                        ALU.subtract).then_inc(s["xel"], 1)

            def tile_out(n, par, t, e):
                dve.wait_ge(s["yps"], 2 * n + t + 1)
                if t == 0 and not (isinstance(n, int) and n < 2):
                    dve.wait_ge(s[f"st{par}"], in_slot(n - 2, par))
                nc.vector.tensor_tensor(yo[:, par, t, :], ps[:, 4 + t, 0:C], b2b[:, bass.ds(e, 1), :].rearrange("p a n -> p (a n)"),
                                        ALU.add).then_inc(s["yo"], 1)

            def expert(j):
                return dve.value_load(tile_tab[0:1, 0, bass.ds(j, 1)], min_val=0, max_val=E - 1)

            tile_low(0, 0)
            e0 = expert(0)
            for c in range(HC):
                times(0, 0, c, e0, TW, "")
                hidden_low(0, 0, c, TW, "")

            def body_b(j, par, last):
                e = expert(j)
                if not last:
                    tile_low(j + 1, 1 - par)
                    e1 = expert(j + 1)
                    times(j + 1, 1 - par, 0, e1, TW, "")
                for t in range(2):
                    tile_out(j, par, t, e)
                    if not last:
                        hidden_low(j + 1, 1 - par, t, TW, "")
                        times(j + 1, 1 - par, t + 1, e1, TW, "")
                if not last:
                    hidden_low(j + 1, 1 - par, 2, TW, "")
            pairs(dve, NT, body_b)

            def fetch_idx(n, par):
                if not (isinstance(n, int) and n < 2):
                    dve.wait_ge(s[f"g{par}"], 6 * in_slot(n - 2, par))
                nc.vector.tensor_copy(idxc[:, par], dest[:, bass.ds(n * T, T), :] if not isinstance(n, int) else
                                      dest[:, n * T:(n + 1) * T, :]).then_inc(s["idxc"], 1)
            fetch_idx(0, 0)
            fetch_idx(1, 1)
            dve.wait_ge(s["silu"], 3 * NT)
            for c in range(HC):
                times(0, 0, c, E, N, "c")
                hidden_low(0, 0, c, N, "c")

            def body_c(n, par, last):
                for t in range(T):
                    if not last:
                        times(n + 1, 1 - par, t, E, N, "c")
                    dve.wait_ge(s["cyps"], 3 * n + t + 1)
                    if t == 0:
                        dve.wait_ge(s["h1s"], n + 1)
                        if not (isinstance(n, int) and n < 2):
                            dve.wait_ge(s[f"co{par}"], in_slot(n - 2, par))
                    nc.vector.tensor_tensor(acc[:, par, t, :], ps[:, 4 + t, 0:C], h1c[:, par, t, :], ALU.add).then_inc(s["cacc"], 1)
                    if not last:
                        hidden_low(n + 1, 1 - par, t, N, "c")
                dve.wait_ge(s[f"g{par}"], 6 * in_slot(n, par))
                dve.wait_ge(s["cacc"], 3 * n + 3)
                for k in range(2):
                    for t in range(T):
                        w = wts[:, bass.ds(n * T + t, 1), k] if not isinstance(n, int) else wts[:, n * T + t:n * T + t + 1, k]
                        ins = nc.vector.scalar_tensor_tensor(acc[:, par, t, :], yg[:, par, t, k, :], w, acc[:, par, t, :], ALU.mult, ALU.add)
                    if k == 0:
                        ins.then_inc(s["cfirst"], 1)
                        dve.wait_ge(s["cfirst"], n + 1)
                ins.then_inc(s["cdone"], 1)
                if not (isinstance(n, int) and n + 2 >= B):
                    fetch_idx(n + 2, par)
            pairs(dve, B, body_c)

        @block.gpsimd
        def _(pool):
            gates = []

            def gate():
                gates.append(len(gates))
                nc.gpsimd.tensor_tensor(one_p[:, gates[-1]:gates[-1] + 1], zero[:, :], zero[:, :], ALU.add)

            pool.wait_ge(s["ones"], 1)
            pool.wait_ge(s["consts2"], 16 * N_CONST2)

            def plus_bias(n, par):
                pool.wait_ge(s["edge"], 2 * n + 2)
                pool.wait_ge(s["txt_in"], 16 * n + 16)
                need(pool, s["h1"], 2 * n - 2)
                nc.gpsimd.tensor_tensor(hp[:, par], h[:, :, :], pb[:, :].rearrange("p (a c) -> p a c", a=1).to_broadcast([P, T, C]),
                                        ALU.add).then_inc(s["hp"], 1)

            def scatter(n):
                pool.wait_ge(s["idx"], (PP_ + 1) * (n + 1))
                gate()
                for t in range(T):
                    for k in range(2):
                        nc.gpsimd.indirect_dma_start(out=xs_d, out_offset=bass.IndirectOffsetOnAxis(ap=idx[:, t, k:k + 1], axis=0),
                                                     in_=xn2[:, t, :], in_offset=None).then_inc(s["scat"], 16)

            def weights_in(e, nth):
                if not (isinstance(nth, int) and nth == 0):
                    pool.wait_ge(s["w_lo"], 4 * nth)
                    gate()
                a1, a3, a2 = (sw1, sw3, sw2) if isinstance(e, int) and e == E else (w1[e], w3[e], w2[e])
                d = stage
                for dst, src in ((d[:, 0:NW].rearrange("p (k n) -> p k n", k=KC), a1.rearrange("(k p) n -> p k n", p=P)),
                                 (d[:, NW:2 * NW].rearrange("p (k n) -> p k n", k=KC), a3.rearrange("(k p) n -> p k n", p=P)),
                                 (d[:, 2 * NW:2 * NW + 2 * C].rearrange("p (k n) -> p k n", k=2), a2[0:2 * P].rearrange("(k p) n -> p k n", p=P)),
                                 (d[0:HLAST, 2 * NW + 2 * C:2 * NW + 3 * C], a2[2 * P:])):
                    pool.dma_start(dst, src).then_inc(s["w_in"], 16)

            def weights_split(e, nth):
                at = slice(e, e + 1) if isinstance(e, int) else bass.ds(e, 1)
                d = stage
                pool.wait_ge(s["w_in"], 64 * (nth + 1))
                gate()
                parts = []
                for k in range(KC):
                    parts.append((w1_h[:, at, k, :], w1_l[:, at, k, :], d[:, k * HID:(k + 1) * HID]))
                    parts.append((w3_h[:, at, k, :], w3_l[:, at, k, :], d[:, NW + k * HID:NW + (k + 1) * HID]))
                for c in range(HC):
                    m = rows_of(c)
                    parts.append((w2_h[0:m, at, c, :], w2_l[0:m, at, c, :], d[0:m, 2 * NW + c * C:2 * NW + (c + 1) * C]))
                for hi, lo, src in parts:
                    nc.gpsimd.tensor_copy(hi.rearrange("p a n -> p (a n)"), src).then_inc(s["w_hi"], 1)
                pool.wait_ge(s["w_hi"], len(parts) * (nth + 1))
                gate()
                for hi, lo, src in parts:
                    ins = nc.gpsimd.tensor_tensor(lo.rearrange("p a n -> p (a n)"), src, hi.rearrange("p a n -> p (a n)"), ALU.subtract)
                ins.then_inc(s["w_lo"], 4)

            PP_ = 4

            def body(i, par, first, last, e):
                if e is not None:
                    weights_in(e, i)
                if not last:
                    plus_bias(i + 1, 1 - par)
                if not first:
                    scatter(i - 1)
                if e is not None:
                    weights_split(e, i)

            plus_bias(0, 0)
            pool.wait_ge(s["setup_t"], 1)
            body(0, 0, True, False, E)
            with pool.Fori(0, E // 2) as u:
                body(2 * u + 1, 1, False, False, 2 * u)
                body(2 * u + 2, 0, False, False, 2 * u + 1)
            with pool.Fori(E // 2, (B - 2) // 2) as u:
                body(2 * u + 1, 1, False, False, None)
                body(2 * u + 2, 0, False, False, None)
            body(B - 1, 1, False, True, None)
            scatter(B - 1)
            pool.wait_ge(s["padidx"], 2)
            gate()
            for z in range(2):
                for e in range(E):
                    nc.gpsimd.indirect_dma_start(out=xs_d, out_offset=bass.IndirectOffsetOnAxis(ap=padidx[:, z, e:e + 1], axis=0),
                                                 in_=zrow[:, :], in_offset=None).then_inc(s["padsc"], 16)

            pool.wait_ge(s["tab"], 1)

            def hidden_high(n, par, c, width, nm):
                m = rows_of(c)
                o = (par + c) % 2
                pool.wait_ge(s[nm + "silu"], 3 * n + c + 1)
                nc.gpsimd.tensor_tensor(hT_h[0:m, par, c, 0:width], hs[0:m, o, 0:width], zero[0:m, :].to_broadcast([m, width]),
                                        ALU.add).then_inc(s[nm + "hh"], 1)
            for c in range(HC):
                hidden_high(0, 0, c, TW, "")

            def body_b(j, par, last):
                if not last:
                    for c in range(HC):
                        hidden_high(j + 1, 1 - par, c, TW, "")
            pairs(pool, NT, body_b)
            pool.wait_ge(s["st0"], 16 * (NT // 2))
            pool.wait_ge(s["st1"], 16 * (NT // 2))

            def shared_bias(n, par):
                pool.wait_ge(s[f"ch{par}"], in_slot(n, par))
                nc.gpsimd.tensor_tensor(h1c[:, par], h1c[:, par], sb2b[:, :].rearrange("p (a c) -> p a c", a=1).to_broadcast([P, T, C]),
                                        ALU.add).then_inc(s["h1s"], 1)

            def gather(n, par):
                pool.wait_ge(s["idxc"], n + 1)
                need(pool, s["cdone"], n - 1)
                gate()
                for t in range(T):
                    for k in range(2):
                        nc.gpsimd.indirect_dma_start(out=yg[:, par, t, k, :], out_offset=None, in_=ys_d,
                                                     in_offset=bass.IndirectOffsetOnAxis(ap=idxc[:, par, t, k:k + 1], axis=0)
                                                     ).then_inc(s[f"g{par}"], 16)
            gather(0, 0)
            shared_bias(0, 0)
            for c in range(HC):
                hidden_high(0, 0, c, N, "c")

            def body_c(n, par, last):
                if not last:
                    gather(n + 1, 1 - par)
                    shared_bias(n + 1, 1 - par)
                    for c in range(HC):
                        hidden_high(n + 1, 1 - par, c, N, "c")
            pairs(pool, B, body_c)


_INS = ['x', 'txt', 'L0_tok_scharr', 'L0_attn_qkv_w', 'L0_attn_qkv_b', 'L0_attn_proj_w', 'L0_attn_proj_b',
        'L0_ffn_gate_w', 'L0_ffn_gate_b', 'L0_ffn_w1', 'L0_ffn_b1', 'L0_ffn_w3', 'L0_ffn_b3', 'L0_ffn_w2', 'L0_ffn_b2',
        'L0_ffn_sw1', 'L0_ffn_sb1', 'L0_ffn_sw3', 'L0_ffn_sb3', 'L0_ffn_sw2', 'L0_ffn_sb2']


def shape_constants(B, T, E):
    import numpy as np
    heads, window, p = HEADS, WINDOW, P
    i = np.arange(p)
    eye = np.eye(p, dtype=np.float32)
    shift = np.zeros((p, 5, p), np.float32)
    for dy in range(3):
        shift[:, dy, :] = (i[:, None] == i[None, :] + dy - 1)
    shift[0, 3, p - 1] = 1
    shift[p - 1, 4, 0] = 1
    base = 2.0 ** (-2.0 ** (-(np.log2(heads) - 3)))
    slopes = (np.float64(base) ** np.arange(1, heads + 1, dtype=np.float32)).astype(np.float32).astype(np.float64)
    off = -30000.0
    n, m = i[:, None], np.arange(-window, p)[None, :]
    ok = (m <= n) & (n - m < window)
    mask_a = np.where(ok[:, None, :], slopes[None, :, None] * (m - n)[:, None, :], off).astype(np.float16)
    m, n = i[:, None], np.arange(p + window)[None, :]
    mask_t = np.where((m <= n) & (n - m < window), 0.0, off).astype(np.float16)

    def parts(v):
        out = []
        for _ in range(3):
            a = v.astype(np.float16)
            out.append(a)
            v = v - a.astype(np.float64)
        return out

    aug_l = np.zeros((p, T, QUADS, p), np.float16)
    aug_c = np.zeros((p, T * p), np.float16)
    for g in range(G):
        r = 32 * g
        aug_c[r + 1:r + 4] = 1
        aug_c[r + 4:r + 7] = np.arange(T * p)
        for q in range(QUADS):
            sl = slopes[head_of(q, g)]
            aug_l[r, :, q, :] = 1
            for t in range(T):
                for j, a in enumerate(parts(sl * (t * p + i))):
                    aug_l[r + 1 + j, t, q] = a
                for j, a in enumerate(parts(-sl * np.ones(1))):
                    aug_l[r + 4 + j, t, q] = a
    par = ((i[:, None] // HD) % 2 == np.arange(2)[None, :]).astype(np.float32)
    before = np.broadcast_to((np.arange(E)[None, :] < np.arange(E)[:, None]).astype(np.float32), (p, E, E)).copy()
    tri = np.ones((p, 2, p), np.float16)
    tri[:, 0, :] = i[:, None] < i[None, :]
    region = B * T * p + TW
    ebase = np.broadcast_to(np.arange(E, dtype=np.float32) * region, (p, E)).copy()
    pad = (ebase[:, None, :] + i[:, None, None] + p * np.arange(2)[None, :, None]).astype(np.float32)
    nt = tile_count(B * T * p, E)
    tile = np.broadcast_to(np.arange(nt, dtype=np.float32)[None, :, None], (1, nt, E)).copy()
    return [("ident", eye), ("shift", shift), ("mask_a", mask_a), ("mask_t", mask_t), ("aug_l", aug_l),
            ("aug_c", aug_c), ("parity", par), ("before", before), ("tri", tri), ("ebase", ebase), ("pad", pad), ("tile", tile)]


def kernel(**inputs):
    import numpy as _np
    import concourse.bacc as _bacc
    from concourse import mybir as _mybir
    from concourse.bass_utils import run_bass_kernel_spmd as _run

    nc = _bacc.Bacc("TRN2", target_bir_lowering=False, num_devices=1)
    arrays, args = {}, []
    items = [(n, _np.ascontiguousarray(inputs[n])) for n in _INS]
    B, rows = inputs['x'].shape[0], inputs['x'].shape[2] + inputs['txt'].shape[1]
    items += shape_constants(B, rows // P, inputs['L0_ffn_w1'].shape[0])
    for name, a in items:
        arrays[f"in_{name}_dram"] = a
        args.append(nc.dram_tensor(f"in_{name}_dram", a.shape, _mybir.dt.from_np(a.dtype), kind="ExternalInput").ap())
    args.append(nc.dram_tensor("out_dram", (B, rows, C), _mybir.dt.float32, kind="ExternalOutput").ap())
    program(nc, *args)
    r = _run(nc, [arrays], core_ids=[0])
    return r.results[0]["out_dram"]
```

```python
from contextlib import ExitStack

import concourse.bass as bass
from concourse import mybir

F32 = mybir.dt.float32
F16 = mybir.dt.float16
U32 = mybir.dt.uint32
I32 = mybir.dt.int32
ALU = mybir.AluOpType
ACT = mybir.ActivationFunctionType
AX = mybir.AxisListType.X

P = 128
IMG = 256
C = 256
KC = C // P
HEADS, HD = 16, 16
QUADS, G = 4, 4
WINDOW = 64
SCALE = HD ** -0.5
SPAN = P + WINDOW
EPS = 1e-5
HID = 352
HC = 3
HLAST = HID - 2 * P
TW = 2 * P
TILES_PER = 4
GRAY_W = (0.2989, 0.587, 0.114)
FB = 6


def tile_count(tokens, experts):
    n = (2 * tokens + experts * (TW - 1)) // TW
    return -(-n // TILES_PER) * TILES_PER


def head_of(q, g):
    return 8 * (q // 2) + 2 * g + q % 2


def need(eng, sem, value):
    if not (isinstance(value, int) and value <= 0):
        eng.wait_ge(sem, value)


def program(nc, x, txt, scharr, qkv_w, qkv_b, proj_w, proj_b, gate_w, gate_b, w1, b1, w3, b3, w2, b2,
            sw1, sb1, sw3, sb3, sw2, sb2, k_ident, k_shift, k_seam_sel, k_seam_part, k_mask_a, k_mask_t, k_aug_l, k_aug_c,
            k_parity, k_before, k_tri, k_ebase, k_tile, out):
    B = x.shape[0]
    E = w1.shape[0]
    EA = E + 1
    T = (IMG + txt.shape[1]) // P
    N = T * P
    REGION = B * N + TW
    NT = tile_count(B * N, E)
    NW = KC * HID
    xs_d = nc.dram_tensor("xs_scratch", (E * REGION, C), F32, kind="Internal").ap()
    ys_d = nc.dram_tensor("ys_scratch", (NT * TW, C), F32, kind="Internal").ap()
    h1_d = nc.dram_tensor("h1_scratch", (B, P, T, C), F32, kind="Internal").ap()
    x2_d = nc.dram_tensor("x2_scratch", (B, P, 2, KC, N), F16, kind="Internal").ap()

    with ExitStack() as ctx:
        def sb(name, shape, dt=F32):
            return ctx.enter_context(nc.sbuf_tensor(name, shape, dt))

        ps = ctx.enter_context(nc.psum_tensor("ps", [P, 8, 512], F32))

        before = sb("before", [P, E, E])
        tri = sb("tri", [P, 2, P], F16)
        ident = sb("ident", [P, P])
        ebase = sb("ebase", [P, E])
        sb2b = sb("sb2b", [P, C])
        bias1 = sb("bias1", [P, HC, EA])
        bias3 = sb("bias3", [P, HC, EA])
        one_v = sb("one_v", [P, 1])
        one_p = sb("one_p", [P, 64])
        one_a = sb("one_a", [P, 1])
        zero = sb("zero", [P, 1])
        eps = sb("eps", [P, 1])
        place = sb("place", [P, B * T, 2])
        dest = sb("dest", [P, B * T, 2], U32)
        wts = sb("wts", [P, B * T, 2])
        counts = sb("counts", [P, E], F16)
        tile_no = sb("tile_no", [1, NT])
        pad_row = sb("pad_row", [1, E], I32)
        zrow = sb("zrow", [P, C])
        tile_i = sb("tile_i", [P, E], I32)
        tile_f = sb("tile_f", [P, E])
        back = sb("back", [P, E])
        tile_cum = sb("tile_cum", [1, E])
        tile_red = sb("tile_red", [1, 4, NT])
        tile_tab = sb("tile_tab", [1, 2, NT], I32)
        w1_h = sb("w1_h", [P, EA, KC, HID], F16)
        w1_l = sb("w1_l", [P, EA, KC, HID], F16)
        w3_h = sb("w3_h", [P, EA, KC, HID], F16)
        w3_l = sb("w3_l", [P, EA, KC, HID], F16)
        w2_h = sb("w2_h", [P, EA, HC, C], F16)
        w2_l = sb("w2_l", [P, EA, HC, C], F16)

        with ExitStack() as pa:
            def sa(name, shape, dt=F32):
                return pa.enter_context(nc.sbuf_tensor(name, shape, dt))
            stage = sa("stage", [P, 2 * NW + HC * C])
            nat = stage[:, 0:8 * C].rearrange("p (j c) -> p j c", c=C)
            ident_h = sa("ident_h", [P, P], F16)
            mask_a = sa("mask_a", [P, HEADS, SPAN], F16)
            mask_t = sa("mask_t", [P, SPAN], F16)
            aug_l = sa("aug_l", [P, T, QUADS, P], F16)
            aug_c = sa("aug_c", [P, N], F16)
            parity = sa("parity", [P, 2])
            filt = sa("filt", [P, 18])
            band_h = sa("band_h", [P, 6, P], F16)
            band_l = sa("band_l", [P, 6, P], F16)
            seam_w = sa("seam_w", [P, 2, P], F16)
            seam = sa("seam", [64, IMG], F16)
            seam_part = sa("seam_part", [P, 1])
            bq4 = sa("bq4", [P, 6])
            bv = sa("bv", [P, C])
            pb = sa("pb", [P, C])
            gb = sa("gb", [P, E])
            qkvT_h = sa("qkvT_h", [P, KC, 3 * C], F16)
            qkvT_l = sa("qkvT_l", [P, KC, 3 * C], F16)
            projT_h = sa("projT_h", [P, KC, C], F16)
            projT_l = sa("projT_l", [P, KC, C], F16)
            gateT_h = sa("gateT_h", [P, KC, E], F16)
            gateT_l = sa("gateT_l", [P, KC, E], F16)
            xin = sa("xin", [P, 2, 3, IMG])
            gray = xin[:, :, 0]
            gray_h = sa("gray_h", [P, 2, IMG + 2], F16)
            gray_l = sa("gray_l", [P, 2, IMG + 2], F16)
            ab = sa("ab", [P, 2, IMG])
            h = sa("h", [P, T, C])
            hp = sa("hp", [P, 2, T, C])
            stats = sa("stats", [P, 2, T, 6])
            mv = sa("mv", [P, 2, T, 2])
            std = sa("std", [P, 2, T])
            rstd = sa("rstd", [P, 2, T])
            xn1 = sa("xn1", [P, T, C])
            xT_h = sa("xT_h", [P, KC, N], F16)
            xT_l = sa("xT_l", [P, KC, N], F16)
            qs = sa("qs", [P, N])
            q_h = sa("q_h", [P, 2, 2, 2, N], F16)
            q_l = sa("q_l", [P, 2, 2, 2, N], F16)
            k_h = sa("k_h", [P, 2, 2, N], F16)
            k_l = sa("k_l", [P, 2, 2, N], F16)
            v_aug = sa("v_aug", [P, 2, T, HEADS, HD + 1])
            mx = sa("mx", [P, T, P])
            aug_r = sa("aug_r", [P, N], F16)
            prob = sa("prob", [P, 2, G, 512])
            flat = prob[:, :, :, :].rearrange("p a g n -> p (a g n)")
            shift = flat[:, 0:3 * P].rearrange("p (j n) -> p j n", j=3)
            seam_sel = flat[:, 18 * P:24 * P].rearrange("p (j n) -> p j n", j=6)
            band = flat[:, 24 * P:30 * P].rearrange("p (j n) -> p j n", j=6)
            seam_f = flat[:, 30 * P:32 * P].rearrange("p (j n) -> p j n", j=2)
            rows_b1 = flat[0:EA, 8 * P:11 * P].rearrange("p (c n) -> p c n", c=HC)
            rows_b3 = flat[0:EA, 11 * P:14 * P].rearrange("p (c n) -> p c n", c=HC)
            rows_qb = flat[0:6, 14 * P:15 * P]
            gate_n = flat[0:E, 16 * P:18 * P]
            rs = sa("rs", [P, T, G])
            ao = sa("ao", [P, T, C])
            aoT_h = sa("aoT_h", [P, KC, N], F16)
            aoT_l = sa("aoT_l", [P, KC, N], F16)
            h1 = sa("h1", [P, T, C])
            xn2 = sa("xn2", [P, 2, T, C])
            x2 = sa("x2", [P, 2, KC, N], F16)
            lgs = sa("lgs", [P, T, E])
            rmax = sa("rmax", [P, T])
            rex = sa("rex", [P, T, E])
            rsum = sa("rsum", [P, T])
            rinv = sa("rinv", [P, T])
            score = sa("score", [P, T, E])
            biased = sa("biased", [P, T, E])
            cmp1 = sa("cmp1", [P, T, E, E])
            cmp2 = sa("cmp2", [P, T, E, E])
            rank = sa("rank", [P, T, E])
            pick = sa("pick", [P, T, 2, E])
            pickw = sa("pickw", [P, T, 2, E])
            chosen = sa("chosen", [P, T, E], F16)
            chosen_n = sa("chosen_n", [P, E])
            slot = sa("slot", [P, T, E])
            slot_f = sa("slot_f", [P, T, 2])
            idx = sa("idx", [P, T, 2], U32)

        with ExitStack() as pe_:
            def se(name, shape, dt=F32):
                return pe_.enter_context(nc.sbuf_tensor(name, shape, dt))
            tile_cmp = se("tile_cmp", [1, NT, E])
            tile_mul = se("tile_mul", [1, NT, E])
            moved = se("moved", [P, E, B * T, 2])
            b2b = se("b2b", [P, E, C])
            xg = se("xg", [P, 2, 2, C])
            xe_h = se("xe_h", [P, 2, KC, TW], F16)
            xe_l = se("xe_l", [P, 2, KC, TW], F16)
            yo = se("yo", [P, 2, 2, C])
            x2c = se("x2c", [P, 2, 2, KC, N], F16)
            h1c = se("h1c", [P, 2, T, C])
            yg = se("yg", [P, 2, T, 2, C])
            idxc = se("idxc", [P, 2, T, 2], U32)
            acc = se("acc", [P, 2, T, C])
            u3 = se("u3", [P, 2, N])
            prd = se("prd", [P, 2, N])
            hs = se("hs", [P, 2, N])
            hT_h = se("hT_h", [P, 2, HC, N], F16)
            hT_l = se("hT_l", [P, 2, HC, N], F16)

        s = {n: ctx.enter_context(nc.semaphore(n)) for n in (
            "consts", "consts2", "nat_in", "rb_in", "pads", "ones", "ident_h", "setup_t", "setup_h", "setup_l",
            "bias_done", "filt_done", "chain", "w_in", "w_hi", "w_lo",
            "x_in", "txt_in", "gsum", "gray", "gray_hi", "gray_lo", "seam", "conv", "absd", "edge", "hp", "var1", "std1", "rst1", "xn1", "xT", "xTh", "xTl",
            "qk", "q_ev", "vps", "vaug", "q_hi", "k_hi", "q_lo", "k_lo", "smax", "mx", "mxT", "aug", "st", "exp", "av",
            "rs", "ao", "aoT", "aoh", "aol", "pj", "h1", "var2", "std2", "rst2", "xn2", "xT2", "x2h", "x2l",
            "lg", "lgs", "rexp", "chosen", "pos", "rt", "pp", "idx", "h1s", "h1_out", "x2_out", "scat",
            "stat1", "stat2",
            "total", "padidx", "padsc", "tab", "tabc",
            "xg0", "xg1", "xT3", "xeh", "xel", "up", "u3", "prod", "silu", "hl", "yps", "yo", "st0", "st1",
            "cx0", "cx1", "ch0", "ch1", "idxc", "g0", "g1", "cup", "cu3", "cprod", "csilu", "chl", "cyps", "gated", "bgated",
            "cacc", "cfirst", "cdone", "co0", "co1")}
        N_CONST, N_CONST2 = 10, 8

        def mm3(out_ap, lh, ll, rh, rl, start, stop):
            nc.tensor.matmul(out_ap, lh, rh, start=start, stop=False)
            nc.tensor.matmul(out_ap, lh, rl, start=False, stop=False)
            return nc.tensor.matmul(out_ap, ll, rh, start=False, stop=stop)

        def row(v):
            return v.rearrange("(a n) -> a n", a=1)

        def rows_of(c):
            return P if c < HC - 1 else HLAST

        def bank_tiles(k):
            return ps[:, FB + k, :].rearrange("p (t d) -> p t d", t=2) if k == 0 else ps[:, FB + 1:FB + 2, 0:C]

        def shifted(line):
            return bass.AP(tensor=line.tensor, offset=line.offset, ap=[line.ap[0], [1, 3], [1, IMG]])

        block = ctx.enter_context(nc.Block())
        x_r = x.rearrange("b c (f p) w -> b f p c w", p=P)
        out_r = out.rearrange("b (t p) d -> b p t d", p=P)

        def images(eng, body):
            body(0, 0, False, False, False)
            body(1, 1, True, False, False)
            with eng.Fori(1, B // 2 - 1) as u:
                body(2 * u, 0, True, True, False)
                body(2 * u + 1, 1, True, True, False)
            body(B - 2, 0, True, True, False)
            body(B - 1, 1, True, True, True)

        def after_next(i):
            return not (isinstance(i, int) and i + 2 >= B)

        def groups(eng, count, body, per=2, value=None):
            def group(j, end):
                seen = {}

                def read(at):
                    if at not in seen:
                        seen[at] = value(j + at)
                    return seen[at]

                for k in range(per):
                    body(j + k, k % 2, end and k == per - 1, *([lambda d, k=k: read(k + d)] if value else []))
            group(0, False)
            with eng.Fori(1, count // per - 1) as u:
                group(per * u, False)
            group(count - per, True)

        def in_slot(n, par):
            return 8 * n + 8 * (2 - par)

        @block.sync
        def _(sp):
            sp.dma_start(nat[:, 0:6, :], qkv_w.rearrange("(j p) c -> p j c", p=P)).then_inc(s["nat_in"], 16)
            sp.dma_start(nat[:, 6:8, :], proj_w.rearrange("(j p) c -> p j c", p=P)).then_inc(s["nat_in"], 16)
            sp.dma_start(gate_n[:, :], gate_w).then_inc(s["nat_in"], 16)
            sp.dma_start(rows_qb[:, :], qkv_b.rearrange("(j p) -> j p", p=P)).then_inc(s["nat_in"], 16)
            sp.dma_start(filt[:, :], scharr.rearrange("a b c d -> b (a c d)").to_broadcast([P, 18])).then_inc(s["consts"], 16)
            for dst, src in ((ident, k_ident), (shift, k_shift), (seam_sel, k_seam_sel), (seam_part, k_seam_part), (parity, k_parity), (mask_a, k_mask_a), (mask_t, k_mask_t),
                             (aug_l, k_aug_l), (aug_c, k_aug_c)):
                sp.dma_start(dst[:], src).then_inc(s["consts"], 16)

            def load_x(n):
                need(sp, s["gray_lo"], n)
                for f in range(2):
                    sp.dma_start(xin[:, f], x_r[n, f]).then_inc(s["x_in"], 16)

            def load_txt(n):
                need(sp, s["hp"], n)
                need(sp, s["xn1"], n)
                sp.dma_start(h[:, 2, :], txt[n]).then_inc(s["txt_in"], 16)

            load_x(0)
            load_txt(0)
            for dst, src in ((bv, row(qkv_b[2 * C:3 * C])), (pb, row(proj_b)), (sb2b, row(sb2)), (gb, row(gate_b))):
                sp.dma_start(dst[:, :], src.to_broadcast([P, src.shape[1]])).then_inc(s["consts2"], 16)
            for dst, src in ((before, k_before), (tri, k_tri), (ebase, k_ebase), (tile_no, k_tile)):
                sp.dma_start(dst[:], src).then_inc(s["consts2"], 16)
            sp.wait_ge(s["pads"], 2)
            for dst, be, bs in ((rows_b1, b1, sb1), (rows_b3, b3, sb3)):
                f = dst[:, :, :].rearrange("e c p -> e (c p)")
                sp.dma_start(f[0:E, 0:HID], be).then_inc(s["rb_in"], 16)
                sp.dma_start(f[E:EA, 0:HID], row(bs)).then_inc(s["rb_in"], 16)

            def load_seam(n):
                need(sp, s["gray_lo"], n + 1)
                for f in range(2):
                    row_of = 0 if f == 0 else P - 1
                    for a, g in enumerate((gray_h, gray_l)):
                        for b in range(2):
                            at = 32 * f + 6 * a + 3 * b
                            line = g[row_of:row_of + 1, 1 - f, 0:IMG]
                            sp.dma_start(seam[at:at + 3, :], shifted(line)).then_inc(s["seam"], 16)

            load_seam(0)
            load_x(1)
            load_seam(1)

            def store(n):
                need(sp, s["h1s"], n + 1)
                sp.dma_start(h1_d[n], h1[:, :, :]).then_inc(s["h1_out"], 16)
                need(sp, s["x2l"], n + 1)
                sp.dma_start(x2_d[n], x2[:, :, :, :]).then_inc(s["x2_out"], 16)

            def body(i, par, back1, back2, last):
                if not last:
                    load_txt(i + 1)
                if after_next(i):
                    load_x(i + 2)
                if back1:
                    store(i - 1)
                if after_next(i):
                    load_seam(i + 2)

            images(sp, body)
            store(B - 1)

            def rows(dram, r):
                return dram[bass.ds(r, TW), :].rearrange("(t p) d -> p t d", p=P)

            sp.wait_ge(s["total"], 1)
            sp.wait_ge(s["scat"], 96 * B)
            sp.wait_ge(s["x2_out"], 16 * B)
            sp.wait_ge(s["h1_out"], 16 * B)
            sp.wait_ge(s["padidx"], 1)
            for e in range(E):
                behind = sp.value_load(pad_row[0:1, e:e + 1], min_val=0, max_val=E * REGION - TW)
                sp.dma_start(rows(xs_d, behind), zrow[:, :].rearrange("p (a c) -> p a c", a=1).to_broadcast([P, 2, C])).then_inc(s["padsc"], 16)

            sp.wait_ge(s["padsc"], 16 * E)
            sp.wait_ge(s["tab"], 1)

            def load_tile(j, par, used):
                need(sp, s["xT3"], used)
                first = sp.value_load(tile_tab[0:1, 1, bass.ds(j, 1)], min_val=0, max_val=E * REGION - TW)
                sp.dma_start(xg[:, par], rows(xs_d, first)).then_inc(s[f"xg{par}"], 16)

            load_tile(0, 0, 0)
            load_tile(1, 1, 0)
            for e in range(E):
                sp.dma_start(b2b[:, e, :], b2[e:e + 1, :].to_broadcast([P, C])).then_inc(s["tabc"], 16)

            def body_b(j, par, last):
                if not (isinstance(j, int) and j + 2 >= NT):
                    load_tile(j + 2, par, j + 1)
            groups(sp, NT, body_b)
            def load_x2(n, par):
                need(sp, s["cup"], 6 * n - 6)
                sp.dma_start(x2c[:, par], x2_d[n]).then_inc(s[f"cx{par}"], 16)

            def load_h1(n, par):
                need(sp, s["cacc"], 3 * n - 3)
                sp.dma_start(h1c[:, par], h1_d[n]).then_inc(s[f"ch{par}"], 16)

            load_x2(0, 0)
            load_h1(0, 0)
            sp.dma_start(x2c[:, 1], x2_d[1]).then_inc(s["cx1"], 16)
            sp.dma_start(h1c[:, 1], h1_d[1]).then_inc(s["ch1"], 16)

            def body_c(n, par, last):
                if after_next(n):
                    load_x2(n + 2, par)
                    load_h1(n + 2, par)
                sp.wait_ge(s["cdone"], n + 1)
                sp.dma_start(out_r[n], acc[:, par]).then_inc(s[f"co{par}"], 16)
            groups(sp, B, body_c)
            sp.wait_ge(s["co0"], 16 * (B // 2))
            sp.wait_ge(s["co1"], 16 * (B // 2))

        @block.tensor
        def _(pe):
            pe.wait_ge(s["nat_in"], 64)
            pe.wait_ge(s["consts"], 16 * N_CONST)
            pe.wait_ge(s["rb_in"], 64)

            def turn(slot, in_, n):
                return nc.tensor.transpose(ps[:, slot // 4, P * (slot % 4):P * (slot % 4) + n], in_, ident[0:n, 0:n])

            for j in range(8):
                for k in range(KC):
                    turn(j * KC + k, nat[:, j, k * P:(k + 1) * P], P)
            for k in range(KC):
                turn(16 + k, gate_n[:, k * P:(k + 1) * P], E)
            turn(18, rows_qb[:, :], 6)
            for c in range(HC):
                turn(20 + c, rows_b1[:, c, :], EA)
                last = turn(24 + c, rows_b3[:, c, :], EA)
            last.then_inc(s["setup_t"], 1)
            pe.wait_ge(s["setup_l"], 2)
            pe.wait_ge(s["bias_done"], 3)
            pe.wait_ge(s["filt_done"], 1)
            pe.wait_ge(s["ident_h"], 1)
            pe.wait_ge(s["consts2"], 16 * N_CONST2)

            def conv(n, f, filters=range(2)):
                pe.wait_ge(s["gray_lo"], n + 1)
                pe.wait_ge(s["seam"], 128 * n + 128)
                for q in filters:
                    o = ps[:, FB + f, q * IMG:(q + 1) * IMG]
                    for dx in range(3):
                        i = 3 * q + dx
                        nc.tensor.matmul(o, band_h[:, i, :], gray_h[:, f, dx:dx + IMG], start=dx == 0, stop=False)
                        nc.tensor.matmul(o, band_h[:, i, :], gray_l[:, f, dx:dx + IMG], start=False, stop=False)
                        nc.tensor.matmul(o, band_l[:, i, :], gray_h[:, f, dx:dx + IMG], start=False, stop=False)
                    r = slice(32 * f, 32 * f + 12)
                    last = nc.tensor.matmul(o, seam_w[r, q, :], seam[r, :],
                                            start=False, stop=True)
                if q == 1:
                    last.then_inc(s["conv"], 1)

            def turn_rows(src, sem):
                for k in range(KC):
                    for t in range(T):
                        last = nc.tensor.transpose(ps[:, FB + k, t * P:(t + 1) * P], src[:, t, k * P:(k + 1) * P], ident[:, :])
                last.then_inc(sem, 1)

            def qk(n, c):
                for k in range(KC):
                    w = slice(c * P, (c + 1) * P)
                    last = mm3(ps[:, FB + (c < 2), 0:N], qkvT_h[:, k, w], qkvT_l[:, k, w], xT_h[:, k, :], xT_l[:, k, :],
                               k == 0, k == KC - 1)
                last.then_inc(s["qk"], 1)

            def by_rows(lh, ll, rh, rl, sem, tiles=range(T)):
                for t in tiles:
                    for k in range(KC):
                        r = slice(t * P, (t + 1) * P)
                        last = mm3(ps[:, FB + t // 2, (t % 2) * C:(t % 2 + 1) * C], lh[:, k, r], ll[:, k, r],
                                   rh[:, k], rl[:, k], k == 0, k == KC - 1)
                if t == T - 1:
                    last.then_inc(sem, 1)

            def smax(n, par, q):
                need(pe, s["exp"], 16 * n + 4 * q)
                c, pr = q // 2, q % 2
                cols = [(t, 0 if t == 0 else t * P - WINDOW, (t + 1) * P, 0 if t == 0 else P + (t - 1) * SPAN) for t in range(T)]
                for t, lo, hi, at in cols:
                    for g in range(G):
                        r = slice(32 * g, 32 * g + 32)
                        nc.tensor.matmul(ps[:, g, at:at + hi - lo], q_h[r, par, pr, c, t * P:(t + 1) * P], k_h[r, par, c, lo:hi],
                                         start=t == 0, stop=False, skip_group_check=True)
                for g in range(G):
                    for t, lo, hi, at in cols:
                        last = nc.tensor.matmul(ps[:, g, at:at + hi - lo], ident_h[:, :], mask_a[:, head_of(q, g), SPAN - hi + lo:],
                                                start=False, stop=True, skip_group_check=True)
                last.then_inc(s["smax"], 1)

            def max_turn(n, q):
                pe.wait_ge(s["mx"], 4 * n + q + 1)
                for t in range(T):
                    last = nc.tensor.transpose(ps[:, 0, t * P:(t + 1) * P], mx[:, t, :], ident[:, :])
                last.then_inc(s["mxT"], 1)

            def masks(heads, tiles):
                for g in heads:
                    for j in tiles:
                        w = min(SPAN, N - j * P)
                        nc.tensor.matmul(ps[:, g, j * SPAN:j * SPAN + w], ident_h[:, :], mask_t[:, 0:w], start=j == 0, stop=False,
                                         skip_group_check=True)

            def scores(n, par, q, j):
                if 0 < j < T - 1:
                    masks(range(G), (j,))
                c, pr = q // 2, q % 2
                w = min(SPAN, N - j * P)
                km, qn, at = slice(j * P, (j + 1) * P), slice(j * P, j * P + w), j * SPAN
                for step in range(4):
                    for g in range(G):
                        r = slice(32 * g, 32 * g + 32)
                        kk, qq = ((k_h[r, par, c, km], q_h[r, par, pr, c, qn]), (k_h[r, par, c, km], q_l[r, par, pr, c, qn]),
                                  (k_l[r, par, c, km], q_h[r, par, pr, c, qn]), (aug_l[r, j, q, :], aug_r[r, qn]))[step]
                        ins = nc.tensor.matmul(ps[:, g, at:at + w], kk, qq, start=False, stop=step == 3, skip_group_check=True)
                        if j == T - 1 and step == 3:
                            ins.then_inc(s["st"], 1)

            def masks_and_first(n, par, q):
                masks(range(1, G), (0, T - 1))
                pe.wait_ge(s["aug"], 4 * n + q + 1)
                masks(range(1), (0, T - 1))
                scores(n, par, q, 0)

            def attend(n, par, q, g, t):
                if g == 0 and t == 0:
                    need(pe, s["ao"], 4 * n + q - 1)
                if t == 0:
                    pe.wait_ge(s["exp"], 16 * n + 4 * q + g + 1)
                hh = head_of(q, g)
                o = ps[:, 4 + q % 2, (t * G + g) * (HD + 1):(t * G + g + 1) * (HD + 1)]
                last = nc.tensor.matmul(o, prob[:, q % 2, g, t * SPAN:t * SPAN + P], v_aug[:, par, t, hh, :], start=True, stop=True)
                if t > 0:
                    last = nc.tensor.matmul(o[0:WINDOW], prob[:, q % 2, g, (t - 1) * SPAN + P:t * SPAN],
                                            v_aug[:, par, t - 1, hh, :], start=False, stop=True, skip_group_check=True)
                if g == G - 1 and t == T - 1:
                    last.then_inc(s["av"], 1)

            def attend_half(n, par, q, half):
                for g in range(2 * half, 2 * half + 2):
                    for t in range(T):
                        attend(n, par, q, g, t)

            def gate(n):
                for t in range(T):
                    for k in range(KC):
                        r = slice(t * P, (t + 1) * P)
                        last = mm3(ps[:, FB + 1, C + t * E:C + (t + 1) * E], x2[:, 0, k, r], x2[:, 1, k, r], gateT_h[:, k, :], gateT_l[:, k, :],
                                   k == 0, k == KC - 1)
                last.then_inc(s["lg"], 1)

            def position(n):
                pe.wait_ge(s["chosen"], n + 1)
                need(pe, s["pp"], n)
                for t in range(T):
                    o = ps[:, FB + 1, N + t * E:N + (t + 1) * E]
                    nc.tensor.matmul(o, tri[:, 0, :], chosen[:, t, :], start=True, stop=False)
                    for t2 in range(t):
                        nc.tensor.matmul(o, tri[:, 1, :], chosen[:, t2, :], start=False, stop=False)
                    last = nc.tensor.matmul(o, tri[:, 1, :], counts[:, :], start=False, stop=True)
                last.then_inc(s["pos"], 1)

            def front_x(n):
                pe.wait_ge(s["xn1"], n + 1)
                turn_rows(xn1, s["xT"])

            def value(tiles):
                by_rows(xT_h, xT_l, qkvT_h[:, :, 2 * C:], qkvT_l[:, :, 2 * C:], s["vps"], tiles)

            def tail_logits(n):
                pe.wait_ge(s["x2l"], n + 1)
                gate(n)

            conv(0, 0)
            conv(0, 1)
            pe.wait_ge(s["absd"], 2)
            front_x(0)
            pe.wait_ge(s["xTl"], 1)
            qk(0, 2)
            qk(0, 0)
            pe.wait_ge(s["k_lo"], 1)
            pe.wait_ge(s["q_ev"], 1)
            qk(0, 3)
            qk(0, 1)
            pe.wait_ge(s["q_lo"], 2)

            def body(i, par, back1, back2, last):
                smax(i, par, 0)
                if back1:
                    attend_half(i - 1, 1 - par, 3, 0)
                pe.wait_ge(s["k_lo"], 2 * i + 2)
                pe.wait_ge(s["q_ev"], 2 * i + 2)
                if back2:
                    tail_logits(i - 2)
                value(range(2))
                max_turn(i, 0)
                masks_and_first(i, par, 0)
                value(range(2, T))
                scores(i, par, 0, 1)
                scores(i, par, 0, 2)
                pe.wait_ge(s["vaug"], 2 * i + 2)
                if not last:
                    conv(i + 1, 0)
                if back2:
                    pe.wait_ge(s["lgs"], i - 1)
                if not last:
                    conv(i + 1, 1, (0,))
                if back1:
                    attend_half(i - 1, 1 - par, 3, 1)
                smax(i, par, 1)
                attend_half(i, par, 0, 0)
                if not last:
                    conv(i + 1, 1, (1,))
                max_turn(i, 1)
                masks_and_first(i, par, 1)
                if not last:
                    pe.wait_ge(s["absd"], 2 * i + 4)
                if back2:
                    position(i - 2)
                if back1:
                    pe.wait_ge(s["ao"], 4 * i)
                    turn_rows(ao, s["aoT"])
                scores(i, par, 1, 1)
                scores(i, par, 1, 2)
                if back2:
                    pe.wait_ge(s["pp"], i - 1)
                if back1:
                    pe.wait_ge(s["aol"], i)
                    by_rows(aoT_h, aoT_l, projT_h, projT_l, s["pj"])
                attend_half(i, par, 0, 1)
                pe.wait_ge(s["q_lo"], 4 * i + 4)
                smax(i, par, 2)
                attend_half(i, par, 1, 0)
                if back1:
                    pe.wait_ge(s["h1"], 2 * i)
                if not last:
                    front_x(i + 1)
                max_turn(i, 2)
                masks_and_first(i, par, 2)
                if not last:
                    pe.wait_ge(s["xTl"], i + 2)
                    qk(i + 1, 2)
                scores(i, par, 2, 1)
                scores(i, par, 2, 2)
                if not last:
                    qk(i + 1, 0)
                attend_half(i, par, 1, 1)
                smax(i, par, 3)
                attend_half(i, par, 2, 0)
                if not last:
                    pe.wait_ge(s["k_lo"], 2 * i + 3)
                    pe.wait_ge(s["q_ev"], 2 * i + 3)
                if back1:
                    pe.wait_ge(s["xn2"], i)
                    turn_rows(xn2[:, 1 - par], s["xT2"])
                max_turn(i, 3)
                masks_and_first(i, par, 3)
                if back1:
                    pe.wait_ge(s["x2l"], i)
                if not last:
                    qk(i + 1, 3)
                scores(i, par, 3, 1)
                scores(i, par, 3, 2)
                if not last:
                    qk(i + 1, 1)
                attend_half(i, par, 2, 1)
                if not last:
                    pe.wait_ge(s["q_lo"], 4 * i + 6)

            images(pe, body)
            attend_half(B - 1, 1, 3, 0)
            attend_half(B - 1, 1, 3, 1)
            tail_logits(B - 2)
            pe.wait_ge(s["lgs"], B - 1)
            position(B - 2)
            pe.wait_ge(s["ao"], 4 * B)
            pe.wait_ge(s["pp"], B - 1)
            turn_rows(ao, s["aoT"])
            pe.wait_ge(s["aol"], B)
            by_rows(aoT_h, aoT_l, projT_h, projT_l, s["pj"])
            pe.wait_ge(s["h1"], 2 * B)
            pe.wait_ge(s["xn2"], B)
            turn_rows(xn2[:, (B - 1) % 2], s["xT2"])
            tail_logits(B - 1)
            pe.wait_ge(s["lgs"], B)
            position(B - 1)
            pe.wait_ge(s["pp"], B)
            nc.tensor.matmul(ps[:, 0, 0:E], tri[:, 1, :], counts[:, :], start=True, stop=True).then_inc(s["total"], 1)

            pe.wait_ge(s["tab"], 1)
            pe.wait_ge(s["w_lo"], 4 * EA)

            def turn_tile(n, par, nth):
                pe.wait_ge(s[f"xg{par}"], nth)
                need(pe, s["xel"], n - 1)
                for t in range(2):
                    for k in range(KC):
                        last = nc.tensor.transpose(ps[:, 6 + par, k * TW + t * P:k * TW + (t + 1) * P], xg[:, par, t, k * P:(k + 1) * P], ident[:, :])
                last.then_inc(s["xT3"], 1)

            def up(n, par, c, e, xh, xl, width, names):
                m = rows_of(c)
                need(pe, s[names["prod"]], 3 * n + c - 1)
                o = (par + c) % 2
                for j, (wh, wl) in enumerate(((w3_h, w3_l), (w1_h, w1_l))):
                    for k in range(KC):
                        wv = [a[:, e, k, c * P:c * P + m] if isinstance(e, int) else
                              a[:, bass.ds(e, 1), k, c * P:c * P + m].rearrange("p a n -> p (a n)") for a in (wh, wl)]
                        last = mm3(ps[0:m, 2 * o + j, 0:width], wv[0], wv[1], xh[:, k, :], xl[:, k, :], k == 0, k == KC - 1)
                    last.then_inc(s[names["up"]], 1)

            def down(n, par, t, e, names):
                for c in range(HC):
                    m = rows_of(c)
                    r = slice(t * P, (t + 1) * P)
                    wv = [a[0:m, e, c, :] if isinstance(e, int) else
                          a[0:m, bass.ds(e, 1), c, :].rearrange("p a n -> p (a n)") for a in (w2_h, w2_l)]
                    last = mm3(ps[:, 4 + t, 0:C], hT_h[0:m, par, c, r], hT_l[0:m, par, c, r], wv[0], wv[1], c == 0, c == HC - 1)
                last.then_inc(s[names["yps"]], 1)

            def expert(j):
                return pe.value_load(tile_tab[0:1, 0, bass.ds(j, 1)], min_val=0, max_val=E - 1)

            NB = dict(prod="prod", up="up", yps="yps")
            turn_tile(0, 0, 16)
            turn_tile(1, 1, 16)
            pe.wait_ge(s["xel"], 1)
            e0 = expert(0)
            for c in range(HC):
                up(0, 0, c, e0, xe_h[:, 0], xe_l[:, 0], TW, NB)

            def body_b(j, par, last, expert_of):
                if not last:
                    e1 = expert_of(1)
                    pe.wait_ge(s["xel"], j + 2)
                    up(j + 1, 1 - par, 0, e1, xe_h[:, 1 - par], xe_l[:, 1 - par], TW, NB)
                if not (isinstance(j, int) and j + 2 >= NT):
                    turn_tile(j + 2, par, in_slot(j + 2, par))
                e = expert_of(0)
                pe.wait_ge(s["hl"], 3 * j + 3)
                need(pe, s["yo"], 2 * j - 1)
                down(j, par, 0, e, NB)
                if not last:
                    for c in range(1, HC):
                        up(j + 1, 1 - par, c, e1, xe_h[:, 1 - par], xe_l[:, 1 - par], TW, NB)
                need(pe, s["yo"], 2 * j)
                down(j, par, 1, e, NB)
            groups(pe, NT, body_b, TILES_PER, expert)

            NC = dict(prod="cprod", up="cup", yps="cyps")
            pe.wait_ge(s["yo"], 2 * NT)
            pe.wait_ge(s["prod"], 3 * NT)
            pe.wait_ge(s["cx0"], 16)
            for c in range(HC):
                up(0, 0, c, E, x2c[:, 0, 0], x2c[:, 0, 1], N, NC)

            def body_c(n, par, last):
                if not last:
                    pe.wait_ge(s[f"cx{1 - par}"], in_slot(n + 1, 1 - par))
                for t in range(T):
                    if not last:
                        up(n + 1, 1 - par, t, E, x2c[:, 1 - par, 0], x2c[:, 1 - par, 1], N, NC)
                    if t == 0:
                        pe.wait_ge(s["chl"], 3 * n + 3)
                    need(pe, s["cacc"], 3 * n + t - 2)
                    down(n, par, t, E, NC)
            groups(pe, B, body_c)

        @block.scalar
        def _(act):
            act.wait_ge(s["consts"], 16 * N_CONST)
            act.wait_ge(s["ones"], 1)
            nc.scalar.copy(ident_h[:, :], ident[:, :]).then_inc(s["ident_h"], 1)
            act.wait_ge(s["setup_t"], 1)
            for j in range(8):
                for k in range(KC):
                    at = j * KC + k
                    dst = qkvT_h[:, k, j * P:(j + 1) * P] if j < 6 else projT_h[:, k, (j - 6) * P:(j - 5) * P]
                    nc.scalar.copy(dst, ps[:, at // 4, P * (at % 4):P * (at % 4 + 1)])
            nc.scalar.copy(gateT_h[:, :, :], ps[:, 4, 0:KC * P].rearrange("p (k n) -> p k n", k=KC)[:, :, 0:E]).then_inc(s["setup_h"], 1)
            nc.scalar.copy(bias1[:, :, :], ps[:, 5, 0:HC * P].rearrange("p (c n) -> p c n", c=HC)[:, :, 0:EA]).then_inc(s["bias_done"], 1)
            nc.scalar.copy(bias3[:, :, :], ps[:, 6, 0:HC * P].rearrange("p (c n) -> p c n", c=HC)[:, :, 0:EA]).then_inc(s["bias_done"], 1)
            nc.scalar.copy(bq4[:, 2:6], ps[:, 4, 2 * P + 2:2 * P + 6])
            nc.scalar.mul(bq4[:, 0:2], ps[:, 4, 2 * P:2 * P + 2], SCALE).then_inc(s["bias_done"], 1)
            act.wait_ge(s["bias_done"], 3)

            def edge_abs(n, f):
                act.wait_ge(s["conv"], 2 * n + f + 1)
                need(act, s["edge"], 2 * n + f)
                nc.scalar.activation(ab[:, :, :], ps[:, FB + f, :].rearrange("p (q w) -> p q w", q=2), ACT.Abs, scale=0.5).then_inc(s["absd"], 1)

            def root(n, k):
                act.wait_ge(s["var1" if k == 0 else "var2"], n + 1)
                nc.scalar.activation(std[:, k, :], mv[:, k, :, 1], ACT.Sqrt, bias=eps[:, :]).then_inc(s["std1" if k == 0 else "std2"], 1)

            def xt_high(n):
                act.wait_ge(s["xT"], n + 1)
                need(act, s["vps"], n)
                nc.scalar.copy(xT_h[:, :, :], ps[:, FB:FB + 2, 0:N]).then_inc(s["xTh"], 1)

            def qk_out(n, par, c):
                act.wait_ge(s["qk"], 4 * n + 2 * c + 1)
                nc.scalar.activation(k_h[:, par, c, :], ps[:, FB, 0:N], ACT.Identity, bias=bq4[:, 2 + c:3 + c]).then_inc(s["k_hi"], 1)
                act.wait_ge(s["qk"], 4 * n + 2 * c + 2)
                need(act, s["q_lo"], 4 * n + 2 * c)
                nc.scalar.activation(qs[:, :], ps[:, FB + 1, 0:N], ACT.Identity, scale=SCALE, bias=bq4[:, c:c + 1]).then_inc(s["q_ev"], 1)

            def q_high(n, par, c):
                act.wait_ge(s["q_ev"], 2 * n + c + 1)
                for pr in range(2):
                    nc.scalar.activation(q_h[:, par, pr, c], qs[:, :], ACT.Copy, scale=parity[:, pr:pr + 1]).then_inc(s["q_hi"], 1)

            def softmax_exp(n, q):
                for g in range(G):
                    act.wait_ge(s["st"], 16 * n + 4 * q + g + 1)
                    if g == 0:
                        need(act, s["av"], 4 * n + q - 1)
                    nc.scalar.activation(prob[:, q % 2, g, :], ps[:, g, :], ACT.Exp).then_inc(s["exp"], 1)

            def ao_high(n):
                act.wait_ge(s["aoT"], n + 1)
                nc.scalar.copy(aoT_h[:, :, :], ps[:, FB:FB + 2, 0:N]).then_inc(s["aoh"], 1)

            def x2_high(n):
                act.wait_ge(s["xT2"], n + 1)
                need(act, s["x2_out"], 16 * n)
                nc.scalar.copy(x2[:, 0], ps[:, FB:FB + 2, 0:N]).then_inc(s["x2h"], 1)

            def gate_exp(n):
                act.wait_ge(s["lgs"], n + 1)
                nc.scalar.activation(rex[:, :, :], lgs[:, :, :], ACT.Exp).then_inc(s["rexp"], 1)

            def gray_high(n):
                act.wait_ge(s["gray"], n + 1)
                need(act, s["conv"], 2 * n)
                need(act, s["seam"], 128 * n)
                nc.scalar.copy(gray_h[:, :, 1:IMG + 1], gray).then_inc(s["gray_hi"], 1)

            gray_high(0)
            edge_abs(0, 0)
            edge_abs(0, 1)
            root(0, 0)
            gray_high(1)
            xt_high(0)
            qk_out(0, 0, 0)
            q_high(0, 0, 0)

            def body(i, par, back1, back2, last):
                qk_out(i, par, 1)
                q_high(i, par, 1)
                if back2:
                    gate_exp(i - 2)
                softmax_exp(i, 0)
                if not last:
                    edge_abs(i + 1, 0)
                    edge_abs(i + 1, 1)
                if not last:
                    root(i + 1, 0)
                if back1:
                    ao_high(i - 1)
                softmax_exp(i, 1)
                if not last:
                    xt_high(i + 1)
                if back1:
                    root(i - 1, 1)
                softmax_exp(i, 2)
                if not last:
                    qk_out(i + 1, 1 - par, 0)
                    q_high(i + 1, 1 - par, 0)
                if back1:
                    x2_high(i - 1)
                softmax_exp(i, 3)
                if after_next(i):
                    gray_high(i + 2)

            images(act, body)
            gate_exp(B - 2)
            ao_high(B - 1)
            root(B - 1, 1)
            x2_high(B - 1)
            gate_exp(B - 1)

            act.wait_ge(s["tab"], 1)

            def up_bias(n, par, c, e, width, nm):
                m = rows_of(c)
                o = (par + c) % 2
                act.wait_ge(s[nm + "up"], 6 * n + 2 * c + 1)
                need(act, s[nm + "prod"], 3 * n + c - 1)
                bias = bias3[0:m, c, e:e + 1] if isinstance(e, int) else bias3[0:m, c, bass.ds(e, 1)]
                nc.scalar.activation(u3[0:m, o, 0:width], ps[0:m, 2 * o, 0:width], ACT.Identity, bias=bias).then_inc(s[nm + "u3"], 1)

            def up_silu(n, par, c, width, nm):
                m = rows_of(c)
                o = (par + c) % 2
                act.wait_ge(s[nm + "prod"], 3 * n + c + 1)
                need(act, s[nm + "hl"], 3 * n + c - 1)
                nc.scalar.activation(hT_h[0:m, par, c, 0:width], prd[0:m, o, 0:width], ACT.Silu)
                nc.scalar.activation(hs[0:m, o, 0:width], prd[0:m, o, 0:width], ACT.Silu).then_inc(s[nm + "silu"], 1)

            def tile_high(n, par):
                act.wait_ge(s["xT3"], n + 1)
                need(act, s["up"], 6 * n - 6)
                nc.scalar.copy(xe_h[:, par], ps[:, 6 + par, :].rearrange("p (k n) -> p k n", k=KC)).then_inc(s["xeh"], 1)

            def up_all(n, par, e, width, nm, next_high=None):
                up_bias(n, par, 0, e, width, nm)
                if next_high is not None:
                    tile_high(*next_high)
                for c in range(1, HC):
                    up_bias(n, par, c, e, width, nm)
                    up_silu(n, par, c - 1, width, nm)
                up_silu(n, par, HC - 1, width, nm)

            def expert(n):
                return act.value_load(tile_tab[0:1, 0, bass.ds(n, 1)], min_val=0, max_val=E - 1)

            def one_tile(n, par, e, next_high=None):
                nc.scalar.activation(one_a[:, :], zero[:, :], ACT.Silu)
                up_all(n, par, e, TW, "", next_high)

            tile_high(0, 0)
            tile_high(1, 1)
            one_tile(0, 0, expert(0))

            def body_b(j, par, last, expert_of):
                if not last:
                    one_tile(j + 1, 1 - par, expert_of(1), None if isinstance(j, int) and j + 2 >= NT else (j + 2, par))
            groups(act, NT, body_b, TILES_PER, expert)
            act.wait_ge(s["hl"], 3 * NT)
            up_all(0, 0, E, N, "c")

            def body_c(n, par, last):
                nc.scalar.activation(one_a[:, :], zero[:, :], ACT.Silu)
                if not last:
                    up_all(n + 1, 1 - par, E, N, "c")
            groups(act, B, body_c)

        @block.vector
        def _(dve):
            nc.vector.memset(rows_b1[:, :, :], 0.0).then_inc(s["pads"], 1)
            nc.vector.memset(rows_b3[:, :, :], 0.0).then_inc(s["pads"], 1)
            nc.vector.memset(gray_h[:, :, :], 0.0)
            nc.vector.memset(gray_l[:, :, :], 0.0)
            nc.vector.memset(mx[:, :, :], 0.0)
            nc.vector.memset(v_aug[:, :, :, :, HD:HD + 1], 1.0)
            nc.vector.memset(counts[:, :], 0.0)
            nc.vector.memset(zrow[:, :], 0.0)
            nc.vector.memset(zero[:, :], 0.0)
            nc.vector.memset(eps[:, :], EPS).then_inc(s["ones"], 1)
            dve.wait_ge(s["ones"], 1)
            dve.wait_ge(s["consts"], 16 * N_CONST)
            count = [0]

            def link(ins):
                count[0] += 1
                ins.then_inc(s["chain"], 1)
                dve.wait_ge(s["chain"], count[0])

            for q in range(2):
                for dx in range(3):
                    i = 3 * q + dx
                    tap = [filt[:, 9 * q + 3 * dy + dx:9 * q + 3 * dy + dx + 1] for dy in range(3)]
                    link(nc.vector.tensor_scalar(band[:, i, :], shift[:, 0, :], tap[0], None, ALU.mult))
                    link(nc.vector.scalar_tensor_tensor(band[:, i, :], shift[:, 1, :], tap[1], band[:, i, :], ALU.mult, ALU.add))
                    link(nc.vector.scalar_tensor_tensor(band[:, i, :], shift[:, 2, :], tap[2], band[:, i, :], ALU.mult, ALU.add))
                for f in range(2):
                    for dx in range(3):
                        at = 9 * q + (6 if f == 0 else 0) + dx
                        if f == 0 and dx == 0:
                            link(nc.vector.tensor_scalar(seam_f[:, q, :], seam_sel[:, 0, :], filt[:, at:at + 1], None, ALU.mult))
                        else:
                            link(nc.vector.scalar_tensor_tensor(seam_f[:, q, :], seam_sel[:, 3 * f + dx, :], filt[:, at:at + 1],
                                                                seam_f[:, q, :], ALU.mult, ALU.add))
            link(nc.vector.tensor_copy(band_h[:, :, :], band[:, :, :]))
            nc.vector.tensor_tensor(band_l[:, :, :], band[:, :, :], band_h[:, :, :], ALU.subtract)
            link(nc.vector.tensor_copy(seam_w[:, :, :], seam_f[:, :, :]))
            link(nc.vector.tensor_scalar(seam_w[:, :, :], seam_w[:, :, :], seam_part[:, 0:1], None, ALU.mult))
            link(nc.vector.tensor_tensor(seam_w[:, :, :], seam_f[:, :, :], seam_w[:, :, :], ALU.subtract))
            nc.vector.memset(one_v[:, :], 1.0).then_inc(s["filt_done"], 1)
            dve.wait_ge(s["setup_h"], 1)
            dve.wait_ge(s["bias_done"], 3)
            for j in range(8):
                for k in range(KC):
                    at = j * KC + k
                    w = slice(j * P, (j + 1) * P) if j < 6 else slice((j - 6) * P, (j - 5) * P)
                    lo, hi = (qkvT_l, qkvT_h) if j < 6 else (projT_l, projT_h)
                    ins = nc.vector.tensor_tensor(lo[:, k, w], ps[:, at // 4, P * (at % 4):P * (at % 4 + 1)], hi[:, k, w], ALU.subtract)
            ins.then_inc(s["setup_l"], 1)
            nc.vector.tensor_tensor(gateT_l[:, :, :], ps[:, 4, 0:KC * P].rearrange("p (k n) -> p k n", k=KC)[:, :, 0:E], gateT_h[:, :, :],
                                    ALU.subtract).then_inc(s["setup_l"], 1)
            dve.wait_ge(s["consts2"], 16 * N_CONST2)

            def to_gray(n):
                dve.wait_ge(s["x_in"], 32 * n + 32)
                need(dve, s["gray_lo"], n)
                g = gray
                nc.vector.tensor_scalar(g, g, GRAY_W[0], None, ALU.mult).then_inc(s["gsum"], 1)
                dve.wait_ge(s["gsum"], 2 * n + 1)
                nc.vector.scalar_tensor_tensor(g, xin[:, :, 1], GRAY_W[1], g, ALU.mult, ALU.add).then_inc(s["gsum"], 1)
                dve.wait_ge(s["gsum"], 2 * n + 2)
                nc.vector.scalar_tensor_tensor(g, xin[:, :, 2], GRAY_W[2], g, ALU.mult, ALU.add).then_inc(s["gray"], 1)

            def edge_sum(n, f):
                dve.wait_ge(s["absd"], 2 * n + f + 1)
                if f == 0:
                    need(dve, s["hp"], n)
                nc.vector.tensor_tensor(h[:, f, :], ab[:, 0, :], ab[:, 1, :], ALU.add).then_inc(s["edge"], 1)

            def norm_stats(n, k, src):
                tag = str(k + 1)
                need(dve, s["var" + tag], n)
                for t in range(T):
                    ins = nc.vector.bn_stats(stats[:, k, t, :], src[:, t, :])
                ins.then_inc(s["stat" + tag], 1)
                dve.wait_ge(s["stat" + tag], n + 1)
                nc.vector.memset(one_v[:, :], 1.0)
                for t in range(T):
                    ins = nc.vector.bn_aggr(mv[:, k, t, :], stats[:, k, t, :])
                ins.then_inc(s["var" + tag], 1)

            def norm_rows(n, k, src, dst, done):
                tag = str(k + 1)
                dve.wait_ge(s["std" + tag], n + 1)
                nc.vector.reciprocal(rstd[:, k, :], std[:, k, :]).then_inc(s["rst" + tag], 1)
                dve.wait_ge(s["rst" + tag], n + 1)
                for t in range(T):
                    ins = nc.vector.tensor_scalar(dst[:, t, :], src[:, t, :], mv[:, k, t, 0:1], rstd[:, k, t:t + 1], ALU.subtract, ALU.mult)
                ins.then_inc(done, 1)

            def norm1_stats(n):
                dve.wait_ge(s["edge"], 2 * n + 2)
                dve.wait_ge(s["txt_in"], 16 * n + 16)
                norm_stats(n, 0, h)

            def norm1_rows(n):
                need(dve, s["xT"], n)
                norm_rows(n, 0, h, xn1, s["xn1"])

            def xt_low(n):
                dve.wait_ge(s["xTh"], n + 1)
                nc.vector.tensor_tensor(xT_l[:, :, :], ps[:, FB:FB + 2, 0:N], xT_h[:, :, :], ALU.subtract).then_inc(s["xTl"], 1)

            def v_out(n, par):
                dve.wait_ge(s["vps"], n + 1)
                for k, (t0, t1) in enumerate(((0, 2), (2, T))):
                    nc.vector.tensor_tensor(v_aug[:, par, t0:t1, :, 0:HD], bank_tiles(k).rearrange("p t (h d) -> p t h d", h=HEADS),
                                            bv[:, :].rearrange("p (a h d) -> p a h d", a=1, h=HEADS).to_broadcast([P, t1 - t0, HEADS, HD]),
                                            ALU.add).then_inc(s["vaug"], 1)

            def q_low(n, par, c):
                dve.wait_ge(s["q_hi"], 4 * n + 2 * c + 2)
                for pr in range(2):
                    nc.vector.scalar_tensor_tensor(q_l[:, par, pr, c], qs[:, :], parity[:, pr:pr + 1], q_h[:, par, pr, c],
                                                   ALU.mult, ALU.subtract).then_inc(s["q_lo"], 1)

            def k_low(n, par, c):
                dve.wait_ge(s["k_hi"], 2 * n + c + 1)
                nc.vector.scalar_tensor_tensor(k_l[:, par, c, :], ps[:, FB, 0:N], bq4[:, 2 + c:3 + c], k_h[:, par, c, :],
                                               ALU.add, ALU.subtract).then_inc(s["k_lo"], 1)

            def row_max(n, q):
                dve.wait_ge(s["smax"], 4 * n + q + 1)
                need(dve, s["mxT"], 4 * n + q)
                for t in range(T):
                    at, w = (0, P) if t == 0 else (P + (t - 1) * SPAN, SPAN)
                    ins = nc.vector.tensor_reduce(mx[:, t, :].rearrange("p (g r) -> p g r", g=G)[:, :, 0], ps[:, 0:G, at:at + w], AX, ALU.max)
                ins.then_inc(s["mx"], 1)

            def augment(n, q):
                dve.wait_ge(s["mxT"], 4 * n + q + 1)
                need(dve, s["st"], 16 * n + 4 * q)
                nc.vector.tensor_tensor(aug_r[:, :], aug_c[:, :], ps[:, 0, 0:N], ALU.subtract).then_inc(s["aug"], 1)

            def normalise(n, q):
                dve.wait_ge(s["av"], 4 * n + q + 1)
                need(dve, s["aoT"], n)
                need(dve, s["ao"], 4 * n + q)
                o = ps[:, 4 + q % 2, 0:T * G * (HD + 1)].rearrange("p (t g d) -> p t g d", t=T, g=G)
                nc.vector.reciprocal(rs[:, :, :], o[:, :, :, HD]).then_inc(s["rs"], 1)
                dve.wait_ge(s["rs"], 4 * n + q + 1)
                dst = ao[:, :, :].rearrange("p t (c g r d) -> p c r t g d", c=2, g=G, r=2)[:, q // 2, q % 2]
                nc.vector.tensor_tensor(dst, o[:, :, :, 0:HD],
                                        rs[:, :, :].rearrange("p t (g a) -> p t g a", a=1).to_broadcast([P, T, G, HD]),
                                        ALU.mult).then_inc(s["ao"], 1)

            def ao_low(n):
                dve.wait_ge(s["aoh"], n + 1)
                nc.vector.tensor_tensor(aoT_l[:, :, :], ps[:, FB:FB + 2, 0:N], aoT_h[:, :, :], ALU.subtract).then_inc(s["aol"], 1)

            def residual(n, par):
                dve.wait_ge(s["pj"], n + 1)
                dve.wait_ge(s["hp"], n + 1)
                need(dve, s["h1_out"], 16 * n)
                for k, (t0, t1) in enumerate(((0, 2), (2, T))):
                    nc.vector.tensor_tensor(h1[:, t0:t1, :], bank_tiles(k), hp[:, par, t0:t1, :], ALU.add).then_inc(s["h1"], 1)

            def norm2(n, par):
                dve.wait_ge(s["h1"], 2 * n + 2)
                need(dve, s["scat"], 96 * n - 96)
                norm_stats(n, 1, h1)
                norm_rows(n, 1, h1, xn2[:, par], s["xn2"])

            def x2_low(n):
                dve.wait_ge(s["x2h"], n + 1)
                nc.vector.tensor_tensor(x2[:, 1], ps[:, FB:FB + 2, 0:N], x2[:, 0], ALU.subtract).then_inc(s["x2l"], 1)

            RT = 12

            def per_tile(v, k):
                return v.rearrange("p (t a) -> p t a", a=1).to_broadcast([P, T, k])

            def route(n):
                k = [0]

                def then(ins):
                    k[0] += 1
                    ins.then_inc(s["rt"], 1)
                    dve.wait_ge(s["rt"], RT * n + k[0])

                dve.wait_ge(s["lg"], n + 1)
                lg = ps[:, FB + 1, C:C + T * E].rearrange("p (t e) -> p t e", t=T)
                then(nc.vector.tensor_reduce(rmax[:, :], lg, AX, ALU.max))
                nc.vector.tensor_tensor(lgs[:, :, :], lg, per_tile(rmax[:, :], E), ALU.subtract).then_inc(s["lgs"], 1)
                dve.wait_ge(s["rexp"], n + 1)
                then(nc.vector.tensor_reduce(rsum[:, :], rex[:, :, :], AX, ALU.add))
                then(nc.vector.reciprocal(rinv[:, :], rsum[:, :]))
                then(nc.vector.tensor_tensor(score[:, :, :], rex[:, :, :], per_tile(rinv[:, :], E), ALU.mult))
                then(nc.vector.tensor_tensor(biased[:, :, :], score[:, :, :], gb[:, :].rearrange("p (a e) -> p a e", a=1).to_broadcast([P, T, E]), ALU.add))
                for t in range(T):
                    bi = biased[:, t, :]
                    other = bi.rearrange("p (a e) -> p a e", a=1).to_broadcast([P, E, E])
                    own = bi.rearrange("p (e a) -> p e a", a=1).to_broadcast([P, E, E])
                    nc.vector.tensor_tensor(cmp1[:, t], other, own, ALU.is_gt)
                    ins = nc.vector.tensor_tensor(cmp2[:, t], other, own, ALU.is_equal)
                then(ins)
                then(nc.vector.tensor_tensor(cmp2[:, :, :, :], cmp2[:, :, :, :],
                                             before[:, :, :].rearrange("p (a e) f -> p a e f", a=1).to_broadcast([P, T, E, E]), ALU.mult))
                then(nc.vector.tensor_tensor(cmp1[:, :, :, :], cmp1[:, :, :, :], cmp2[:, :, :, :], ALU.add))
                then(nc.vector.tensor_reduce(rank[:, :, :], cmp1[:, :, :, :], AX, ALU.add))
                nc.vector.tensor_scalar(chosen[:, :, :], rank[:, :, :], 1.5, None, ALU.is_lt).then_inc(s["chosen"], 1)
                nc.vector.tensor_scalar(pick[:, :, 0, :], rank[:, :, :], 0.0, None, ALU.is_equal)
                then(nc.vector.tensor_scalar(pick[:, :, 1, :], rank[:, :, :], 1.0, None, ALU.is_equal))
                nc.vector.tensor_tensor(pickw[:, :, 0, :], pick[:, :, 0, :], score[:, :, :], ALU.mult)
                then(nc.vector.tensor_tensor(pickw[:, :, 1, :], pick[:, :, 1, :], score[:, :, :], ALU.mult))
                then(nc.vector.tensor_reduce(wts[:, bass.ds(n * T, T), :] if not isinstance(n, int) else wts[:, n * T:(n + 1) * T, :],
                                             pickw[:, :, :, :], AX, ALU.add))
                assert k[0] == RT

            PP = 4

            def places(n):
                k = [0]

                def then(ins):
                    k[0] += 1
                    ins.then_inc(s["idx"], 1)
                    dve.wait_ge(s["idx"], (PP + 1) * n + k[0])

                dve.wait_ge(s["pos"], n + 1)
                then(nc.vector.tensor_tensor(slot[:, :, :], ps[:, FB + 1, N:N + T * E].rearrange("p (t e) -> p t e", t=T),
                                             ebase[:, :].rearrange("p (a e) -> p a e", a=1).to_broadcast([P, T, E]), ALU.add))
                nc.vector.tensor_tensor(pickw[:, :, 0, :], pick[:, :, 0, :], slot[:, :, :], ALU.mult)
                nc.vector.tensor_tensor(pickw[:, :, 1, :], pick[:, :, 1, :], slot[:, :, :], ALU.mult)
                then(nc.vector.tensor_reduce(chosen_n[:, :], chosen[:, :, :].rearrange("p t e -> p e t"), AX, ALU.add))
                nc.vector.tensor_tensor(counts[:, :], counts[:, :], chosen_n[:, :], ALU.add).then_inc(s["pp"], 1)
                then(nc.vector.tensor_reduce(slot_f[:, :, :], pickw[:, :, :, :], AX, ALU.add))
                need(dve, s["scat"], 96 * n)
                then(nc.vector.tensor_copy(place[:, bass.ds(n * T, T), :] if not isinstance(n, int) else place[:, n * T:(n + 1) * T, :],
                                           slot_f[:, :, :]))
                nc.vector.tensor_copy(idx[:, :, :], slot_f[:, :, :]).then_inc(s["idx"], 1)
                assert k[0] == PP

            to_gray(0)
            edge_sum(0, 0)
            edge_sum(0, 1)
            norm1_stats(0)
            norm1_rows(0)
            to_gray(1)
            xt_low(0)
            k_low(0, 0, 0)
            q_low(0, 0, 0)

            def body(i, par, back1, back2, last):
                k_low(i, par, 1)
                if back1:
                    normalise(i - 1, 2)
                row_max(i, 0)
                augment(i, 0)
                v_out(i, par)
                q_low(i, par, 1)
                if back2:
                    route(i - 2)
                if not last:
                    edge_sum(i + 1, 0)
                if back1:
                    normalise(i - 1, 3)
                row_max(i, 1)
                augment(i, 1)
                if not last:
                    edge_sum(i + 1, 1)
                    norm1_stats(i + 1)
                if back1:
                    ao_low(i - 1)
                if back2:
                    places(i - 2)
                if not last:
                    norm1_rows(i + 1)
                if back1:
                    residual(i - 1, 1 - par)
                normalise(i, 0)
                row_max(i, 2)
                augment(i, 2)
                if not last:
                    xt_low(i + 1)
                if back1:
                    norm2(i - 1, 1 - par)
                if not last:
                    k_low(i + 1, 1 - par, 0)
                normalise(i, 1)
                row_max(i, 3)
                augment(i, 3)
                if back1:
                    x2_low(i - 1)
                if not last:
                    q_low(i + 1, 1 - par, 0)
                if after_next(i):
                    to_gray(i + 2)

            images(dve, body)
            normalise(B - 1, 2)
            normalise(B - 1, 3)
            route(B - 2)
            places(B - 2)
            ao_low(B - 1)
            residual(B - 1, 1)
            norm2(B - 1, 1)
            x2_low(B - 1)
            route(B - 1)
            places(B - 1)

            dve.wait_ge(s["total"], 1)
            tot = ps[:, 0, 0:E]
            nc.vector.tensor_tensor(pad_row[:, :], ps[0:1, 0, 0:E], ebase[0:1, :], ALU.add).then_inc(s["padidx"], 1)
            shift_by = TW.bit_length() - 1
            link(nc.vector.tensor_scalar(tile_i[:, :], tot, float(TW - 1), None, ALU.add))
            link(nc.vector.tensor_scalar(tile_i[:, :], tile_i[:, :], shift_by, None, ALU.arith_shift_right))
            link(nc.vector.tensor_copy(tile_f[:, :], tile_i[:, :]))
            link(nc.vector.tensor_copy(tile_cum[:, :], tile_f[0:1, :]))
            for e in range(1, E):
                link(nc.vector.tensor_tensor(tile_cum[:, e:e + 1], tile_cum[:, e - 1:e], tile_f[0:1, e:e + 1], ALU.add))
            wide = [1, NT, E]
            link(nc.vector.tensor_tensor(tile_cmp[:, :, :], tile_no[:, :].rearrange("p (n a) -> p n a", a=1).to_broadcast(wide),
                                         tile_cum[:, :].rearrange("p (a e) -> p a e", a=1).to_broadcast(wide), ALU.is_ge))
            link(nc.vector.tensor_tensor(tile_mul[:, :, :], tile_cmp[:, :, :],
                                         tile_f[0:1, :].rearrange("p (a e) -> p a e", a=1).to_broadcast(wide), ALU.mult))
            link(nc.vector.tensor_reduce(tile_red[:, 0, :], tile_cmp[:, :, :], AX, ALU.add))
            link(nc.vector.tensor_reduce(tile_red[:, 1, :], tile_mul[:, :, :], AX, ALU.add))
            link(nc.vector.tensor_scalar(tile_red[:, 2, :], tile_red[:, 0, :], float(E), None, ALU.is_lt))
            link(nc.vector.tensor_tensor(tile_red[:, 0, :], tile_red[:, 0, :], tile_red[:, 2, :], ALU.mult))
            link(nc.vector.tensor_tensor(tile_red[:, 1, :], tile_no[:, :], tile_red[:, 1, :], ALU.subtract))
            link(nc.vector.tensor_scalar(tile_red[:, 1, :], tile_red[:, 1, :], float(TW), None, ALU.mult))
            link(nc.vector.tensor_tensor(tile_red[:, 1, :], tile_red[:, 1, :], tile_red[:, 2, :], ALU.mult))
            link(nc.vector.tensor_scalar(tile_red[:, 3, :], tile_red[:, 0, :], float(REGION), None, ALU.mult))
            link(nc.vector.tensor_tensor(tile_red[:, 3, :], tile_red[:, 3, :], tile_red[:, 1, :], ALU.add))
            link(nc.vector.tensor_copy(tile_tab[:, 0, :], tile_red[:, 0, :]))
            nc.vector.tensor_copy(tile_tab[:, 1, :], tile_red[:, 3, :]).then_inc(s["tab"], 1)
            dve.wait_ge(s["tab"], 1)
            link(nc.vector.tensor_scalar(back[:, :], tile_f[:, :], float(TW), float(-REGION), ALU.mult, ALU.add))
            for e in range(1, E):
                nc.vector.tensor_scalar(moved[:, e - 1], place[:, :, :], float(e * REGION), back[:, e - 1:e], ALU.is_ge, ALU.mult)
            link(nc.vector.tensor_copy(moved[:, E - 1], place[:, :, :]))
            link(nc.vector.tensor_reduce(place[:, :, :], moved[:, :, :, :].rearrange("p e n k -> p n k e"), AX, ALU.add))
            link(nc.vector.tensor_copy(dest[:, :, :], place[:, :, :]))

            def times(n, par, c, e, width, nm):
                m = rows_of(c)
                o = (par + c) % 2
                dve.wait_ge(s[nm + "up"], 6 * n + 2 * c + 2)
                dve.wait_ge(s[nm + "u3"], 3 * n + c + 1)
                need(dve, s[nm + "silu"], 3 * n + c - 1)
                bias = bias1[0:m, c, e:e + 1] if isinstance(e, int) else bias1[0:m, c, bass.ds(e, 1)]
                nc.vector.scalar_tensor_tensor(prd[0:m, o, 0:width], ps[0:m, 2 * o + 1, 0:width], bias, u3[0:m, o, 0:width],
                                               ALU.add, ALU.mult).then_inc(s[nm + "prod"], 1)

            def hidden_low(n, par, c, width, nm):
                m = rows_of(c)
                o = (par + c) % 2
                dve.wait_ge(s[nm + "silu"], 3 * n + c + 1)
                nc.vector.tensor_tensor(hT_l[0:m, par, c, 0:width], hs[0:m, o, 0:width], hT_h[0:m, par, c, 0:width],
                                        ALU.subtract).then_inc(s[nm + "hl"], 1)

            def tile_low(n, par):
                dve.wait_ge(s["xeh"], n + 1)
                nc.vector.tensor_tensor(xe_l[:, par], ps[:, 6 + par, :].rearrange("p (k n) -> p k n", k=KC), xe_h[:, par],
                                        ALU.subtract).then_inc(s["xel"], 1)

            def tile_out(n, par, t, e):
                dve.wait_ge(s["yps"], 2 * n + t + 1)
                if t == 0 and not (isinstance(n, int) and n < 2):
                    dve.wait_ge(s[f"st{par}"], in_slot(n - 2, par))
                nc.vector.tensor_tensor(yo[:, par, t, :], ps[:, 4 + t, 0:C], b2b[:, bass.ds(e, 1), :].rearrange("p a n -> p (a n)"),
                                        ALU.add).then_inc(s["yo"], 1)

            def expert(j):
                return dve.value_load(tile_tab[0:1, 0, bass.ds(j, 1)], min_val=0, max_val=E - 1)

            tile_low(0, 0)
            tile_low(1, 1)
            e0 = expert(0)
            for c in range(HC):
                times(0, 0, c, e0, TW, "")
                hidden_low(0, 0, c, TW, "")

            def body_b(j, par, last, expert_of):
                if not last:
                    e1 = expert_of(1)
                    times(j + 1, 1 - par, 0, e1, TW, "")
                    if not (isinstance(j, int) and j + 2 >= NT):
                        tile_low(j + 2, par)
                e = expert_of(0)
                tile_out(j, par, 0, e)
                if not last:
                    hidden_low(j + 1, 1 - par, 0, TW, "")
                    times(j + 1, 1 - par, 1, e1, TW, "")
                    times(j + 1, 1 - par, 2, e1, TW, "")
                    hidden_low(j + 1, 1 - par, 1, TW, "")
                    hidden_low(j + 1, 1 - par, 2, TW, "")
                tile_out(j, par, 1, e)
            dve.wait_ge(s["tabc"], 16 * E)
            groups(dve, NT, body_b, TILES_PER, expert)

            def fetch_idx(n, par):
                if not (isinstance(n, int) and n < 2):
                    dve.wait_ge(s[f"g{par}"], 6 * in_slot(n - 2, par))
                nc.vector.tensor_copy(idxc[:, par], dest[:, bass.ds(n * T, T), :] if not isinstance(n, int) else
                                      dest[:, n * T:(n + 1) * T, :]).then_inc(s["idxc"], 1)
            fetch_idx(0, 0)
            fetch_idx(1, 1)
            dve.wait_ge(s["silu"], 3 * NT)
            for c in range(HC):
                times(0, 0, c, E, N, "c")
                hidden_low(0, 0, c, N, "c")

            def body_c(n, par, last):
                for t in range(T):
                    if not last:
                        times(n + 1, 1 - par, t, E, N, "c")
                    dve.wait_ge(s["cyps"], 3 * n + t + 1)
                    if t == 0:
                        dve.wait_ge(s[f"ch{par}"], in_slot(n, par))
                        if not (isinstance(n, int) and n < 2):
                            dve.wait_ge(s[f"co{par}"], in_slot(n - 2, par))
                    nc.vector.tensor_tensor(acc[:, par, t, :], ps[:, 4 + t, 0:C], h1c[:, par, t, :], ALU.add).then_inc(s["cacc"], 1)
                    if not last:
                        hidden_low(n + 1, 1 - par, t, N, "c")
                dve.wait_ge(s[f"g{par}"], 6 * in_slot(n, par))
                dve.wait_ge(s["cacc"], 3 * n + 3)
                for k in range(2):
                    for t in range(T):
                        w = wts[:, bass.ds(n * T + t, 1), k] if not isinstance(n, int) else wts[:, n * T + t:n * T + t + 1, k]
                        ins = nc.vector.scalar_tensor_tensor(acc[:, par, t, :], yg[:, par, t, k, :], w, acc[:, par, t, :], ALU.mult, ALU.add)
                    if k == 0:
                        ins.then_inc(s["cfirst"], 1)
                        dve.wait_ge(s["cfirst"], n + 1)
                ins.then_inc(s["cdone"], 1)
                if not (isinstance(n, int) and n + 2 >= B):
                    fetch_idx(n + 2, par)
            groups(dve, B, body_c)

        @block.gpsimd
        def _(pool):
            gates = []

            def gate():
                gates.append(len(gates))
                return nc.gpsimd.tensor_tensor(one_p[:, gates[-1]:gates[-1] + 1], zero[:, :], zero[:, :], ALU.add)

            pool.wait_ge(s["ones"], 1)
            pool.wait_ge(s["consts2"], 16 * N_CONST2)

            def plus_bias(n, par):
                pool.wait_ge(s["edge"], 2 * n + 2)
                pool.wait_ge(s["txt_in"], 16 * n + 16)
                need(pool, s["h1"], 2 * n - 2)
                nc.gpsimd.tensor_tensor(hp[:, par], h[:, :, :], pb[:, :].rearrange("p (a c) -> p a c", a=1).to_broadcast([P, T, C]),
                                        ALU.add).then_inc(s["hp"], 1)

            def shared_bias(n):
                pool.wait_ge(s["xn2"], n + 1)
                nc.gpsimd.tensor_tensor(h1[:, :, :], h1[:, :, :], sb2b[:, :].rearrange("p (a c) -> p a c", a=1).to_broadcast([P, T, C]),
                                        ALU.add).then_inc(s["h1s"], 1)

            def gray_low(n):
                pool.wait_ge(s["gray_hi"], n + 1)
                nc.gpsimd.tensor_tensor(gray_l[:, :, 1:IMG + 1], gray, gray_h[:, :, 1:IMG + 1], ALU.subtract).then_inc(s["gray_lo"], 1)

            def scatter(n, par):
                pool.wait_ge(s["idx"], (PP_ + 1) * (n + 1))
                gate()
                for t in range(T):
                    for k in range(2):
                        nc.gpsimd.indirect_dma_start(out=xs_d, out_offset=bass.IndirectOffsetOnAxis(ap=idx[:, t, k:k + 1], axis=0),
                                                     in_=xn2[:, par, t, :], in_offset=None).then_inc(s["scat"], 16)

            def weights_in(e, nth):
                if not (isinstance(nth, int) and nth == 0):
                    pool.wait_ge(s["w_lo"], 4 * nth)
                    gate()
                a1, a3, a2 = (sw1, sw3, sw2) if isinstance(e, int) and e == E else (w1[e], w3[e], w2[e])
                d = stage
                for dst, src in ((d[:, 0:NW].rearrange("p (k n) -> p k n", k=KC), a1.rearrange("(k p) n -> p k n", p=P)),
                                 (d[:, NW:2 * NW].rearrange("p (k n) -> p k n", k=KC), a3.rearrange("(k p) n -> p k n", p=P)),
                                 (d[:, 2 * NW:2 * NW + 2 * C].rearrange("p (k n) -> p k n", k=2), a2[0:2 * P].rearrange("(k p) n -> p k n", p=P)),
                                 (d[0:HLAST, 2 * NW + 2 * C:2 * NW + 3 * C], a2[2 * P:])):
                    pool.dma_start(dst, src).then_inc(s["w_in"], 16)

            def weights_split(e, nth):
                at = slice(e, e + 1) if isinstance(e, int) else bass.ds(e, 1)
                d = stage
                pool.wait_ge(s["w_in"], 64 * (nth + 1))
                gate()
                parts = []
                for k in range(KC):
                    parts.append((w1_h[:, at, k, :], w1_l[:, at, k, :], d[:, k * HID:(k + 1) * HID]))
                    parts.append((w3_h[:, at, k, :], w3_l[:, at, k, :], d[:, NW + k * HID:NW + (k + 1) * HID]))
                for c in range(HC):
                    m = rows_of(c)
                    parts.append((w2_h[0:m, at, c, :], w2_l[0:m, at, c, :], d[0:m, 2 * NW + c * C:2 * NW + (c + 1) * C]))
                for hi, lo, src in parts:
                    nc.gpsimd.tensor_copy(hi.rearrange("p a n -> p (a n)"), src).then_inc(s["w_hi"], 1)
                pool.wait_ge(s["w_hi"], len(parts) * (nth + 1))
                gate()
                for hi, lo, src in parts:
                    ins = nc.gpsimd.tensor_tensor(lo.rearrange("p a n -> p (a n)"), src, hi.rearrange("p a n -> p (a n)"), ALU.subtract)
                ins.then_inc(s["w_lo"], 4)

            PP_ = 4

            def body(i, par, back1, back2, last, e):
                if back2:
                    scatter(i - 2, par)
                if not last:
                    plus_bias(i + 1, 1 - par)
                if back1:
                    shared_bias(i - 1)
                if e is not None:
                    weights_in(e, e + 1)
                    weights_split(e, e + 1)
                if after_next(i):
                    gray_low(i + 2)

            gray_low(0)
            plus_bias(0, 0)
            gray_low(1)
            pool.wait_ge(s["setup_t"], 1)
            weights_in(E, 0)
            weights_split(E, 0)
            body(0, 0, False, False, False, 0)
            body(1, 1, True, False, False, 1)
            with pool.Fori(1, E // 2) as u:
                body(2 * u, 0, True, True, False, 2 * u)
                body(2 * u + 1, 1, True, True, False, 2 * u + 1)
            with pool.Fori(E // 2, B // 2 - 1) as u:
                body(2 * u, 0, True, True, False, None)
                body(2 * u + 1, 1, True, True, False, None)
            body(B - 2, 0, True, True, False, None)
            body(B - 1, 1, True, True, True, None)
            scatter(B - 2, 0)
            shared_bias(B - 1)
            scatter(B - 1, 1)
            pool.wait_ge(s["tab"], 1)

            def body_b(j, par, last):
                pool.wait_ge(s["yo"], 2 * j + 2)
                need(pool, s["bgated"], j)
                gate().then_inc(s["bgated"], 1)
                pool.dma_start(ys_d[bass.ds(j * TW, TW), :].rearrange("(t p) d -> p t d", p=P), yo[:, par]).then_inc(s[f"st{par}"], 16)
            groups(pool, NT, body_b)
            pool.wait_ge(s["st0"], 16 * (NT // 2))
            pool.wait_ge(s["st1"], 16 * (NT // 2))

            def gather(n, par):
                pool.wait_ge(s["idxc"], n + 1)
                need(pool, s["cdone"], n - 1)
                need(pool, s["gated"], n)
                gate().then_inc(s["gated"], 1)
                for t in range(T):
                    for k in range(2):
                        nc.gpsimd.indirect_dma_start(out=yg[:, par, t, k, :], out_offset=None, in_=ys_d,
                                                     in_offset=bass.IndirectOffsetOnAxis(ap=idxc[:, par, t, k:k + 1], axis=0)
                                                     ).then_inc(s[f"g{par}"], 16)
            gather(0, 0)

            def body_c(n, par, last):
                if not last:
                    gather(n + 1, 1 - par)
            groups(pool, B, body_c)


_INS = ['x', 'txt', 'L0_tok_scharr', 'L0_attn_qkv_w', 'L0_attn_qkv_b', 'L0_attn_proj_w', 'L0_attn_proj_b',
        'L0_ffn_gate_w', 'L0_ffn_gate_b', 'L0_ffn_w1', 'L0_ffn_b1', 'L0_ffn_w3', 'L0_ffn_b3', 'L0_ffn_w2', 'L0_ffn_b2',
        'L0_ffn_sw1', 'L0_ffn_sb1', 'L0_ffn_sw3', 'L0_ffn_sb3', 'L0_ffn_sw2', 'L0_ffn_sb2']


def shape_constants(B, T, E):
    import numpy as np
    heads, window, p = HEADS, WINDOW, P
    i = np.arange(p)
    eye = np.eye(p, dtype=np.float32)
    shift = np.zeros((p, 3, p), np.float32)
    for dy in range(3):
        shift[:, dy, :] = (i[:, None] == i[None, :] + dy - 1)
    seam_sel = np.zeros((p, 6, p), np.float32)
    seam_part = np.zeros((p, 1), np.float32)
    for f in range(2):
        for a in range(2):
            for b in range(2):
                for dx in range(3):
                    seam_sel[32 * f + 6 * a + 3 * b + dx, 3 * f + dx, 0 if f else p - 1] = 1
                    seam_part[32 * f + 6 * a + 3 * b + dx, 0] = b
    base = 2.0 ** (-2.0 ** (-(np.log2(heads) - 3)))
    slopes = (np.float64(base) ** np.arange(1, heads + 1, dtype=np.float32)).astype(np.float32).astype(np.float64)
    off = -30000.0
    n, m = i[:, None], np.arange(-window, p)[None, :]
    ok = (m <= n) & (n - m < window)
    mask_a = np.where(ok[:, None, :], slopes[None, :, None] * (m - n)[:, None, :], off).astype(np.float16)
    m, n = i[:, None], np.arange(p + window)[None, :]
    mask_t = np.where((m <= n) & (n - m < window), 0.0, off).astype(np.float16)

    def parts(v):
        out = []
        for _ in range(3):
            a = v.astype(np.float16)
            out.append(a)
            v = v - a.astype(np.float64)
        return out

    aug_l = np.zeros((p, T, QUADS, p), np.float16)
    aug_c = np.zeros((p, T * p), np.float16)
    for g in range(G):
        r = 32 * g
        aug_c[r + 1:r + 4] = 1
        aug_c[r + 4:r + 7] = np.arange(T * p)
        for q in range(QUADS):
            sl = slopes[head_of(q, g)]
            aug_l[r, :, q, :] = 1
            for t in range(T):
                for j, a in enumerate(parts(sl * (t * p + i))):
                    aug_l[r + 1 + j, t, q] = a
                for j, a in enumerate(parts(-sl * np.ones(1))):
                    aug_l[r + 4 + j, t, q] = a
    par = ((i[:, None] // HD) % 2 == np.arange(2)[None, :]).astype(np.float32)
    before = np.broadcast_to((np.arange(E)[None, :] < np.arange(E)[:, None]).astype(np.float32), (p, E, E)).copy()
    tri = np.ones((p, 2, p), np.float16)
    tri[:, 0, :] = i[:, None] < i[None, :]
    region = B * T * p + TW
    ebase = np.broadcast_to(np.arange(E, dtype=np.float32) * region, (p, E)).copy()
    nt = tile_count(B * T * p, E)
    tile = np.arange(nt, dtype=np.float32)[None, :]
    return [("ident", eye), ("shift", shift), ("seam_sel", seam_sel), ("seam_part", seam_part), ("mask_a", mask_a), ("mask_t", mask_t), ("aug_l", aug_l),
            ("aug_c", aug_c), ("parity", par), ("before", before), ("tri", tri), ("ebase", ebase), ("tile", tile)]


def kernel(**inputs):
    import numpy as _np
    import concourse.bacc as _bacc
    from concourse import mybir as _mybir
    from concourse.bass_utils import run_bass_kernel_spmd as _run

    nc = _bacc.Bacc("TRN2", target_bir_lowering=False, num_devices=1)
    arrays, args = {}, []
    items = [(n, _np.ascontiguousarray(inputs[n])) for n in _INS]
    B, rows = inputs['x'].shape[0], inputs['x'].shape[2] + inputs['txt'].shape[1]
    items += shape_constants(B, rows // P, inputs['L0_ffn_w1'].shape[0])
    for name, a in items:
        arrays[f"in_{name}_dram"] = a
        args.append(nc.dram_tensor(f"in_{name}_dram", a.shape, _mybir.dt.from_np(a.dtype), kind="ExternalInput").ap())
    args.append(nc.dram_tensor("out_dram", (B, rows, C), _mybir.dt.float32, kind="ExternalOutput").ap())
    program(nc, *args)
    r = _run(nc, [arrays], core_ids=[0])
    return r.results[0]["out_dram"]
```
